# Optimizing a Trainium2 kernel written in Bass

```python
import numpy as np
import jax
import jax.numpy as jnp

def _softmax(x, axis=-1):
    return jax.nn.softmax(x, axis=axis)

def _gelu(x):
    return jax.nn.gelu(x, approximate=True)

def _silu(x):
    return jax.nn.silu(x)

def _sigmoid(x):
    return jax.nn.sigmoid(x)

def _layernorm(x, axis=-1, eps=1e-05):
    m = jnp.mean(x, axis=axis, keepdims=True)
    v = jnp.var(x, axis=axis, keepdims=True)
    return (x - m) / jnp.sqrt(v + eps)

def _scatter_add(tgt, idx, src, axis=0):
    return tgt.at[idx].add(src)

def _segment_sum(src, seg, n):
    return jax.ops.segment_sum(src, seg, n)
kernel_name = 'mk_seq_postln_d2_jaxref_r8_a2d4ea'

def setup_inputs(seed: int=0):
    np.random.seed(seed)
    _w = jnp.asarray

    def _L0_attn_setup():
        import jax, jax.numpy as jnp
        import numpy as np
        from jax import lax
        D_MODEL = 256
        D_INNER = 512
        D_CONV = 4
        B, T = (4, 256)

        def _rmsnorm(h):
            n = jnp.sqrt(jnp.sum(h * h, axis=-1, keepdims=True))
            return h / jnp.maximum(n, 1e-12) * h.shape[-1] ** 0.5

        def _mamba_fallback(h, W_in, conv_w, conv_b, W_out):
            xz = jnp.einsum('btd,ed->bte', h, W_in)
            xp, z = jnp.split(xz, 2, axis=-1)
            xc = lax.conv_general_dilated(xp.transpose(0, 2, 1), conv_w, window_strides=(1,), padding=[(D_CONV - 1, 0)], dimension_numbers=('NCH', 'OIH', 'NCH'), feature_group_count=D_INNER) + conv_b[None, :, None]
            xc = xc.transpose(0, 2, 1)
            y = jax.nn.silu(xc) * jax.nn.silu(z)
            return jnp.einsum('bte,de->btd', y, W_out)
        key = jax.random.key(seed)
        ks = jax.random.split(key, 7)
        std = 0.02
        return {'x': jax.random.normal(ks[0], (B, T, D_MODEL), jnp.float32), 'W_in': jax.random.normal(ks[1], (2 * D_INNER, D_MODEL), jnp.float32) * std, 'conv_w': jax.random.normal(ks[2], (D_INNER, 1, D_CONV), jnp.float32) * std, 'conv_b': jnp.zeros((D_INNER,), jnp.float32), 'W_out': jax.random.normal(ks[3], (D_MODEL, D_INNER), jnp.float32) * std, 'W_mlp1': jax.random.normal(ks[4], (4 * D_MODEL, D_MODEL), jnp.float32) * std, 'W_mlp2': jax.random.normal(ks[5], (D_MODEL, 4 * D_MODEL), jnp.float32) * std}
    _L0_attn_in = _L0_attn_setup()

    def _L0_ffn_setup():
        import jax, jax.numpy as jnp
        import numpy as np
        HIDDEN = 256
        NUM_EXPERTS = 32
        TOP_K = 4
        MOE_INTER = 96
        GROUP = 2
        NUM_CHUNK = NUM_EXPERTS // GROUP
        CHUNK_INTER = 128
        SMALL_SCALE = 0.05

        def _routing(x2d, gate_w):
            logits = x2d @ gate_w.T
            rw = jax.nn.softmax(logits.astype(jnp.float32), axis=-1)
            scores = jax.nn.sigmoid(logits.astype(jnp.float32))
            _, sel = jax.lax.top_k(scores, TOP_K)
            w = jnp.take_along_axis(rw, sel, axis=-1)
            w = w / w.sum(axis=-1, keepdims=True)
            return (w.astype(x2d.dtype), sel)

        def _moe(x2d, Wg, Wu, Wd, cw):
            g = jnp.einsum('th,ehi->eti', x2d, Wg)
            u = jnp.einsum('th,ehi->eti', x2d, Wu)
            a = jax.nn.silu(g) * u * cw.T[:, :, None]
            return jnp.einsum('eti,eih->th', a, Wd)
        key = jax.random.key(seed)
        ks = jax.random.split(key, 8)
        s = 0.02
        B, S = (2, 256)
        return {'hidden_states': jax.random.normal(ks[0], (B, S, HIDDEN), jnp.float32), 'gate_w': jax.random.normal(ks[1], (NUM_EXPERTS, HIDDEN), jnp.float32) * s, 'Wg': jax.random.normal(ks[2], (NUM_EXPERTS, HIDDEN, MOE_INTER), jnp.float32) * s, 'Wu': jax.random.normal(ks[3], (NUM_EXPERTS, HIDDEN, MOE_INTER), jnp.float32) * s, 'Wd': jax.random.normal(ks[4], (NUM_EXPERTS, MOE_INTER, HIDDEN), jnp.float32) * s, 'cWg': jax.random.normal(ks[5], (NUM_CHUNK, HIDDEN, CHUNK_INTER), jnp.float32) * s, 'cWu': jax.random.normal(ks[6], (NUM_CHUNK, HIDDEN, CHUNK_INTER), jnp.float32) * s, 'cWd': jax.random.normal(ks[7], (NUM_CHUNK, CHUNK_INTER, HIDDEN), jnp.float32) * s}
    _L0_ffn_in = _L0_ffn_setup()

    def _L1_attn_setup():
        import jax, jax.numpy as jnp
        import numpy as np
        B, S, D = (2, 256, 256)
        H, DH, GROUPS = (16, 128, 4)
        KV = H // GROUPS
        G = GROUPS
        key = jax.random.key(seed)
        ks = jax.random.split(key, 5)
        sd = 1.0 / np.sqrt(D)
        return {'x': jax.random.normal(ks[0], (B, S, D), dtype=jnp.float32), 'Wq': jax.random.normal(ks[1], (D, H * DH), dtype=jnp.float32) * sd, 'bq': jnp.zeros((H * DH,), dtype=jnp.float32), 'Wk': jax.random.normal(ks[2], (D, KV * DH), dtype=jnp.float32) * sd, 'bk': jnp.zeros((KV * DH,), dtype=jnp.float32), 'Wv': jax.random.normal(ks[3], (D, KV * DH), dtype=jnp.float32) * sd, 'bv': jnp.zeros((KV * DH,), dtype=jnp.float32), 'Wo': jax.random.normal(ks[4], (H * DH, D), dtype=jnp.float32) * (1.0 / np.sqrt(H * DH)), 'bo': jnp.zeros((D,), dtype=jnp.float32)}
    _L1_attn_in = _L1_attn_setup()

    def _L1_ffn_setup():
        import jax, jax.numpy as jnp
        import numpy as np
        HIDDEN = 256
        FFN = 176
        N_EXPERTS = 16
        TOP_K = 4
        SHARED_FFN = 2 * FFN

        def _glu_ffn(x, gate_up, down):
            gu = x @ gate_up.T
            g, u = jnp.split(gu, 2, axis=-1)
            return jax.nn.silu(g) * u @ down.T
        key = jax.random.key(seed)
        ks = jax.random.split(key, 6)
        s = 0.02
        return {'hidden_states': jax.random.normal(ks[0], (1, 256, HIDDEN), jnp.float32), 'gate_weight': jax.random.normal(ks[1], (N_EXPERTS, HIDDEN), jnp.float32) * s, 'gate_up_weights': jax.random.normal(ks[2], (N_EXPERTS, 2 * FFN, HIDDEN), jnp.float32) * s, 'down_weights': jax.random.normal(ks[3], (N_EXPERTS, HIDDEN, FFN), jnp.float32) * s, 'shared_gate_up': jax.random.normal(ks[4], (2 * SHARED_FFN, HIDDEN), jnp.float32) * s, 'shared_down': jax.random.normal(ks[5], (HIDDEN, SHARED_FFN), jnp.float32) * s}
    _L1_ffn_in = _L1_ffn_setup()
    _d = {'L0_attn_x': _L0_attn_in['x'], 'L0_attn_W_in': _L0_attn_in['W_in'], 'L0_attn_conv_w': _L0_attn_in['conv_w'], 'L0_attn_conv_b': _L0_attn_in['conv_b'], 'L0_attn_W_out': _L0_attn_in['W_out'], 'L0_attn_W_mlp1': _L0_attn_in['W_mlp1'], 'L0_attn_W_mlp2': _L0_attn_in['W_mlp2'], 'L0_ffn_gate_w': _L0_ffn_in['gate_w'], 'L0_ffn_Wg': _L0_ffn_in['Wg'], 'L0_ffn_Wu': _L0_ffn_in['Wu'], 'L0_ffn_Wd': _L0_ffn_in['Wd'], 'L0_ffn_cWg': _L0_ffn_in['cWg'], 'L0_ffn_cWu': _L0_ffn_in['cWu'], 'L0_ffn_cWd': _L0_ffn_in['cWd'], 'L1_attn_Wq': _L1_attn_in['Wq'], 'L1_attn_bq': _L1_attn_in['bq'], 'L1_attn_Wk': _L1_attn_in['Wk'], 'L1_attn_bk': _L1_attn_in['bk'], 'L1_attn_Wv': _L1_attn_in['Wv'], 'L1_attn_bv': _L1_attn_in['bv'], 'L1_attn_Wo': _L1_attn_in['Wo'], 'L1_attn_bo': _L1_attn_in['bo'], 'L1_ffn_gate_weight': _L1_ffn_in['gate_weight'], 'L1_ffn_gate_up_weights': _L1_ffn_in['gate_up_weights'], 'L1_ffn_down_weights': _L1_ffn_in['down_weights'], 'L1_ffn_shared_gate_up': _L1_ffn_in['shared_gate_up'], 'L1_ffn_shared_down': _L1_ffn_in['shared_down']}
    _x0 = _d['L0_attn_x']
    _d['L0_attn_x'] = jax.random.normal(jax.random.fold_in(jax.random.key(seed), 1), (8, 256, 256), dtype=_x0.dtype)
    del _x0
    return _d

def reference(L0_attn_x, L0_attn_W_in, L0_attn_conv_w, L0_attn_conv_b, L0_attn_W_out, L0_attn_W_mlp1, L0_attn_W_mlp2, L0_ffn_gate_w, L0_ffn_Wg, L0_ffn_Wu, L0_ffn_Wd, L0_ffn_cWg, L0_ffn_cWu, L0_ffn_cWd, L1_attn_Wq, L1_attn_bq, L1_attn_Wk, L1_attn_bk, L1_attn_Wv, L1_attn_bv, L1_attn_Wo, L1_attn_bo, L1_ffn_gate_weight, L1_ffn_gate_up_weights, L1_ffn_down_weights, L1_ffn_shared_gate_up, L1_ffn_shared_down):

    def _L0_attn_ref(x, W_in, conv_w, conv_b, W_out, W_mlp1, W_mlp2):
        import jax, jax.numpy as jnp
        import numpy as np
        from jax import lax
        D_MODEL = 256
        D_INNER = 512
        D_CONV = 4
        B, T = (4, 256)

        def _rmsnorm(h):
            n = jnp.sqrt(jnp.sum(h * h, axis=-1, keepdims=True))
            return h / jnp.maximum(n, 1e-12) * h.shape[-1] ** 0.5

        def _mamba_fallback(h, W_in, conv_w, conv_b, W_out):
            xz = jnp.einsum('btd,ed->bte', h, W_in)
            xp, z = jnp.split(xz, 2, axis=-1)
            xc = lax.conv_general_dilated(xp.transpose(0, 2, 1), conv_w, window_strides=(1,), padding=[(D_CONV - 1, 0)], dimension_numbers=('NCH', 'OIH', 'NCH'), feature_group_count=D_INNER) + conv_b[None, :, None]
            xc = xc.transpose(0, 2, 1)
            y = jax.nn.silu(xc) * jax.nn.silu(z)
            return jnp.einsum('bte,de->btd', y, W_out)
        h = _rmsnorm(x)
        x = x + _mamba_fallback(h, W_in, conv_w, conv_b, W_out)
        h = _rmsnorm(x)
        m = jnp.einsum('bte,de->btd', jax.nn.relu(jnp.einsum('btd,ed->bte', h, W_mlp1)), W_mlp2)
        return x + m

    def _L0_ffn_ref(hidden_states, gate_w, Wg, Wu, Wd, cWg, cWu, cWd):
        import jax, jax.numpy as jnp
        import numpy as np
        HIDDEN = 256
        NUM_EXPERTS = 32
        TOP_K = 4
        MOE_INTER = 96
        GROUP = 2
        NUM_CHUNK = NUM_EXPERTS // GROUP
        CHUNK_INTER = 128
        SMALL_SCALE = 0.05

        def _routing(x2d, gate_w):
            logits = x2d @ gate_w.T
            rw = jax.nn.softmax(logits.astype(jnp.float32), axis=-1)
            scores = jax.nn.sigmoid(logits.astype(jnp.float32))
            _, sel = jax.lax.top_k(scores, TOP_K)
            w = jnp.take_along_axis(rw, sel, axis=-1)
            w = w / w.sum(axis=-1, keepdims=True)
            return (w.astype(x2d.dtype), sel)

        def _moe(x2d, Wg, Wu, Wd, cw):
            g = jnp.einsum('th,ehi->eti', x2d, Wg)
            u = jnp.einsum('th,ehi->eti', x2d, Wu)
            a = jax.nn.silu(g) * u * cw.T[:, :, None]
            return jnp.einsum('eti,eih->th', a, Wd)
        B, S, H = hidden_states.shape
        T = B * S
        x = hidden_states.reshape(T, H)
        w, sel = _routing(x, gate_w)
        rows = jnp.arange(T)[:, None]
        cw_large = jnp.zeros((T, NUM_EXPERTS), x.dtype).at[rows, sel].add(w)
        cw_small = jnp.zeros((T, NUM_CHUNK), x.dtype).at[rows, sel // GROUP].add(w)
        large = _moe(x, Wg, Wu, Wd, cw_large)
        small = _moe(x, cWg, cWu, cWd, cw_small)
        return (large + SMALL_SCALE * small).reshape(B, S, H)

    def _L1_attn_ref(x, Wq, bq, Wk, bk, Wv, bv, Wo, bo):
        import jax, jax.numpy as jnp
        import numpy as np
        B, S, D = (2, 256, 256)
        H, DH, GROUPS = (16, 128, 4)
        KV = H // GROUPS
        G = GROUPS
        b, s, _ = x.shape
        Q = (x @ Wq + bq).reshape(b, s, KV, G, DH)
        K = (x @ Wk + bk).reshape(b, s, KV, DH)
        V = (x @ Wv + bv).reshape(b, s, KV, DH)
        scale = 1.0 / np.sqrt(DH).astype(np.float32)
        scores = jnp.einsum('bqkgd,bpkd->bkgqp', Q, K) * scale
        attn = jax.nn.softmax(scores, axis=-1)
        out = jnp.einsum('bkgqp,bpkd->bqkgd', attn, V)
        out = out.reshape(b, s, H * DH)
        return out @ Wo + bo

    def _L1_ffn_ref(hidden_states, gate_weight, gate_up_weights, down_weights, shared_gate_up, shared_down):
        import jax, jax.numpy as jnp
        import numpy as np
        HIDDEN = 256
        FFN = 176
        N_EXPERTS = 16
        TOP_K = 4
        SHARED_FFN = 2 * FFN

        def _glu_ffn(x, gate_up, down):
            gu = x @ gate_up.T
            g, u = jnp.split(gu, 2, axis=-1)
            return jax.nn.silu(g) * u @ down.T
        orig_shape = hidden_states.shape
        x = hidden_states.reshape(-1, orig_shape[-1])
        scores = jax.nn.softmax(x @ gate_weight.T, axis=-1)
        topk_weight, topk_idx = jax.lax.top_k(scores, TOP_K)
        y = jnp.zeros_like(x)
        for e in range(N_EXPERTS):
            w_e = jnp.sum(jnp.where(topk_idx == e, topk_weight, 0.0), axis=-1)
            y = y + w_e[:, None] * _glu_ffn(x, gate_up_weights[e], down_weights[e])
        y = y + _glu_ffn(x, shared_gate_up, shared_down)
        return y.reshape(orig_shape)
    x = L0_attn_x
    x = _layernorm(x + _L0_attn_ref(x, L0_attn_W_in, L0_attn_conv_w, L0_attn_conv_b, L0_attn_W_out, L0_attn_W_mlp1, L0_attn_W_mlp2), axis=-1)
    x = _layernorm(x + _L0_ffn_ref(x, L0_ffn_gate_w, L0_ffn_Wg, L0_ffn_Wu, L0_ffn_Wd, L0_ffn_cWg, L0_ffn_cWu, L0_ffn_cWd), axis=-1)
    x = _layernorm(x + _L1_attn_ref(x, L1_attn_Wq, L1_attn_bq, L1_attn_Wk, L1_attn_bk, L1_attn_Wv, L1_attn_bv, L1_attn_Wo, L1_attn_bo), axis=-1)
    x = _layernorm(x + _L1_ffn_ref(x, L1_ffn_gate_weight, L1_ffn_gate_up_weights, L1_ffn_down_weights, L1_ffn_shared_gate_up, L1_ffn_shared_down), axis=-1)
    return x

_drawn_inputs = setup_inputs


def setup_inputs(seed=0):
    import zlib

    import numpy as np

    out = dict(_drawn_inputs(seed))
    spreads = {'L0_attn_conv_b': (0.0, 0.8),
     'L1_attn_bq': (0.0, 0.685),
     'L1_attn_bk': (0.0, 0.8),
     'L1_attn_bv': (0.0, 0.1),
     'L1_attn_bo': (0.0, 0.1)}
    factors = {'L0_attn_W_in': 8.0,
     'L0_attn_conv_w': 8.0,
     'L0_attn_W_out': 8.0,
     'L0_ffn_gate_w': 8.0,
     'L0_ffn_Wg': 8.0,
     'L0_ffn_Wu': 8.0,
     'L0_ffn_Wd': 8.0,
     'L0_ffn_cWg': 8.0,
     'L0_ffn_cWu': 8.0,
     'L0_ffn_cWd': 8.0,
     'L1_ffn_gate_weight': 8.0,
     'L1_ffn_gate_up_weights': 8.0,
     'L1_ffn_down_weights': 8.0,
     'L1_ffn_shared_gate_up': 2.839,
     'L1_ffn_shared_down': 2.831}
    for name, (base, spread) in spreads.items():
        noise = np.random.default_rng([zlib.crc32(name.encode()), seed]).standard_normal(out[name].shape)
        drawn = base * np.exp(spread * noise) if base else spread * noise
        out[name] = jnp.asarray(drawn.astype(out[name].dtype))
    for name, factor in factors.items():
        out[name] = (out[name] * factor).astype(out[name].dtype)
    return out
```

```python
from contextlib import ExitStack

import numpy as np

import concourse.bass as bass
from concourse import mybir

ALU = mybir.AluOpType
ACT = mybir.ActivationFunctionType
AX_X = mybir.AxisListType.X
F32 = mybir.dt.float32
F32R = mybir.dt.float32r
BF16 = mybir.dt.bfloat16
U32 = mybir.dt.uint32
U16 = mybir.dt.uint16

P = 128
D = 256
DC = D // P
N_TOK = 8 * 256
SEQ = 256
BLK = 512
N_BLK = N_TOK // BLK
BPH = 2
N_HALF = N_BLK // BPH
TT = BLK // P
D_IN = 512
CT = D_IN // P
TAPS = 4
D_MLP = 4 * D
MT = D_MLP // P
E0, I0, C0, IC0 = 32, 96, 16, 128
E1, I1, IS1 = 16, 176, 352
TILES_L = E0 * I0 // P
TILES_S = C0 * IC0 // P
H1 = E1 * I1 + IS1
TILES_1 = -(-H1 // P)
TILES_0 = TILES_L + TILES_S
NE = 32
SMALL = 0.05
HEADS, DH, KV = 16, 128, 4
GRP = HEADS // KV
SCALE = float(1.0 / np.sqrt(np.float32(DH)))
EPS = 1e-5
TINY = 1e-24 / D


def build_program(nc, xT, w_mix, conv_wb, gw0, gw1, moe_w, sel, w_att, att_b, ident_d, outT):
    with ExitStack() as keep:
        stack = [keep]

        def sb(name, shape, dt=F32):
            return stack[-1].enter_context(nc.sbuf_tensor(name, shape, dt))

        def sem(name):
            return keep.enter_context(nc.semaphore(name))

        xh = sb("xh", [P, DC, N_TOK], F32R)
        xl = sb("xl", [P, DC, N_TOK], F32R)
        ident = sb("ident", [P, P])
        ident_r = sb("ident_r", [P, P], F32R)
        ident_b = sb("ident_b", [P, P], BF16)
        mean_w = sb("mean_w", [P, P])
        eps_c = sb("eps_c", [P, 1])
        one_c = sb("one_c", [P, 1])
        iota_f = sb("iota_f", [P, NE])
        ln_r = [sb(f"ln_r{i}", [P, DC, BLK]) for i in range(2)]
        ln_sq = sb("ln_sq", [P, DC, BLK])
        ln_sum = sb("ln_sum", [P, BLK])
        ln_std = sb("ln_std", [P, BLK])
        convw = sb("convw", [P, CT, TAPS + 1])
        attb = sb("attb", [P, HEADS + KV + KV + DC])
        gwr = sb("gwr", [P, 2, DC, NE])
        gwh = sb("gwh", [P, 2, DC, NE], F32R)
        gwl = sb("gwl", [P, 2, DC, NE], F32R)
        raw = [sb(f"raw{i}", [P, 1024]) for i in range(2)]

        with ExitStack() as phase:
            stack.append(phase)
            W_MIX = DC * 2 * D_IN + CT * D + DC * D_MLP + MT * D
            mixh = sb("mixh", [P, W_MIX], F32R)
            mixl = sb("mixl", [P, W_MIX], F32R)
            a_x = sb("a_x", [P, DC, BLK])
            a_xr = sb("a_xr", [P, DC, BLK])
            a_x1 = sb("a_x1", [P, DC, BLK])
            rsq = [sb(f"rsq{i}", [P, DC, BLK]) for i in range(2)]
            rsum = [sb(f"rsum{i}", [P, BLK]) for i in range(2)]
            rrt = [sb(f"rrt{i}", [P, BLK]) for i in range(2)]
            hh = [sb(f"hh{i}", [P, DC, BLK], F32R) for i in range(2)]
            hl = [sb(f"hl{i}", [P, DC, BLK], F32R) for i in range(2)]
            xp = [sb(f"xp{i}", [P, 2, SEQ + TAPS - 1]) for i in range(2)]
            cacc = [sb(f"cacc{i}", [P, 2, SEQ]) for i in range(2)]
            sxc = sb("sxc", [P, BLK])
            sz = [sb(f"sz{i}", [P, BLK]) for i in range(2)]
            yt = sb("yt", [P, BLK])
            yh = sb("yh", [P, CT, BLK], F32R)
            yl = sb("yl", [P, CT, BLK], F32R)
            NR = 3
            rh = sb("rh", [P, NR, BLK], F32R)
            rl = sb("rl", [P, NR, BLK], F32R)
            stack.pop()
        W_ATT = DC * HEADS * DH + 2 * DC * KV * DH + HEADS * D
        atth = sb("atth", [P, W_ATT], F32R)
        attl = sb("attl", [P, W_ATT], F32R)
        with ExitStack() as phase:
            stack.append(phase)
            WT = 3 * D
            wraw = [sb(f"wraw{i}", [P, WT]) for i in range(2)]
            selt = [sb(f"selt{i}", [3 * NE, P], BF16) for i in range(2)]
            wh = [sb(f"wh{i}", [P, WT], F32R) for i in range(2)]
            wl = [sb(f"wl{i}", [P, WT], F32R) for i in range(2)]
            sg = [sb(f"sg{i}", [P, BLK]) for i in range(2)]
            t1 = sb("t1", [P, BLK])
            t2 = [sb(f"t2_{i}", [P, BLK]) for i in range(2)]
            ah = [sb(f"ah{i}", [P, BLK], F32R) for i in range(2)]
            al = [sb(f"al{i}", [P, BLK], F32R) for i in range(2)]
            HT = BPH * TT
            lg = sb("lg", [P, HT, NE])
            lmx = sb("lmx", [P, HT])
            ex = sb("ex", [P, HT, NE])
            sc = sb("sc", [P, HT, NE])
            top = sb("top", [P, HT, 8])
            tix = sb("tix", [P, HT, 8], U32)
            tif = sb("tif", [P, HT, 8])
            msk = sb("msk", [P, HT, NE])
            eqk = sb("eqk", [P, HT, NE])
            den = sb("den", [P, HT])
            cw = sb("cw", [P, HT, NE])
            cws = sb("cws", [P, HT, NE])
            cpart = [sb(f"cpart{i}", [P, HT, 3, NE], BF16) for i in range(2)]
            cwt = [sb(f"cwt{i}", [3 * NE, BPH * BLK], BF16) for i in range(2)]
            stack.pop()
        with ExitStack() as phase:
            stack.append(phase)
            xbh = sb("xbh", [P, DC, BLK], F32R)
            xbl = sb("xbl", [P, DC, BLK], F32R)
            qh = [sb(f"qh{i}", [P, BLK], F32R) for i in range(2)]
            ql = [sb(f"ql{i}", [P, BLK], F32R) for i in range(2)]
            kh = [sb(f"kh{i}", [P, BLK], F32R) for i in range(2)]
            kl = [sb(f"kl{i}", [P, BLK], F32R) for i in range(2)]
            vh = sb("vh", [P, TT, KV * DH], F32R)
            vl = sb("vl", [P, TT, KV * DH], F32R)
            pr = [sb(f"pr{i}", [P, TT, SEQ]) for i in range(2)]
            pth = sb("pth", [P, 2, 2, SEQ], F32R)
            ptl = sb("ptl", [P, 2, 2, SEQ], F32R)
            oh = sb("oh", [P, BLK], F32R)
            ol = sb("ol", [P, BLK], F32R)
            smx = [sb(f"smx{i}", [P, TT]) for i in range(2)]
            ssum = [sb(f"ssum{i}", [P, TT]) for i in range(2)]
            stack.pop()

        ps = keep.enter_context(nc.psum_tensor("ps", [P, 8, BLK], F32))
        STAT = 7

        def f32(ap):
            return ap.bitcast(F32)

        def cols(b):
            return bass.ds(b * BLK, BLK)

        const_in = sem("const_in")
        const_ready = sem("const_ready")
        raw_in = [sem("raw_in0"), sem("raw_in1")]
        raw_hi = sem("raw_hi")
        raw_lo = sem("raw_lo")
        ax_in = sem("ax_in")
        axr_in = sem("axr_in")
        r_sq = [sem("r1_sq"), sem("r2_sq")]
        r_sum = [sem("r1_sum"), sem("r2_sum")]
        r_stat = [sem("r1_stat"), sem("r2_stat")]
        r_floor = [sem("r1_floor"), sem("r2_floor")]
        r_root = [sem("r1_root"), sem("r2_root")]
        r_inv = [sem("r1_inv"), sem("r2_inv")]
        r_h = [sem("r1_h"), sem("r2_h")]
        r_hh = [sem("r1_hh"), sem("r2_hh")]
        r_hl = [sem("r1_hl"), sem("r2_hl")]
        xp_mm = sem("xp_mm")
        z_mm = sem("z_mm")
        xp_ev = sem("xp_ev")
        z_ev = sem("z_ev")
        conv_tap = sem("conv_tap")
        xc_silu = sem("xc_silu")
        y_prod = sem("y_prod")
        y_hi = sem("y_hi")
        y_lo = sem("y_lo")
        mix_out = sem("mix_out")
        x1_done = sem("x1_done")
        x01_done = sem("x01_done")
        m1_mm = sem("m1_mm")
        m1_hi = sem("m1_hi")
        m1_lo = sem("m1_lo")
        m2_mm = sem("m2_mm")
        pad_zero = sem("pad_zero")
        n_r = sem("n_r")
        n_sum = sem("n_sum")
        n_stat = sem("n_stat")
        n_xc = sem("n_xc")
        n_sq = sem("n_sq")
        n_std = sem("n_std")
        n_inv = sem("n_inv")
        n_xn = sem("n_xn")
        n_xh = sem("n_xh")
        n_xl = sem("n_xl")
        g_mm = sem("g_mm")
        g_dve = sem("g_dve")
        g_lg = sem("g_lg")
        g_dif = sem("g_dif")
        g_exp = sem("g_exp")
        g_part = sem("g_part")
        g_tr = sem("g_tr")
        g_cwt = sem("g_cwt")
        w_in = [sem("w_in0"), sem("w_in1")]
        sel_in = [sem("sel_in0"), sem("sel_in1")]
        att_in = [sem("att_in0"), sem("att_in1")]
        att_hi = sem("att_hi")
        att_lo = sem("att_lo")
        w_hi = sem("w_hi")
        w_lo = sem("w_lo")
        seed_mm = sem("seed_mm")
        e_g = sem("e_g")
        e_u = sem("e_u")
        e_c = sem("e_c")
        e_dn = sem("e_dn")
        e_sg = sem("e_sg")
        e_t1 = sem("e_t1")
        e_t2 = sem("e_t2")
        e_ah = sem("e_ah")
        e_al = sem("e_al")
        xb_in = sem("xb_in")
        q_mm = sem("q_mm")
        k_mm = sem("k_mm")
        v_mm = sem("v_mm")
        q_hi = sem("q_hi")
        q_lo = sem("q_lo")
        k_hi = sem("k_hi")
        k_lo = sem("k_lo")
        v_hi = sem("v_hi")
        v_lo = sem("v_lo")
        s_mm = sem("s_mm")
        s_max = sem("s_max")
        s_neg = sem("s_neg")
        s_exp = sem("s_exp")
        s_inv = sem("s_inv")
        s_prob = sem("s_prob")
        t_mm = sem("t_mm")
        t_hi = sem("t_hi")
        t_lo = sem("t_lo")
        o_mm = sem("o_mm")
        o_hi = sem("o_hi")
        o_lo = sem("o_lo")
        y_mm = sem("y_mm")
        store = sem("store")

        RAWW = 1024
        N_RAW_A = W_MIX // RAWW
        N_RAW_C = W_ATT // RAWW

        def raw_load(sp, c):
            if c >= 2:
                sp.wait_ge(raw_lo, c - 1)
            sp.dma_start(raw[c % 2][:], w_mix[:, c * RAWW:(c + 1) * RAWW]).then_inc(raw_in[c % 2], 16)

        def raw_split_hi(eng, copy, c):
            eng.wait_ge(raw_in[c % 2], 16 * (c // 2 + 1))
            copy(mixh[:, c * RAWW:(c + 1) * RAWW], raw[c % 2][:]).then_inc(raw_hi, 1)

        def raw_split_lo(eng, sub, c):
            eng.wait_ge(raw_hi, c + 1)
            o = c * RAWW
            sub(mixl[:, o:o + RAWW], raw[c % 2][:], f32(mixh[:, o:o + RAWW])).then_inc(raw_lo, 1)

        o_in, o_out, o_m1 = 0, DC * 2 * D_IN, DC * 2 * D_IN + CT * D
        o_m2 = o_m1 + DC * D_MLP

        def w_in_t(w, c, ot):
            return w[:, o_in + c * 2 * D_IN + ot * P:o_in + c * 2 * D_IN + (ot + 1) * P]

        def w_out_t(w, c, m):
            return w[:, o_out + c * D + m * P:o_out + c * D + (m + 1) * P]

        def w_m1_t(w, c, j):
            return w[:, o_m1 + c * D_MLP + j * P:o_m1 + c * D_MLP + (j + 1) * P]

        def w_m2_t(w, c, m):
            return w[:, o_m2 + c * D + m * P:o_m2 + c * D + (m + 1) * P]

        o_q, o_k = 0, DC * HEADS * DH
        o_v = o_k + DC * KV * DH
        o_o = o_v + DC * KV * DH

        def w_q_t(w, c, h):
            return w[:, o_q + c * HEADS * DH + h * DH:o_q + c * HEADS * DH + (h + 1) * DH]

        def w_k_t(w, c, k):
            return w[:, o_k + c * KV * DH + k * DH:o_k + c * KV * DH + (k + 1) * DH]

        def w_v_t(w, c):
            return w[:, o_v + c * KV * DH:o_v + (c + 1) * KV * DH]

        def w_o_t(w, h, m):
            return w[:, o_o + h * D + m * P:o_o + h * D + (m + 1) * P]

        def product(out, terms, first=True, last=True):
            n = 0
            for (ah_, al_), (bh_, bl_) in terms:
                for a, b in ((ah_, bh_), (ah_, bl_), (al_, bh_)):
                    mm = nc.tensor.matmul(out, a, b, start=first and n == 0, stop=last and n == 3 * len(terms) - 1,
                                          skip_group_check=True)
                    n += 1
            return mm

        block = keep.enter_context(nc.Block())

        @block.sync
        def _(sp):
            sp.dma_start(ident[:], ident_d).then_inc(const_in, 16)
            sp.dma_start(a_x[:], xT[:, :, 0:BLK]).then_inc(ax_in, 16)
            raw_load(sp, 0)
            raw_load(sp, 1)
            sp.dma_start(convw[:], conv_wb).then_inc(const_in, 16)
            sp.dma_start(attb[:], att_b).then_inc(const_in, 16)
            sp.dma_start(gwr[:, 0], gw0).then_inc(const_in, 16)
            sp.dma_start(gwr[:, 1], gw1).then_inc(const_in, 16)
            sp.dma_start(a_xr[:], xT[:, :, 0:BLK]).then_inc(axr_in, 16)
            for c in range(2, N_RAW_A):
                raw_load(sp, c)
            with sp.Fori(1, N_BLK) as b:
                sp.wait_ge(r_h[0], b)
                sp.dma_start(a_x[:], xT[:, :, cols(b)]).then_inc(ax_in, 16)
                sp.wait_ge(n_r, b)
                sp.dma_start(a_xr[:], xT[:, :, cols(b)]).then_inc(axr_in, 16)

            def att_load(c, r):
                if not isinstance(c, int):
                    sp.wait_ge(att_lo, c - 1)
                sp.dma_start(raw[r][:], w_att[:, bass.ds(c * RAWW, RAWW)]).then_inc(att_in[r], 16)

            def tile_loads(g, t, s, first=False):
                if not first:
                    sp.wait_ge(w_lo, g - 1)
                sp.dma_start(wraw[s][:], moe_w[t]).then_inc(w_in[s], 16)
                if not first:
                    sp.wait_ge(e_c, BPH * (g - 1))
                sp.dma_start(selt[s][:].bitcast(U16), sel[t]).then_inc(sel_in[s], 16)

            sp.wait_ge(n_xl, N_BLK)
            for half in range(N_HALF):
                for s in range(2):
                    tile_loads(half * TILES_0 + s, s, s, first=half == 0)

                if half == 0:
                    for r in range(2):
                        att_load(r, r)

                def pairs(first, end, chunks):
                    with sp.Fori(first, end) as i:
                        for s in range(2):
                            tile_loads(half * TILES_0 + 2 * i + s, sp.snap(2 * i + s), s)
                        if chunks:
                            for r in range(2):
                                att_load(2 * i + r, r)
                if half == 0:
                    pairs(1, N_RAW_C // 2, True)
                    pairs(N_RAW_C // 2, TILES_0 // 2, False)
                else:
                    pairs(1, TILES_0 // 2, False)
            sp.wait_ge(n_xl, 2 * N_BLK)
            with sp.Fori(0, N_BLK) as b:
                sp.wait_ge(n_xl, b + 2 * N_BLK)
                sp.dma_start(f32(xbh[:]), f32(xh[:, :, cols(b)])).then_inc(xb_in, 16)
                sp.dma_start(f32(xbl[:]), f32(xl[:, :, cols(b)])).then_inc(xb_in, 16)
            sp.wait_ge(n_xl, 3 * N_BLK)
            base = N_HALF * TILES_0
            for half in range(N_HALF):
                g0, par = base + half * TILES_1, half * TILES_1
                for s in range(2):
                    tile_loads(g0 + s, TILES_0 + s, (par + s) % 2, first=half == 0)
                with sp.Fori(1, TILES_1 // 2) as i:
                    for s in range(2):
                        tile_loads(g0 + 2 * i + s, sp.snap(TILES_0 + 2 * i + s), (par + s) % 2)
                tile_loads(g0 + TILES_1 - 1, TILES_0 + TILES_1 - 1, (par + TILES_1 - 1) % 2)
            for b in range(N_BLK):
                sp.wait_ge(n_xn, 3 * N_BLK + b + 1)
                sp.dma_start(outT[:, :, b * BLK:(b + 1) * BLK], ln_r[b % 2][:]).then_inc(store, 16)
            sp.wait_ge(store, 16 * N_BLK)

        @block.gpsimd
        def _(pool):
            def rms_sum(i, b):
                pool.wait_ge(r_sq[i], b + 1)
                nc.gpsimd.tensor_tensor(rsum[i][:], rsq[i][:, 0], rsq[i][:, 1], ALU.add).then_inc(r_sum[i], 1)

            def ln_pool(k, r, later=True):
                if later:
                    pool.wait_ge(n_stat, 2 * k)
                pool.wait_ge(n_r, k + 1)
                nc.gpsimd.tensor_tensor(ln_sum[:], ln_r[r][:, 0], ln_r[r][:, 1], ALU.add).then_inc(n_sum, 1)
                pool.wait_ge(n_sq, k + 1)
                nc.gpsimd.tensor_tensor(ln_sum[:], ln_sq[:, 0], ln_sq[:, 1], ALU.add).then_inc(n_sum, 1)

            with pool.Fori(0, N_BLK) as b:
                rms_sum(0, b)
                for ct in range(CT):
                    pool.wait_ge(y_hi, b * CT + ct + 1)
                    nc.gpsimd.tensor_tensor(yl[:, ct], yt[:], f32(yh[:, ct]), ALU.subtract).then_inc(y_lo, 1)
                pool.wait_ge(axr_in, b * 16 + 16)
                pool.wait_ge(x1_done, b + 1)
                nc.gpsimd.tensor_tensor(a_xr[:], a_xr[:], a_x1[:], ALU.add).then_inc(x01_done, 1)
                rms_sum(1, b)
                ln_pool(b, 0, later=False)

            def pool_round(out, x):
                return nc.gpsimd.tensor_tensor(out, x, one_c[:].broadcast_to(list(x.shape)), ALU.mult)

            def tile_split(g, s, first=False):
                pool.wait_ge(w_in[s], 8 * (g - s) + 16)
                if not first:
                    pool.wait_ge(e_dn, BPH * (g - 1))
                pool_round(wh[s][:], wraw[s][:]).then_inc(w_hi, 1)
                pool.wait_ge(w_hi, g + 1)
                nc.gpsimd.tensor_tensor(wl[s][:], wraw[s][:], f32(wh[s][:]), ALU.subtract).then_inc(w_lo, 1)

            def att_split(c, r):
                pool.wait_ge(att_in[r], 8 * (c - r) + 16)
                cols_ = bass.ds(c * RAWW, RAWW)
                pool_round(atth[:, cols_], raw[r][:]).then_inc(att_hi, 1)
                pool.wait_ge(att_hi, c + 1)
                nc.gpsimd.tensor_tensor(attl[:, cols_], raw[r][:], f32(atth[:, cols_]), ALU.subtract).then_inc(att_lo, 1)

            for half in range(N_HALF):
                for s in range(2):
                    tile_split(half * TILES_0 + s, s, first=half == 0)

                if half == 0:
                    for r in range(2):
                        att_split(r, r)

                def pairs(first, end, chunks):
                    with pool.Fori(first, end) as i:
                        for s in range(2):
                            tile_split(half * TILES_0 + 2 * i + s, s)
                        if chunks:
                            for r in range(2):
                                att_split(2 * i + r, r)
                if half == 0:
                    pairs(1, N_RAW_C // 2, True)
                    pairs(N_RAW_C // 2, TILES_0 // 2, False)
                else:
                    pairs(1, TILES_0 // 2, False)
                for q in range(BPH):
                    ln_pool(N_BLK + half * BPH + q, q)
            with pool.Fori(0, N_BLK) as b:
                ln_pool(2 * N_BLK + b, 0)
            base = N_HALF * TILES_0
            for half in range(N_HALF):
                g0, par = base + half * TILES_1, half * TILES_1
                for s in range(2):
                    tile_split(g0 + s, (par + s) % 2)
                with pool.Fori(1, TILES_1 // 2) as i:
                    for s in range(2):
                        tile_split(g0 + 2 * i + s, (par + s) % 2)
                tile_split(g0 + TILES_1 - 1, (par + TILES_1 - 1) % 2)
                for q in range(BPH):
                    ln_pool(3 * N_BLK + half * BPH + q, q)

        @block.scalar
        def _(act):
            act.wait_ge(const_in, 5 * 16)
            nc.scalar.copy(gwh[:], gwr[:]).then_inc(const_ready, 1)
            nc.scalar.copy(ident_r[:], ident[:]).then_inc(const_ready, 1)
            nc.scalar.copy(ident_b[:], ident[:]).then_inc(const_ready, 1)
            for c in range(N_RAW_A):
                raw_split_hi(act, nc.scalar.copy, c)

            def rms_act(i, b, x):
                nc.scalar.activation(rsq[i][:], x[:], ACT.Square).then_inc(r_sq[i], 1)
                act.wait_ge(r_floor[i], b + 1)
                nc.scalar.activation(rrt[i][:], rrt[i][:], ACT.Sqrt).then_inc(r_root[i], 1)
                act.wait_ge(r_h[i], b + 1)
                nc.scalar.copy(hh[i][:], rsq[i][:]).then_inc(r_hh[i], 1)

            def ln_act(k, r, b, to_x=True):
                act.wait_ge(n_xc, k + 1)
                nc.scalar.activation(ln_sq[:], ln_r[r][:], ACT.Square).then_inc(n_sq, 1)
                act.wait_ge(n_stat, 2 * k + 2)
                nc.scalar.activation(ln_std[:], ps[:, STAT], ACT.Sqrt, bias=eps_c[:]).then_inc(n_std, 1)
                if to_x:
                    act.wait_ge(n_xn, k + 1)
                    nc.scalar.copy(xh[:, :, cols(b)], ln_r[r][:]).then_inc(n_xh, 1)

            with act.Fori(0, N_BLK) as b:
                act.wait_ge(ax_in, b * 16 + 16)
                rms_act(0, b, a_x)

                def xz_ev(ct):
                    act.wait_ge(xp_mm, b * CT + ct + 1)
                    nc.scalar.copy(xp[ct % 2][:, :, TAPS - 1:], ps[:, 4 + ct % 2].rearrange("p (a t) -> p a t", a=2)).then_inc(xp_ev, 1)
                    act.wait_ge(z_mm, b * CT + ct + 1)
                    nc.scalar.activation(sz[ct % 2][:], ps[:, 6], ACT.Silu).then_inc(z_ev, 1)

                def xc_act(ct):
                    act.wait_ge(conv_tap, (b * CT + ct + 1) * TAPS)
                    nc.scalar.activation(sxc[:], cacc[ct % 2][:].rearrange("p a t -> p (a t)"), ACT.Silu).then_inc(xc_silu, 1)

                def y_act(ct):
                    act.wait_ge(y_prod, b * CT + ct + 1)
                    nc.scalar.copy(yh[:, ct], yt[:]).then_inc(y_hi, 1)

                for ct in range(CT + 1):
                    if ct < CT:
                        xz_ev(ct)
                    if ct >= 1:
                        xc_act(ct - 1)
                        y_act(ct - 1)
                act.wait_ge(x1_done, b + 1)
                rms_act(1, b, a_x1)
                for j in range(MT):
                    act.wait_ge(m1_mm, b * MT + j + 1)
                    if j >= NR:
                        act.wait_ge(m2_mm, b * MT + j - NR + 1)
                    nc.scalar.activation(rh[:, j % NR], ps[:, 4 + j % 3], ACT.Relu).then_inc(m1_hi, 1)
                ln_act(b, 0, b)

            def routing_act(u, layer):
                act.wait_ge(g_dif, u + 1)
                nc.scalar.activation(ex[:], ex[:], ACT.Exp).then_inc(g_exp, 1)
                if layer == 0:
                    nc.scalar.activation(sc[:], lg[:], ACT.Exp, scale=-1.0).then_inc(g_exp, 1)

            def step_silu(n, q):
                act.wait_ge(e_g, n + 1)
                nc.scalar.activation(sg[q][:], ps[:, 4], ACT.Silu).then_inc(e_sg, 1)

            def step_hi(n, q):
                act.wait_ge(e_t2, n + 1)
                nc.scalar.copy(ah[q][:], t2[q][:]).then_inc(e_ah, 1)

            def tile_act(g, s):
                for q in range(BPH):
                    step_silu(BPH * g + q, q)
                    step_hi(BPH * g + q, q)

            def half_end_act(k0, done, b0, bias=None, to_x=True):
                act.wait_ge(e_dn, done)
                for q in range(BPH):
                    nc.scalar.copy(ln_r[q][:], ps[:, 2 * q:2 * q + 2]).then_inc(n_r, 1)
                for q in range(BPH):
                    ln_act(k0 + q, q, b0 + q, to_x)

            for half in range(N_HALF):
                routing_act(half, 0)
                with act.Fori(0, TILES_0 // 2) as i:
                    for s in range(2):
                        tile_act(half * TILES_0 + 2 * i + s, s)
                half_end_act(N_BLK + half * BPH, BPH * TILES_0 * (half + 1), half * BPH)

            def head_q(b, h):
                act.wait_ge(q_mm, b * HEADS + h + 1)
                nc.scalar.activation(qh[h % 2][:], ps[:, 6], ACT.Identity, bias=attb[:, h:h + 1]).then_inc(q_hi, 1)

            def head_soft(b, h):
                act.wait_ge(s_neg, b * HEADS + h + 1)
                for t in range(TT):
                    nc.scalar.activation(pr[h % 2][:, t], ps[:, 2 + t // 2, (t % 2) * SEQ:(t % 2 + 1) * SEQ], ACT.Exp,
                                         bias=smx[h % 2][:, t:t + 1], scale=SCALE,
                                         accum_out=ssum[h % 2][:, t:t + 1]).then_inc(s_exp, 1)

            def head_t(b, h):
                act.wait_ge(t_mm, b * HEADS + h + 1)
                nc.scalar.copy(pth[:], ps[:, 4:6].rearrange("p a (k q) -> p a k q", k=2)).then_inc(t_hi, 1)

            def head_o(b, h):
                act.wait_ge(o_mm, b * HEADS + h + 1)
                nc.scalar.activation(oh[:], ps[:, 7], ACT.Identity, bias=attb[:, HEADS + KV + h // GRP:HEADS + KV + h // GRP + 1]).then_inc(o_hi, 1)

            def kv_k(b, k):
                act.wait_ge(k_mm, b * KV + k + 1)
                nc.scalar.activation(kh[k % 2][:], ps[:, 6], ACT.Identity, bias=attb[:, HEADS + k:HEADS + k + 1]).then_inc(k_hi, 1)

            with act.Fori(0, N_BLK) as b:
                for t in range(TT):
                    act.wait_ge(v_mm, b * TT + t + 1)
                    nc.scalar.copy(vh[:, t], ps[:, 2 + t]).then_inc(v_hi, 1)
                att_schedule(b, k=kv_k, q=head_q, soft=head_soft, t=head_t, o=head_o)
                act.wait_ge(y_mm, b * HEADS + HEADS)
                for m in range(DC):
                    ins = nc.scalar.activation(ln_r[0][:, m], ps[:, m], ACT.Identity, bias=attb[:, HEADS + 2 * KV + m:HEADS + 2 * KV + m + 1])
                ins.then_inc(n_r, 1)
                ln_act(2 * N_BLK + b, 0, b)

            base = N_HALF * TILES_0
            for half in range(N_HALF):
                routing_act(N_HALF + half, 1)
                h0 = base + half * TILES_1
                par = half * TILES_1
                with act.Fori(0, TILES_1 // 2) as i:
                    for s in range(2):
                        tile_act(h0 + 2 * i + s, (par + s) % 2)
                tile_act(h0 + TILES_1 - 1, (par + TILES_1 - 1) % 2)
                if half:
                    act.wait_ge(store, 16 * BPH)
                half_end_act(3 * N_BLK + half * BPH, BPH * (base + TILES_1 * (half + 1)), half * BPH, to_x=False)

        @block.vector
        def _(dve):
            nc.vector.memset(mean_w[:], 1.0 / D).then_inc(const_ready, 1)
            nc.vector.memset(eps_c[:], EPS).then_inc(const_ready, 1)
            nc.vector.memset(one_c[:], 1.0).then_inc(const_ready, 1)
            for i in range(2):
                nc.vector.memset(xp[i][:, :, 0:TAPS - 1], 0.0).then_inc(pad_zero, 1)
            dve.wait_ge(const_ready, 6)
            nc.vector.tensor_tensor(gwl[:], gwr[:], f32(gwh[:]), ALU.subtract).then_inc(const_ready, 1)
            for c in range(N_RAW_A):
                raw_split_lo(dve, lambda o, a, b_: nc.vector.tensor_tensor(o, a, b_, ALU.subtract), c)

            def rms_dve(i, b, x):
                dve.wait_ge(r_stat[i], b + 1)
                nc.vector.tensor_scalar(rrt[i][:], ps[:, STAT], TINY, None, ALU.max).then_inc(r_floor[i], 1)
                dve.wait_ge(r_root[i], b + 1)
                nc.vector.reciprocal(rrt[i][:], rrt[i][:]).then_inc(r_inv[i], 1)
                dve.wait_ge(r_inv[i], b + 1)
                nc.vector.tensor_tensor(rsq[i][:], x[:], rrt[i][:, None, :].broadcast_to([P, DC, BLK]), ALU.mult).then_inc(r_h[i], 1)
                dve.wait_ge(r_hh[i], b + 1)
                nc.vector.tensor_tensor(hl[i][:], rsq[i][:], f32(hh[i][:]), ALU.subtract).then_inc(r_hl[i], 1)

            def ln_dve(k, r, b, to_x=True):
                dve.wait_ge(n_stat, 2 * k + 1)
                nc.vector.tensor_tensor(ln_r[r][:], ln_r[r][:], ps[:, STAT:STAT + 1].broadcast_to([P, DC, BLK]), ALU.subtract).then_inc(n_xc, 1)
                dve.wait_ge(n_std, k + 1)
                nc.vector.reciprocal(ln_std[:], ln_std[:]).then_inc(n_inv, 1)
                dve.wait_ge(n_inv, k + 1)
                nc.vector.tensor_tensor(ln_r[r][:], ln_r[r][:], ln_std[:, None, :].broadcast_to([P, DC, BLK]), ALU.mult).then_inc(n_xn, 1)
                if to_x:
                    dve.wait_ge(n_xh, k + 1)
                    nc.vector.tensor_tensor(xl[:, :, cols(b)], ln_r[r][:], f32(xh[:, :, cols(b)]), ALU.subtract).then_inc(n_xl, 1)

            with dve.Fori(0, N_BLK) as b:
                rms_dve(0, b, a_x)

                def conv(ct):
                    src, dst = xp[ct % 2], cacc[ct % 2]
                    dve.wait_ge(xp_ev, b * CT + ct + 1)
                    n = (b * CT + ct) * TAPS
                    nc.vector.tensor_scalar(dst[:], src[:, :, TAPS - 1:], convw[:, ct, TAPS - 1:TAPS], convw[:, ct, TAPS:],
                                            ALU.mult, ALU.add).then_inc(conv_tap, 1)
                    for k in range(1, TAPS):
                        w = TAPS - 1 - k
                        dve.wait_ge(conv_tap, n + k)
                        nc.vector.scalar_tensor_tensor(out=dst[:], in0=src[:, :, w:w + SEQ], scalar=convw[:, ct, w:w + 1],
                                                       in1=dst[:], op0=ALU.mult, op1=ALU.add).then_inc(conv_tap, 1)

                def prod(ct):
                    dve.wait_ge(xc_silu, b * CT + ct + 1)
                    if ct >= 1:
                        dve.wait_ge(y_lo, b * CT + ct)
                    nc.vector.tensor_tensor(yt[:], sxc[:], sz[ct % 2][:], ALU.mult).then_inc(y_prod, 1)

                for ct in range(CT + 1):
                    if ct < CT:
                        conv(ct)
                    if ct >= 1:
                        prod(ct - 1)
                dve.wait_ge(mix_out, b + 1)
                dve.wait_ge(axr_in, b * 16 + 16)
                nc.vector.tensor_tensor(a_x1[:], ps[:, 0:2], a_xr[:], ALU.add).then_inc(x1_done, 1)
                rms_dve(1, b, a_x1)
                for j in range(MT):
                    dve.wait_ge(m1_hi, b * MT + j + 1)
                    nc.vector.scalar_tensor_tensor(out=rl[:, j % NR], in0=ps[:, 4 + j % 3], scalar=0.0, in1=f32(rh[:, j % NR]),
                                                   op0=ALU.max, op1=ALU.subtract).then_inc(m1_lo, 1)
                dve.wait_ge(m2_mm, b * MT + MT)
                dve.wait_ge(x01_done, b + 1)
                nc.vector.tensor_tensor(ln_r[0][:], ps[:, 2:4], a_xr[:], ALU.add).then_inc(n_r, 1)
                ln_dve(b, 0, b)

            chain = [0]

            def link(ins):
                chain[0] += 1
                ins.then_inc(g_dve, 1)
                dve.wait_ge(g_dve, chain[0])

            for e in range(NE):
                ins = nc.vector.memset(iota_f[:, e:e + 1], float(e))
            link(ins)

            def bc(v):
                return v[:, :, None].broadcast_to([P, HT, NE])

            def routing_dve(u, layer):
                ne = E0 if layer == 0 else E1
                dve.wait_ge(g_mm, u + 1)
                link(nc.vector.tensor_copy(lg[:, :, 0:ne], ps[:, STAT, 0:HT * ne].rearrange("p (t e) -> p t e", t=HT)))
                link(nc.vector.reduce_max(lmx[:], lg[:, :, 0:ne], AX_X))
                if layer == 1:
                    link(nc.vector.memset(lg[:, :, ne:], -1e30))
                    link(nc.vector.memset(cw[:], 0.0))
                nc.vector.tensor_tensor(ex[:], lg[:], bc(lmx[:]), ALU.subtract).then_inc(g_dif, 1)
                if layer == 0:
                    dve.wait_ge(g_exp, 2 * (u + 1))
                    link(nc.vector.tensor_scalar(sc[:], sc[:], 1.0, None, ALU.add))
                    link(nc.vector.reciprocal(sc[:], sc[:]))
                else:
                    dve.wait_ge(g_exp, 2 * N_HALF + u - N_HALF + 1)
                    link(nc.vector.reduce_sum(den[:], ex[:, :, 0:ne], AX_X))
                    link(nc.vector.reciprocal(den[:], den[:]))
                    link(nc.vector.tensor_tensor(sc[:], ex[:], bc(den[:]), ALU.mult))
                for t in range(HT):
                    ins = nc.vector.max(top[:, t], sc[:, t, 0:ne])
                link(ins)
                for t in range(HT):
                    ins = nc.vector.max_index(tix[:, t], top[:, t], sc[:, t, 0:ne])
                link(ins)
                link(nc.vector.tensor_copy(tif[:], tix[:]))
                for k in range(4):
                    dst = msk if k == 0 else eqk
                    link(nc.vector.tensor_tensor(dst[:], iota_f[:, None, :].broadcast_to([P, HT, NE]), tif[:, :, k:k + 1].broadcast_to([P, HT, NE]), ALU.is_equal))
                    if k:
                        link(nc.vector.tensor_tensor(msk[:], msk[:], eqk[:], ALU.add))
                if layer == 0:
                    link(nc.vector.tensor_tensor(cw[:], ex[:], msk[:], ALU.mult))
                    link(nc.vector.reduce_sum(den[:], cw[:], AX_X))
                    link(nc.vector.reciprocal(den[:], den[:]))
                    link(nc.vector.tensor_tensor(cw[:], cw[:], bc(den[:]), ALU.mult))
                    link(nc.vector.tensor_scalar(cws[:], cw[:], SMALL, None, ALU.mult))
                else:
                    link(nc.vector.tensor_tensor(cw[:, :, 0:ne], sc[:, :, 0:ne], msk[:, :, 0:ne], ALU.mult))
                    link(nc.vector.memset(cw[:, :, ne:ne + 1], 1.0))
                for i, c in enumerate((cw, cws) if layer == 0 else (cw,)):
                    for part in range(3):
                        link(nc.vector.tensor_copy(cpart[i][:, :, part], c[:]))
                        if part < 2:
                            link(nc.vector.tensor_tensor(c[:], c[:], cpart[i][:, :, part], ALU.subtract))
                    nc.vector.tensor_copy(den[:], den[:]).then_inc(g_part, 1)
                    dve.wait_ge(g_tr, tr_count(u, i) + 1)
                    nc.vector.tensor_copy(cwt[i][:], ps[0:3 * NE, STAT].bitcast(BF16)).then_inc(g_cwt, 1)

            def tile_dve(g, s):
                for q in range(BPH):
                    n = BPH * g + q
                    dve.wait_ge(e_u, n + 1)
                    dve.wait_ge(e_sg, n + 1)
                    nc.vector.tensor_tensor(t1[:], ps[:, 5], sg[q][:], ALU.mult).then_inc(e_t1, 1)
                    dve.wait_ge(e_t1, n + 1)
                    dve.wait_ge(e_c, n + 1)
                    nc.vector.tensor_tensor(t2[q][:], ps[:, 6], t1[:], ALU.mult).then_inc(e_t2, 1)
                    dve.wait_ge(e_ah, n + 1)
                    nc.vector.tensor_tensor(al[q][:], t2[q][:], f32(ah[q][:]), ALU.subtract).then_inc(e_al, 1)

            for half in range(N_HALF):
                routing_dve(half, 0)
                with dve.Fori(0, TILES_0 // 2) as i:
                    for s in range(2):
                        tile_dve(half * TILES_0 + 2 * i + s, s)
                for q in range(BPH):
                    ln_dve(N_BLK + half * BPH + q, q, half * BPH + q)

            def head_q(b, h):
                dve.wait_ge(q_hi, b * HEADS + h + 1)
                nc.vector.scalar_tensor_tensor(out=ql[h % 2][:], in0=ps[:, 6], scalar=attb[:, h:h + 1], in1=f32(qh[h % 2][:]),
                                               op0=ALU.add, op1=ALU.subtract).then_inc(q_lo, 1)

            def head_soft(b, h):
                dve.wait_ge(s_mm, b * HEADS + h + 1)
                nc.vector.reduce_max(smx[h % 2][:], ps[:, 2:4].rearrange("p a (k q) -> p (a k) q", k=2), AX_X).then_inc(s_max, 1)
                dve.wait_ge(s_max, b * HEADS + h + 1)
                nc.vector.tensor_scalar(smx[h % 2][:], smx[h % 2][:], -SCALE, None, ALU.mult).then_inc(s_neg, 1)
                dve.wait_ge(s_exp, (b * HEADS + h + 1) * TT)
                nc.vector.reciprocal(ssum[h % 2][:], ssum[h % 2][:]).then_inc(s_inv, 1)
                dve.wait_ge(s_inv, b * HEADS + h + 1)
                nc.vector.tensor_tensor(pr[h % 2][:], pr[h % 2][:], ssum[h % 2][:, :, None].broadcast_to([P, TT, SEQ]), ALU.mult).then_inc(s_prob, 1)

            def head_t(b, h):
                dve.wait_ge(t_hi, b * HEADS + h + 1)
                nc.vector.tensor_tensor(ptl[:].rearrange("p a k q -> p a (k q)"), ps[:, 4:6], f32(pth[:]).rearrange("p a k q -> p a (k q)"), ALU.subtract).then_inc(t_lo, 1)

            def head_o(b, h):
                dve.wait_ge(o_hi, b * HEADS + h + 1)
                nc.vector.scalar_tensor_tensor(out=ol[:], in0=ps[:, 7], scalar=attb[:, HEADS + KV + h // GRP:HEADS + KV + h // GRP + 1], in1=f32(oh[:]),
                                               op0=ALU.add, op1=ALU.subtract).then_inc(o_lo, 1)

            def kv_k(b, k):
                dve.wait_ge(k_hi, b * KV + k + 1)
                nc.vector.scalar_tensor_tensor(out=kl[k % 2][:], in0=ps[:, 6], scalar=attb[:, HEADS + k:HEADS + k + 1], in1=f32(kh[k % 2][:]),
                                               op0=ALU.add, op1=ALU.subtract).then_inc(k_lo, 1)

            with dve.Fori(0, N_BLK) as b:
                for t in range(TT):
                    dve.wait_ge(v_hi, b * TT + t + 1)
                    nc.vector.tensor_tensor(vl[:, t], ps[:, 2 + t], f32(vh[:, t]), ALU.subtract).then_inc(v_lo, 1)
                att_schedule(b, k=kv_k, q=head_q, soft=head_soft, t=head_t, o=head_o)
                ln_dve(2 * N_BLK + b, 0, b)

            base = N_HALF * TILES_0
            for half in range(N_HALF):
                routing_dve(N_HALF + half, 1)
                h0 = base + half * TILES_1
                par = half * TILES_1
                with dve.Fori(0, TILES_1 // 2) as i:
                    for s in range(2):
                        tile_dve(h0 + 2 * i + s, (par + s) % 2)
                tile_dve(h0 + TILES_1 - 1, 0)
                for q in range(BPH):
                    ln_dve(3 * N_BLK + half * BPH + q, q, 0, to_x=False)

        @block.tensor
        def _(pe):
            pe.wait_ge(const_ready, 7)

            def rms_pe(i, b):
                pe.wait_ge(r_sum[i], b + 1)
                nc.tensor.matmul(ps[:, STAT], mean_w[:], rsum[i][:], start=True, stop=True).then_inc(r_stat[i], 1)

            def ln_pe(k, later=True):
                if later:
                    pe.wait_ge(n_std, k)
                pe.wait_ge(n_sum, 2 * k + 1)
                nc.tensor.matmul(ps[:, STAT], mean_w[:], ln_sum[:], start=True, stop=True).then_inc(n_stat, 1)
                pe.wait_ge(n_sum, 2 * k + 2)
                nc.tensor.matmul(ps[:, STAT], mean_w[:], ln_sum[:], start=True, stop=True).then_inc(n_stat, 1)

            pe.wait_ge(raw_lo, N_RAW_A)
            with pe.Fori(0, N_BLK) as b:
                rms_pe(0, b)
                pe.wait_ge(r_hl[0], b + 1)
                act_h = [(hh[0][:, c], hl[0][:, c]) for c in range(DC)]
                for ct in range(CT):
                    if ct >= 2:
                        pe.wait_ge(xp_ev, b * CT + ct - 1)
                    product(ps[:, 4 + ct % 2], [((w_in_t(mixh, c, ct), w_in_t(mixl, c, ct)), act_h[c]) for c in range(DC)]).then_inc(xp_mm, 1)
                    if ct >= 1:
                        pe.wait_ge(z_ev, b * CT + ct)
                    product(ps[:, 6], [((w_in_t(mixh, c, CT + ct), w_in_t(mixl, c, CT + ct)), act_h[c]) for c in range(DC)]).then_inc(z_mm, 1)
                for ct in range(CT):
                    pe.wait_ge(y_lo, b * CT + ct + 1)
                    for m in range(DC):
                        mm = product(ps[:, m], [((w_out_t(mixh, ct, m), w_out_t(mixl, ct, m)), (yh[:, ct], yl[:, ct]))],
                                     first=ct == 0, last=ct == CT - 1)
                mm.then_inc(mix_out, 1)
                rms_pe(1, b)
                pe.wait_ge(r_hl[1], b + 1)
                act_h = [(hh[1][:, c], hl[1][:, c]) for c in range(DC)]
                for j in range(MT + 2):
                    if j < MT:
                        if j >= 3:
                            pe.wait_ge(m1_lo, b * MT + j - 2)
                        product(ps[:, 4 + j % 3], [((w_m1_t(mixh, c, j), w_m1_t(mixl, c, j)), act_h[c]) for c in range(DC)]).then_inc(m1_mm, 1)
                    if j >= 2:
                        jj = j - 2
                        pe.wait_ge(m1_lo, b * MT + jj + 1)
                        for m in range(DC):
                            mm = product(ps[:, 2 + m], [((w_m2_t(mixh, jj, m), w_m2_t(mixl, jj, m)), (rh[:, jj % NR], rl[:, jj % NR]))],
                                         first=jj == 0, last=jj == MT - 1)
                        mm.then_inc(m2_mm, 1)
                ln_pe(b, later=False)

            def routing_pe(u, half, layer):
                ne = E0 if layer == 0 else E1
                pe.wait_ge(n_xl, (1 if layer == 0 else 3) * N_BLK)
                pe.wait_ge(n_std, (1 if layer == 0 else 3) * N_BLK + half * BPH)
                for t in range(HT):
                    tok = slice(half * HT * P + t * P, half * HT * P + (t + 1) * P)
                    mm = product(ps[:, STAT, t * ne:(t + 1) * ne],
                                 [((xh[:, c, tok], xl[:, c, tok]), (gwh[:, layer, c, 0:ne], gwl[:, layer, c, 0:ne])) for c in range(DC)])
                mm.then_inc(g_mm, 1)
                for i in range(2 if layer == 0 else 1):
                    pe.wait_ge(g_part, tr_count(u, i) + 1)
                    for t in range(HT):
                        mm = nc.tensor.transpose(ps[0:3 * NE, STAT].bitcast(BF16)[:, t * P:(t + 1) * P],
                                                 cpart[i][:, t].rearrange("p a e -> p (a e)"), ident_b[:])
                    mm.then_inc(g_tr, 1)

            def seed(half):
                for q in range(BPH):
                    tok = slice((half * BPH + q) * BLK, (half * BPH + q + 1) * BLK)
                    for m in range(DC):
                        nc.tensor.matmul(ps[:, 2 * q + m], ident_r[:], xh[:, m, tok], start=True, stop=False, skip_group_check=True)
                        mm = nc.tensor.matmul(ps[:, 2 * q + m], ident_r[:], xl[:, m, tok], start=False, stop=False, skip_group_check=True)
                return mm

            def down(n, s, q):
                pe.wait_ge(e_al, n + 1)
                for m in range(DC):
                    o = 2 * D + m * P
                    mm = product(ps[:, 2 * q + m], [((wh[s][:, o:o + P], wl[s][:, o:o + P]), (ah[q][:], al[q][:]))], first=False, last=True)
                mm.then_inc(e_dn, 1)

            def tile_pe(g, s, half, table, first=False):
                pe.wait_ge(w_lo, g + 1)
                for q in range(BPH):
                    n = BPH * g + q
                    tok = slice((half * BPH + q) * BLK, (half * BPH + q + 1) * BLK)
                    for bank, o, freed, done in ((4, 0, e_sg, e_g), (5, D, e_t1, e_u)):
                        if not isinstance(n, int) or n >= 1:
                            pe.wait_ge(freed, n)
                        product(ps[:, bank], [((wh[s][:, o + c * P:o + (c + 1) * P], wl[s][:, o + c * P:o + (c + 1) * P]),
                                               (xh[:, c, tok], xl[:, c, tok])) for c in range(DC)]).then_inc(done, 1)
                    if not (first and q == 0):
                        down(n - 1, s if q else 1 - s, 1 - q)
                    if not isinstance(n, int) or n >= 1:
                        pe.wait_ge(e_t2, n)
                    if q == 0:
                        pe.wait_ge(sel_in[s], 8 * (g - s) + 16)
                    nc.tensor.matmul(ps[:, 6], selt[s][:], cwt[table][:, q * BLK:(q + 1) * BLK], start=True, stop=True).then_inc(e_c, 1)

            for half in range(N_HALF):
                routing_pe(half, half, 0)
                if half:
                    pe.wait_ge(n_r, N_BLK + half * BPH)
                seed(half)
                pe.wait_ge(g_cwt, 2 * (half + 1))
                g0 = half * TILES_0
                for s in range(2):
                    tile_pe(g0 + s, s, half, 0, first=s == 0)
                with pe.Fori(1, TILES_L // 2) as i:
                    for s in range(2):
                        tile_pe(g0 + 2 * i + s, s, half, 0)
                with pe.Fori(TILES_L // 2, TILES_0 // 2) as i:
                    for s in range(2):
                        tile_pe(g0 + 2 * i + s, s, half, 1)
                down(BPH * (g0 + TILES_0) - 1, 1, 1)
                for q in range(BPH):
                    ln_pe(N_BLK + half * BPH + q)

            def kv_k(b, k):
                if k:
                    pass
                wait_q_bank(pe, b, k * GRP)
                product(ps[:, 6], [((w_k_t(atth, c, k), w_k_t(attl, c, k)), (xbh[:, c], xbl[:, c])) for c in range(DC)]).then_inc(k_mm, 1)

            def wait_q_bank(eng, b, h):
                if h:
                    eng.wait_ge(q_lo, b * HEADS + h)

            def head_q(b, h):
                if h % GRP == 0:
                    pe.wait_ge(k_lo, b * KV + h // GRP + 1)
                else:
                    wait_q_bank(pe, b, h)
                product(ps[:, 6], [((w_q_t(atth, c, h), w_q_t(attl, c, h)), (xbh[:, c], xbl[:, c])) for c in range(DC)]).then_inc(q_mm, 1)

            def head_s(b, h):
                pe.wait_ge(q_lo, b * HEADS + h + 1)
                if h:
                    pe.wait_ge(s_exp, (b * HEADS + h) * TT)
                k = (h // GRP) % 2
                for t in range(TT):
                    sq = slice((t // 2) * SEQ, (t // 2 + 1) * SEQ)
                    mm = product(ps[:, 2 + t // 2, (t % 2) * SEQ:(t % 2 + 1) * SEQ],
                                 [((qh[h % 2][:, t * P:(t + 1) * P], ql[h % 2][:, t * P:(t + 1) * P]), (kh[k][:, sq], kl[k][:, sq]))])
                mm.then_inc(s_mm, 1)

            def head_t(b, h):
                pe.wait_ge(s_prob, b * HEADS + h + 1)
                if h:
                    pe.wait_ge(t_lo, b * HEADS + h)
                for a in range(2):
                    for kt in range(2):
                        for qt in range(2):
                            mm = nc.tensor.transpose(ps[:, 4 + a, kt * SEQ + qt * P:kt * SEQ + (qt + 1) * P],
                                                     pr[h % 2][:, 2 * a + qt, kt * P:(kt + 1) * P], ident[:])
                mm.then_inc(t_mm, 1)

            def head_o(b, h):
                pe.wait_ge(t_lo, b * HEADS + h + 1)
                if h:
                    pe.wait_ge(o_lo, b * HEADS + h)
                kc = slice((h // GRP) * DH, (h // GRP + 1) * DH)
                for a in range(2):
                    mm = product(ps[:, 7, a * SEQ:(a + 1) * SEQ],
                                 [((vh[:, 2 * a + kt, kc], vl[:, 2 * a + kt, kc]), (pth[:, a, kt], ptl[:, a, kt])) for kt in range(2)])
                mm.then_inc(o_mm, 1)

            def head_y(b, h):
                pe.wait_ge(o_lo, b * HEADS + h + 1)
                for m in range(DC):
                    mm = product(ps[:, m], [((w_o_t(atth, h, m), w_o_t(attl, h, m)), (oh[:], ol[:]))], first=False, last=h == HEADS - 1)
                mm.then_inc(y_mm, 1)

            pe.wait_ge(att_lo, N_RAW_C)
            with pe.Fori(0, N_BLK) as b:
                pe.wait_ge(xb_in, b * 32 + 32)
                pe.wait_ge(n_r, b + 2 * N_BLK)
                for m in range(DC):
                    nc.tensor.matmul(ps[:, m], ident_r[:], xbh[:, m], start=True, stop=False, skip_group_check=True)
                    nc.tensor.matmul(ps[:, m], ident_r[:], xbl[:, m], start=False, stop=False, skip_group_check=True)
                for t in range(TT):
                    tok = slice(t * P, (t + 1) * P)
                    product(ps[:, 2 + t], [((xbh[:, c, tok], xbl[:, c, tok]), (w_v_t(atth, c), w_v_t(attl, c))) for c in range(DC)]).then_inc(v_mm, 1)
                pe.wait_ge(v_lo, b * TT + TT)
                att_schedule(b, k=kv_k, q=head_q, s=head_s, t=head_t, o=head_o, y=head_y)
                ln_pe(2 * N_BLK + b)

            base = N_HALF * TILES_0
            for half in range(N_HALF):
                routing_pe(N_HALF + half, half, 1)
                pe.wait_ge(n_r, 3 * N_BLK + half * BPH)
                seed(half)
                pe.wait_ge(g_cwt, 2 * N_HALF + half + 1)
                g0 = base + half * TILES_1
                par = half * TILES_1
                for s in range(2):
                    tile_pe(g0 + s, (par + s) % 2, half, 0, first=s == 0)
                with pe.Fori(1, TILES_1 // 2) as i:
                    for s in range(2):
                        tile_pe(g0 + 2 * i + s, (par + s) % 2, half, 0)
                last = (par + TILES_1 - 1) % 2
                tile_pe(g0 + TILES_1 - 1, last, half, 0)
                down(BPH * (g0 + TILES_1) - 1, last, 1)
                for q in range(BPH):
                    ln_pe(3 * N_BLK + half * BPH + q)


def tr_count(u, i):
    return 2 * u + i if u < N_HALF else 2 * N_HALF + (u - N_HALF)


def att_schedule(b, k=None, q=None, s=None, soft=None, t=None, o=None, y=None):
    for h in range(-3, HEADS + 1):
        if t and 0 <= h < HEADS:
            t(b, h)
        if h + 3 < HEADS:
            if k and (h + 3) % GRP == 0:
                k(b, (h + 3) // GRP)
            if q:
                q(b, h + 3)
        if y and 1 <= h <= HEADS:
            y(b, h - 1)
        if o and 0 <= h < HEADS:
            o(b, h)
        if 0 <= h + 2 < HEADS:
            if s:
                s(b, h + 2)
            if soft:
                soft(b, h + 2)


def _rows(w, k):
    n = w.shape[1]
    return w.reshape(k, P, n).transpose(1, 0, 2).reshape(P, k * n)


def _tiles(gate, up, down, n_tiles):
    hidden = gate.shape[0]
    out = np.zeros((n_tiles, P, 3, D), gate.dtype)
    for w, which in ((gate, 0), (up, 1), (down, 2)):
        full = np.zeros((n_tiles * P, D), w.dtype)
        full[:hidden] = w
        full = full.reshape(n_tiles, P, D)
        if which < 2:
            full = full.reshape(n_tiles, P, DC, P).transpose(0, 3, 2, 1).reshape(n_tiles, P, D)
        out[:, :, which] = full
    return out.reshape(n_tiles, P, 3 * D)


def _selectors():
    one = 0x3F80
    s = np.zeros((TILES_0 + TILES_1, 3, NE, P), np.uint16)
    for t in range(TILES_L):
        for r in range(P):
            s[t, :, (t * P + r) // I0, r] = one
    for t in range(TILES_S):
        s[TILES_L + t, :, 2 * t:2 * t + 2, :] = one
    for t in range(TILES_1):
        for r in range(P):
            row = t * P + r
            if row < H1:
                s[TILES_0 + t, :, min(row // I1, E1), r] = one
    return s.reshape(TILES_0 + TILES_1, 3 * NE, P)


def kernel(**inputs):
    import concourse.bacc as bacc
    from concourse.bass_utils import run_bass_kernel_spmd

    a = {k: np.ascontiguousarray(v) for k, v in inputs.items()}
    x = a["L0_attn_x"].reshape(N_TOK, D)
    arrays = {
        "x_t": x.T.reshape(DC, P, N_TOK).transpose(1, 0, 2),
        "w_mix": np.concatenate([
            _rows(a["L0_attn_W_in"].T, DC), _rows(a["L0_attn_W_out"].T, CT),
            _rows(a["L0_attn_W_mlp1"].T, DC), _rows(a["L0_attn_W_mlp2"].T, MT)], axis=1),
        "conv_wb": np.concatenate([
            a["L0_attn_conv_w"].reshape(CT, P, TAPS), a["L0_attn_conv_b"].reshape(CT, P, 1)], axis=2).transpose(1, 0, 2),
    }
    gates = []
    for w in (a["L0_ffn_gate_w"], a["L1_ffn_gate_weight"]):
        g = np.zeros((NE, D), w.dtype)
        g[:w.shape[0]] = w
        gates.append(_rows(g.T, DC).reshape(P, DC, NE))
    arrays["gw0"], arrays["gw1"] = gates

    def hidden_first(w):
        return w.transpose(0, 2, 1).reshape(-1, D)

    gu, dn = a["L1_ffn_gate_up_weights"], a["L1_ffn_down_weights"]
    sgu, sdn = a["L1_ffn_shared_gate_up"], a["L1_ffn_shared_down"]
    arrays["moe_w"] = np.concatenate([
        _tiles(hidden_first(a["L0_ffn_Wg"]), hidden_first(a["L0_ffn_Wu"]), a["L0_ffn_Wd"].reshape(-1, D), TILES_L),
        _tiles(hidden_first(a["L0_ffn_cWg"]), hidden_first(a["L0_ffn_cWu"]), a["L0_ffn_cWd"].reshape(-1, D), TILES_S),
        _tiles(np.concatenate([gu[:, :I1].reshape(-1, D), sgu[:IS1]]),
               np.concatenate([gu[:, I1:].reshape(-1, D), sgu[IS1:]]),
               np.concatenate([hidden_first(dn), sdn.T]), TILES_1)])
    arrays["sel"] = _selectors()
    arrays["w_att"] = np.concatenate([
        _rows(a["L1_attn_Wq"], DC), _rows(a["L1_attn_Wk"], DC), _rows(a["L1_attn_Wv"], DC), _rows(a["L1_attn_Wo"], HEADS)], axis=1)
    arrays["att_b"] = np.concatenate([
        a["L1_attn_bq"].reshape(HEADS, P), a["L1_attn_bk"].reshape(KV, P), a["L1_attn_bv"].reshape(KV, P),
        a["L1_attn_bo"].reshape(DC, P)]).T
    arrays["ident"] = np.eye(P, dtype=np.float32)
    arrays = {k: np.ascontiguousarray(v) for k, v in arrays.items()}

    nc = bacc.Bacc("TRN2", target_bir_lowering=False, num_devices=1)
    ins = [nc.dram_tensor(f"in_{k}", v.shape, mybir.dt.from_np(v.dtype), kind="ExternalInput").ap() for k, v in arrays.items()]
    out = nc.dram_tensor("out_t", (P, DC, N_TOK), F32, kind="ExternalOutput").ap()
    by = dict(zip(arrays, ins))
    build_program(nc, by["x_t"], by["w_mix"], by["conv_wb"], by["gw0"], by["gw1"], by["moe_w"], by["sel"],
                  by["w_att"], by["att_b"], by["ident"], out)
    r = run_bass_kernel_spmd(nc, [{f"in_{k}": v for k, v in arrays.items()}], core_ids=[0])
    got = r.results[0]["out_t"]
    return np.ascontiguousarray(got.transpose(1, 0, 2).reshape(D, N_TOK).T).reshape(8, SEQ, D)
```

```python
from contextlib import ExitStack

import numpy as np

import concourse.bass as bass
from concourse import mybir

ALU = mybir.AluOpType
ACT = mybir.ActivationFunctionType
AX_X = mybir.AxisListType.X
F32 = mybir.dt.float32
F32R = mybir.dt.float32r
BF16 = mybir.dt.bfloat16
U32 = mybir.dt.uint32
U16 = mybir.dt.uint16

P = 128
D = 256
DC = D // P
N_TOK = 8 * 256
SEQ = 256
BLK = 512
N_BLK = N_TOK // BLK
BPH = 2
N_HALF = N_BLK // BPH
TT = BLK // P
D_IN = 512
CT = D_IN // P
TAPS = 4
D_MLP = 4 * D
MT = D_MLP // P
E0, I0, C0, IC0 = 32, 96, 16, 128
E1, I1, IS1 = 16, 176, 352
TILES_L = E0 * I0 // P
TILES_S = C0 * IC0 // P
H1 = E1 * I1 + IS1
TILES_1 = -(-H1 // P)
TILES_0 = TILES_L + TILES_S
NE = 32
SMALL = 0.05
HEADS, DH, KV = 16, 128, 4
GRP = HEADS // KV
VP = 4
SCALE = float(1.0 / np.sqrt(np.float32(DH)))
EPS = 1e-5
TOP_K = 4
TINY = 1e-24 / D


def build_program(nc, xT, w_mix, conv_wb, gw0, gw1, moe_w, sel, w_att, att_b, ident_d, outT):
    with ExitStack() as keep:
        stack = [keep]

        def sb(name, shape, dt=F32):
            return stack[-1].enter_context(nc.sbuf_tensor(name, shape, dt))

        def sem(name):
            return keep.enter_context(nc.semaphore(name))

        xh = sb("xh", [P, DC, N_TOK], F32R)
        xl = sb("xl", [P, DC, N_TOK], F32R)
        ident = sb("ident", [P, P])
        ident_r = sb("ident_r", [P, P], F32R)
        ident_b = sb("ident_b", [P, P], BF16)
        mean_w = sb("mean_w", [P, P])
        half_c = sb("half_c", [P, 1])
        one_c = sb("one_c", [P, 1])
        iota_f = sb("iota_f", [P, NE])
        ln_r = [sb(f"ln_r{i}", [P, DC, BLK]) for i in range(2)]
        n_sqb = sb("n_sqb", [P, DC, BLK])
        n_sumb = sb("n_sumb", [P, BLK])
        n_inb = sb("n_inb", [P, TT])
        n_powb = sb("n_powb", [P, TT])
        convw = sb("convw", [P, CT, TAPS + 1])
        attb = sb("attb", [P, HEADS + KV + KV + DC])
        gwr = sb("gwr", [P, 2, DC, NE])
        gwh = sb("gwh", [P, 2, DC, NE], F32R)
        gwl = sb("gwl", [P, 2, DC, NE], F32R)
        HT = BPH * TT
        lgt = sb("lgt", [NE, BPH, BLK])
        lg = sb("lg", [P, HT, NE])
        lmx = sb("lmx", [P, HT])
        ex = sb("ex", [P, HT, NE])
        sc = sb("sc", [P, HT, NE])
        top = sb("top", [P, HT, 8])
        tix = sb("tix", [P, HT, 8], U32)
        tif = sb("tif", [P, HT, 8])
        msk = sb("msk", [P, HT, NE])
        eqk = sb("eqk", [P, HT, NE])
        den = sb("den", [P, HT])
        cw = sb("cw", [P, HT, NE])
        cpart = [sb("cpart0", [P, HT, 3, NE], BF16)]
        cwt = [sb("cwt0", [3 * NE, N_HALF, BPH * BLK], BF16)]

        W_MIX = DC * 2 * D_IN + CT * D + DC * D_MLP + MT * D
        W_ATT = DC * HEADS * DH + 2 * DC * KV * DH + HEADS * D
        NR = 3
        WT = 3 * D
        with ExitStack() as phase:
            stack.append(phase)
            mixh = sb("mixh", [P, W_MIX], F32R)
            mixl = sb("mixl", [P, W_MIX], F32R)
            hh = [sb(f"hh{i}", [P, DC, BLK], F32R) for i in range(2)]
            hl = [sb(f"hl{i}", [P, DC, BLK], F32R) for i in range(2)]
            yh = sb("yh", [P, CT, BLK], F32R)
            stack.pop()
        atth = sb("atth", [P, W_ATT], F32R)
        attl = sb("attl", [P, W_ATT], F32R)
        with ExitStack() as tables:
            stack.append(tables)
            cws = sb("cws", [P, HT, NE])
            cpart.append(sb("cpart1", [P, HT, 3, NE], BF16))
            cwt.append(sb("cwt1", [3 * NE, N_HALF, BPH * BLK], BF16))
            with ExitStack() as phase:
                stack.append(phase)
                a_x = sb("a_x", [P, DC, BLK])
                xp = [sb(f"xp{i}", [P, 2, SEQ + TAPS - 1]) for i in range(2)]
                cacc = [sb(f"cacc{i}", [P, 2, SEQ]) for i in range(2)]
                sxc = sb("sxc", [P, BLK])
                sz = [sb(f"sz{i}", [P, BLK]) for i in range(2)]
                yt = sb("yt", [P, BLK])
                yl = sb("yl", [P, CT, BLK], F32R)
                rh = sb("rh", [P, NR, BLK], F32R)
                rl = sb("rl", [P, NR, BLK], F32R)
                a_xr = sb("a_xr", [P, DC, BLK])
                a_x1 = sb("a_x1", [P, DC, BLK])
                stack.pop()
            with ExitStack() as phase:
                stack.append(phase)
                wraw = [sb(f"wraw{i}", [P, WT]) for i in range(2)]
                whl = [(sb(f"wh{i}", [P, WT], F32R), sb(f"wl{i}", [P, WT], F32R)) for i in range(2)]
                wh, wl = [h for h, _ in whl], [l for _, l in whl]
                selt = [sb(f"selt{i}", [3 * NE, P], BF16) for i in range(2)]
                sg = [sb(f"sg{i}", [P, BLK]) for i in range(2)]
                t1 = sb("t1", [P, BLK])
                t2 = [sb(f"t2_{i}", [P, BLK]) for i in range(2)]
                ah = [sb(f"ah{i}", [P, BLK], F32R) for i in range(2)]
                al = [sb(f"al{i}", [P, BLK], F32R) for i in range(2)]
                raw = sb("raw", [P, 1024])
                stack.pop()
            stack.pop()
        with ExitStack() as phase:
            stack.append(phase)
            xbh = sb("xbh", [P, DC, BLK], F32R)
            xbl = sb("xbl", [P, DC, BLK], F32R)
            qh = [sb(f"qh{i}", [P, BLK], F32R) for i in range(2)]
            ql = [sb(f"ql{i}", [P, BLK], F32R) for i in range(2)]
            kh = [sb(f"kh{i}", [P, BLK], F32R) for i in range(2)]
            kl = [sb(f"kl{i}", [P, BLK], F32R) for i in range(2)]
            vh = sb("vh", [P, TT, KV * DH], F32R)
            vl = sb("vl", [P, TT, KV * DH], F32R)
            pr = [sb(f"pr{i}", [P, TT, SEQ]) for i in range(2)]
            pth = sb("pth", [P, 2, 2, SEQ], F32R)
            ptl = sb("ptl", [P, 2, 2, SEQ], F32R)
            oh = sb("oh", [P, BLK], F32R)
            ol = sb("ol", [P, BLK], F32R)
            smx = [sb(f"smx{i}", [P, TT]) for i in range(2)]
            ssum = [sb(f"ssum{i}", [P, TT]) for i in range(2)]
            stack.pop()

        ps = keep.enter_context(nc.psum_tensor("ps", [P, 8, BLK], F32))
        STAT = 7

        def f32(ap):
            return ap.bitcast(F32)

        def cols(b):
            return bass.ds(b * BLK, BLK)

        const_in = sem("const_in")
        const_ready = sem("const_ready")
        gwl_ready = sem("gwl_ready")
        mix_in = [sem("mix_in0"), sem("mix_in1")]
        mix_hi = sem("mix_hi")
        mix_lo = sem("mix_lo")
        ax_in = sem("ax_in")
        axr_in = sem("axr_in")
        n_sq = sem("n_sq")
        n_sum = sem("n_sum")
        n_stat = sem("n_stat")
        n_in = sem("n_in")
        n_pow = sem("n_pow")
        n_bc = sem("n_bc")
        n_x = sem("n_x")
        r_hh = sem("r_hh")
        r_hl = sem("r_hl")
        l_r = sem("l_r")
        l_sum = sem("l_sum")
        l_mean = sem("l_mean")
        l_xc = sem("l_xc")
        l_xh = sem("l_xh")
        l_xl = sem("l_xl")
        pad_zero = sem("pad_zero")
        xp_mm = sem("xp_mm")
        z_mm = sem("z_mm")
        xp_ev = sem("xp_ev")
        z_ev = sem("z_ev")
        conv_tap = sem("conv_tap")
        xc_silu = sem("xc_silu")
        y_prod = sem("y_prod")
        y_hi = sem("y_hi")
        y_lo = sem("y_lo")
        mix_out = sem("mix_out")
        x1_done = sem("x1_done")
        x01_done = sem("x01_done")
        m1_mm = sem("m1_mm")
        m1_hi = sem("m1_hi")
        m1_lo = sem("m1_lo")
        m2_mm = sem("m2_mm")
        g_mm = sem("g_mm")
        g_dve = sem("g_dve")
        g_lt = sem("g_lt")
        g_col = sem("g_col")
        g_lg = sem("g_lg")
        g_dif = sem("g_dif")
        g_exp = sem("g_exp")
        g_part = sem("g_part")
        g_tr = sem("g_tr")
        g_cwt = sem("g_cwt")
        w_in = [sem("w_in0"), sem("w_in1")]
        sel_in = [sem("sel_in0"), sem("sel_in1")]
        att_in = sem("att_in")
        att_hi = sem("att_hi")
        att_lo = sem("att_lo")
        w_hi = sem("w_hi")
        w_lo = sem("w_lo")
        e_g = sem("e_g")
        e_u = sem("e_u")
        e_c = sem("e_c")
        e_dn = sem("e_dn")
        e_sg = sem("e_sg")
        e_t1 = sem("e_t1")
        e_t2 = sem("e_t2")
        e_ah = sem("e_ah")
        e_al = sem("e_al")
        xb_in = sem("xb_in")
        q_mm = sem("q_mm")
        k_mm = sem("k_mm")
        v_mm = sem("v_mm")
        q_hi = sem("q_hi")
        q_lo = sem("q_lo")
        k_hi = sem("k_hi")
        k_lo = sem("k_lo")
        v_hi = sem("v_hi")
        v_lo = sem("v_lo")
        s_mm = sem("s_mm")
        s_max = sem("s_max")
        s_neg = sem("s_neg")
        s_exp = sem("s_exp")
        s_inv = sem("s_inv")
        s_prob = sem("s_prob")
        t_mm = sem("t_mm")
        t_hi = sem("t_hi")
        t_lo = sem("t_lo")
        o_mm = sem("o_mm")
        o_hi = sem("o_hi")
        o_lo = sem("o_lo")
        y_mm = sem("y_mm")
        store = sem("store")

        R1, R2, LN = "first", "second", "layer"
        order = [(R1, 0), (R1, 1)]
        for b in range(N_BLK):
            order += [(LN, b - 1)] * (b >= 1) + [(R2, b)] + [(R1, b + 2)] * (b + 2 < N_BLK)
        order += [(LN, k) for k in range(N_BLK - 1, 4 * N_BLK)]
        rank = {norm: n for n, norm in enumerate(order)}
        r_rank = {norm: n for n, norm in enumerate(x for x in order if x[0] != LN)}
        LN_OFF = rank[(LN, N_BLK)] - N_BLK

        def ln_rank(k):
            return rank[(LN, k)] if isinstance(k, int) else k + LN_OFF

        def r_of(k):
            if not isinstance(k, int):
                return ln_r[0]
            return ln_r[{2 * N_BLK - 2: 1, 2 * N_BLK - 1: 0}.get(k, 0 if 2 * N_BLK <= k < 3 * N_BLK else k % 2)]

        ROUTE_AFTER = {0: ln_rank(N_BLK - 2) + 1, 1: ln_rank(N_BLK - 1) + 1, 2: ln_rank(3 * N_BLK - 3) + 1, 3: ln_rank(3 * N_BLK - 1) + 1}

        def due_norms(phase_d, half):
            k0 = (3 if phase_d else 1) * N_BLK
            return [k0, k0 + 1] if half else [k0 - 1]

        def att_norms(b):
            if isinstance(b, int) and b == 0:
                k = 2 * N_BLK - 2
                return {3: k, 8: k + 1}, {4: k, 11: k + 1}, {7: k, 12: k + 1}
            k = b + 2 * N_BLK - 1
            return {3: k}, {4: k}, {7: k}

        def att_norm_block(b, h):
            if isinstance(b, int) and b == 0:
                return N_BLK - 2 if h < 10 else N_BLK - 1
            return b - 1

        RAWW = 1024
        N_RAW_A = W_MIX // RAWW
        N_RAW_C = W_ATT // RAWW
        ROUTE_PAIRS = 4
        PAIRS_N = 2
        o_in, o_out, o_m1 = 0, DC * 2 * D_IN, DC * 2 * D_IN + CT * D
        o_m2 = o_m1 + DC * D_MLP

        def pair(hi, lo, o, n=P):
            return hi[:, o:o + n], lo[:, o:o + n]

        def w_in_t(c, ot):
            return pair(mixh, mixl, o_in + c * 2 * D_IN + ot * P)

        def w_out_t(c, m):
            return pair(mixh, mixl, o_out + c * D + m * P)

        def w_m1_t(c, j):
            return pair(mixh, mixl, o_m1 + c * D_MLP + j * P)

        def w_m2_t(c, m):
            return pair(mixh, mixl, o_m2 + c * D + m * P)

        o_q, o_k = 0, DC * HEADS * DH
        o_v = o_k + DC * KV * DH
        o_o = o_v + DC * KV * DH

        def w_q_t(c, h):
            return pair(atth, attl, o_q + c * HEADS * DH + h * DH)

        def w_k_t(c, k):
            return pair(atth, attl, o_k + c * KV * DH + k * DH)

        def w_v_t(c, g):
            return pair(atth, attl, o_v + c * KV * DH + g * 2 * DH, 2 * DH)

        def v_part(v, i):
            return v[:, (i % 2) * 2:(i % 2) * 2 + 2, (i // 2) * 2 * DH:(i // 2 + 1) * 2 * DH]

        def k_bank(b, k):
            return 6

        def q_bank(b, h):
            return {0: 4, 1: 5, 2: 7}.get(h, 6) if isinstance(b, int) and b == 0 else 6

        def v_bank(b, i):
            return 7 if isinstance(b, int) and b == 0 and i == 1 else 6

        def w_o_t(h, m):
            return pair(atth, attl, o_o + h * D + m * P)

        def product(out, terms, first=True, last=True):
            n = 0
            for (ah_, al_), (bh_, bl_) in terms:
                for a, b in ((ah_, bh_), (ah_, bl_), (al_, bh_)):
                    mm = nc.tensor.matmul(out, a, b, start=first and n == 0, stop=last and n == 3 * len(terms) - 1,
                                          skip_group_check=True)
                    n += 1
            return mm

        def first_tile(phase_d, half):
            return (N_HALF * TILES_0 + half * TILES_1) if phase_d else half * TILES_0

        block = keep.enter_context(nc.Block())

        @block.sync
        def _(sp):
            def mix_load(c):
                if c >= 2:
                    sp.wait_ge(mix_lo, c - 1)
                sp.dma_start(ln_r[c % 2][:].rearrange("p a b -> p (a b)"), w_mix[:, c * RAWW:(c + 1) * RAWW]).then_inc(mix_in[c % 2], 16)

            def x_load(dst, b, done):
                sp.dma_start(dst[:], xT[:, :, b * BLK:(b + 1) * BLK]).then_inc(done, 16)

            x_load(a_x, 0, ax_in)
            mix_load(0)
            mix_load(1)
            sp.dma_start(ident[:], ident_d).then_inc(const_in, 16)
            sp.dma_start(convw[:], conv_wb).then_inc(const_in, 16)
            sp.dma_start(attb[:], att_b).then_inc(const_in, 16)
            sp.dma_start(gwr[:, 0], gw0).then_inc(const_in, 16)
            sp.dma_start(gwr[:, 1], gw1).then_inc(const_in, 16)
            mix_load(2)
            x_load(a_xr, 0, axr_in)
            sp.wait_ge(n_x, rank[(R1, 0)] + 1)
            x_load(a_x, 1, ax_in)
            for c in range(3, N_RAW_A):
                mix_load(c)
            for b in range(1, N_BLK):
                if b + 1 < N_BLK:
                    sp.wait_ge(n_x, rank[(R1, b)] + 1)
                    x_load(a_x, b + 1, ax_in)
                sp.wait_ge(l_r, b)
                x_load(a_xr, b, axr_in)

            def att_load(c):
                if not isinstance(c, int):
                    sp.wait_ge(att_lo, c)
                sp.dma_start(raw[:], w_att[:, bass.ds(c * RAWW, RAWW)]).then_inc(att_in, 16)

            def tile_loads(g, t, s, first=False):
                if not first:
                    sp.wait_ge(w_lo, g - 1)
                sp.dma_start(wraw[s][:], moe_w[t]).then_inc(w_in[s], 16)
                if not first:
                    sp.wait_ge(e_c, BPH * (g - 1))
                sp.dma_start(selt[s][:].bitcast(U16), sel[t]).then_inc(sel_in[s], 16)

            sp.wait_ge(mix_out, N_BLK)
            for half in range(N_HALF):
                for s in range(2):
                    tile_loads(half * TILES_0 + s, s, s, first=half == 0)
                if half:
                    with sp.Fori(1, TILES_0 // 2) as i:
                        for s in range(2):
                            tile_loads(half * TILES_0 + 2 * i + s, sp.snap(2 * i + s), s)
                    continue
                for s in range(2):
                    tile_loads(2 + s, 2 + s, s)
                tile_loads(2 * PAIRS_N, 2 * PAIRS_N, 0)
                sp.wait_ge(e_g, 1)
                att_load(0)
                tile_loads(2 * PAIRS_N + 1, 2 * PAIRS_N + 1, 1)
                with sp.Fori(PAIRS_N + 1, PAIRS_N + N_RAW_C) as i:
                    tile_loads(2 * i, sp.snap(2 * i), 0)
                    att_load(i - PAIRS_N)
                    tile_loads(2 * i + 1, sp.snap(2 * i + 1), 1)
                with sp.Fori(PAIRS_N + N_RAW_C, TILES_0 // 2) as i:
                    for s in range(2):
                        tile_loads(2 * i + s, sp.snap(2 * i + s), s)
            sp.wait_ge(e_dn, BPH * N_HALF * TILES_0)
            for b in range(N_BLK):
                if b:
                    sp.wait_ge(v_mm, b * VP)
                sp.wait_ge(l_xl, N_BLK + b + 1)
                sp.dma_start(f32(xbh[:]), f32(xh[:, :, b * BLK:(b + 1) * BLK])).then_inc(xb_in, 16)
                sp.dma_start(f32(xbl[:]), f32(xl[:, :, b * BLK:(b + 1) * BLK])).then_inc(xb_in, 16)
            sp.wait_ge(v_mm, N_BLK * VP)
            sp.wait_ge(s_mm, N_BLK * HEADS)
            for half in range(N_HALF):
                g0 = first_tile(True, half)
                for s in range(2):
                    tile_loads(g0 + s, TILES_0 + s, (g0 + s) % 2, first=half == 0)
                with sp.Fori(1, TILES_1 // 2) as i:
                    for s in range(2):
                        tile_loads(g0 + 2 * i + s, sp.snap(TILES_0 + 2 * i + s), (g0 + s) % 2)
                tile_loads(g0 + TILES_1 - 1, TILES_0 + TILES_1 - 1, (g0 + TILES_1 - 1) % 2)
            for b in range(N_BLK):
                sp.wait_ge(n_x, ln_rank(3 * N_BLK + b) + 1)
                sp.dma_start(outT[:, :, b * BLK:(b + 1) * BLK], r_of(3 * N_BLK + b)[:]).then_inc(store, 16)
            sp.wait_ge(store, 16 * N_BLK)

        @block.gpsimd
        def _(pool):
            def norm_sum(n):
                pool.wait_ge(n_sq, n + 1)
                nc.gpsimd.tensor_tensor(n_sumb[:], n_sqb[:, 0], n_sqb[:, 1], ALU.add).then_inc(n_sum, 1)

            def norm_pow(n):
                pool.wait_ge(n_in, n + 1)
                nc.gpsimd.tensor_tensor(n_powb[:], n_inb[:], half_c[:].broadcast_to([P, TT]), ALU.pow).then_inc(n_pow, 1)

            def norm(n):
                norm_sum(n)
                norm_pow(n)

            def ln_sum(k):
                pool.wait_ge(l_r, k + 1)
                pool.wait_ge(n_stat, ln_rank(k))
                nc.gpsimd.tensor_tensor(n_sumb[:], r_of(k)[:, 0], r_of(k)[:, 1], ALU.add).then_inc(l_sum, 1)

            def ln(k):
                ln_sum(k)
                norm(ln_rank(k))

            def y_low(b, ct):
                pool.wait_ge(y_hi, b * CT + ct + 1)
                if b >= 1:
                    pool.wait_ge(mix_out, b)
                nc.gpsimd.tensor_tensor(yl[:, ct], yt[:], f32(yh[:, ct]), ALU.subtract).then_inc(y_lo, 1)

            pool.wait_ge(const_ready, 7)
            norm(rank[(R1, 0)])
            norm(rank[(R1, 1)])
            for ct in range(CT):
                y_low(0, ct)
            for b in range(N_BLK):
                if b >= 1:
                    ln(b - 1)
                pool.wait_ge(x1_done, b + 1)
                norm_sum(rank[(R2, b)])
                nc.gpsimd.tensor_tensor(a_xr[:], a_xr[:], a_x1[:], ALU.add).then_inc(x01_done, 1)
                norm_pow(rank[(R2, b)])
                for ct in range(CT):
                    if b + 1 < N_BLK:
                        y_low(b + 1, ct)
                if b + 2 < N_BLK:
                    norm(rank[(R1, b + 2)])

            def pool_round(out, x):
                return nc.gpsimd.tensor_tensor(out, x, one_c[:].broadcast_to(list(x.shape)), ALU.mult)

            def tile_split(g, s, first=False):
                pool.wait_ge(w_in[s], 8 * (g - s) + 16)
                if not first:
                    pool.wait_ge(e_dn, BPH * (g - 1))
                pool_round(wh[s][:], wraw[s][:]).then_inc(w_hi, 1)
                pool.wait_ge(w_hi, g + 1)
                nc.gpsimd.tensor_tensor(wl[s][:], wraw[s][:], f32(wh[s][:]), ALU.subtract).then_inc(w_lo, 1)

            def att_split(c):
                pool.wait_ge(att_in, 16 * c + 16)
                at = bass.ds(c * RAWW, RAWW)
                pool_round(atth[:, at], raw[:]).then_inc(att_hi, 1)
                pool.wait_ge(att_hi, c + 1)
                nc.gpsimd.tensor_tensor(attl[:, at], raw[:], f32(atth[:, at]), ALU.subtract).then_inc(att_lo, 1)

            def first_pairs(phase_d, half):
                g0 = first_tile(phase_d, half)
                tile_split(g0, g0 % 2, first=g0 == 0)
                if phase_d and not half:
                    pool.wait_ge(y_mm, N_BLK * HEADS)
                tile_split(g0 + 1, (g0 + 1) % 2, first=g0 == 0)
                for i, k in enumerate(due_norms(phase_d, half)):
                    g = g0 + 2 * (i + 1)
                    ln_sum(k)
                    tile_split(g, g % 2)
                    norm_sum(ln_rank(k))
                    tile_split(g + 1, (g + 1) % 2)
                    norm_pow(ln_rank(k))

            for half in range(N_HALF):
                first_pairs(False, half)

                def pairs(first, end, chunks=False):
                    with pool.Fori(first, end) as i:
                        for s in range(2):
                            tile_split(half * TILES_0 + 2 * i + s, s)
                        if chunks:
                            att_split(i - PAIRS_N)
                if half == 0:
                    pairs(PAIRS_N, PAIRS_N + N_RAW_C, chunks=True)
                    pairs(PAIRS_N + N_RAW_C, TILES_0 // 2)
                else:
                    pairs(3, TILES_0 // 2)
            ln(2 * N_BLK - 2)
            with pool.Fori(0, N_BLK) as b:
                ln(2 * N_BLK - 1 + b)
            for half in range(N_HALF):
                g0 = first_tile(True, half)
                first_pairs(True, half)
                with pool.Fori(2 + half, TILES_1 // 2) as i:
                    for s in range(2):
                        tile_split(g0 + 2 * i + s, (g0 + s) % 2)
                tile_split(g0 + TILES_1 - 1, (g0 + TILES_1 - 1) % 2)
            for k in range(4 * N_BLK - BPH, 4 * N_BLK):
                ln(k)

        @block.scalar
        def _(act):
            def mix_split_hi(c):
                act.wait_ge(mix_in[c % 2], 16 * (c // 2 + 1))
                nc.scalar.copy(mixh[:, c * RAWW:(c + 1) * RAWW], ln_r[c % 2][:].rearrange("p a b -> p (a b)")).then_inc(mix_hi, 1)

            def norm_sq(n, x):
                if not isinstance(n, int) or n:
                    act.wait_ge(n_sum, n)
                nc.scalar.activation(n_sqb[:], x[:], ACT.Square).then_inc(n_sq, 1)

            def rms_hi(i, b):
                act.wait_ge(n_x, rank[(i, b)] + 1)
                w = 0 if i == R1 else 1
                if i == R1 and b >= 1:
                    act.wait_ge(z_mm, b * CT)
                if i == R2 and b >= 1:
                    act.wait_ge(m1_mm, b * MT)
                nc.scalar.copy(hh[w][:], n_sqb[:]).then_inc(r_hh, 1)

            def rms_sq(i, b):
                if i == R1:
                    act.wait_ge(ax_in, 16 * (b + 1))
                else:
                    act.wait_ge(x1_done, b + 1)
                n = rank[(i, b)]
                if n:
                    act.wait_ge(r_hl, r_rank[(i, b)])
                norm_sq(n, a_x if i == R1 else a_x1)

            def ln_sq(k):
                act.wait_ge(l_xc, k + 1)
                norm_sq(ln_rank(k), r_of(k))

            def ln_hi(k, b):
                act.wait_ge(n_x, ln_rank(k) + 1)
                nc.scalar.copy(xh[:, :, cols(b)], r_of(k)[:]).then_inc(l_xh, 1)

            def xp_out(b, ct):
                act.wait_ge(xp_mm, b * CT + ct + 1)
                nc.scalar.copy(xp[ct % 2][:, :, TAPS - 1:], ps[:, 4 + ct % 2].rearrange("p (a t) -> p a t", a=2)).then_inc(xp_ev, 1)

            def z_out(b, ct):
                act.wait_ge(z_mm, b * CT + ct + 1)
                nc.scalar.activation(sz[ct % 2][:], ps[:, 6], ACT.Silu).then_inc(z_ev, 1)

            def xc_act(b, ct):
                act.wait_ge(conv_tap, (b * CT + ct + 1) * TAPS)
                nc.scalar.activation(sxc[:], cacc[ct % 2][:].rearrange("p a t -> p (a t)"), ACT.Silu).then_inc(xc_silu, 1)

            def y_high(b, ct):
                act.wait_ge(y_prod, b * CT + ct + 1)
                if b >= 1:
                    act.wait_ge(mix_out, b)
                nc.scalar.copy(yh[:, ct], yt[:]).then_inc(y_hi, 1)

            def relu(b, j):
                act.wait_ge(m1_mm, b * MT + j + 1)
                if b or j >= NR:
                    act.wait_ge(m2_mm, b * MT + j - NR + 1)
                nc.scalar.activation(rh[:, j % NR], ps[:, 4 + j % 3], ACT.Relu).then_inc(m1_hi, 1)

            def routing_out(u, i):
                ne = E0 if u < N_HALF else E1
                act.wait_ge(g_mm, u * BPH + i + 1)
                nc.scalar.copy(lgt[0:ne, i], ps[0:ne, STAT]).then_inc(g_lt, 1)

            def routing_act(u):
                act.wait_ge(g_dif, u + 1)
                nc.scalar.activation(ex[:], ex[:], ACT.Exp).then_inc(g_exp, 1)
                if u < N_HALF:
                    nc.scalar.activation(sc[:], lg[:], ACT.Exp, scale=-1.0).then_inc(g_exp, 1)

            mix_split_hi(0)
            rms_sq(R1, 0)
            mix_split_hi(1)
            act.wait_ge(const_in, 5 * 16)
            nc.scalar.copy(gwh[:], gwr[:]).then_inc(const_ready, 1)
            nc.scalar.copy(ident_r[:], ident[:]).then_inc(const_ready, 1)
            nc.scalar.copy(ident_b[:], ident[:]).then_inc(const_ready, 1)
            rms_hi(R1, 0)
            for b in range(-1, N_BLK):
                if b >= 1:
                    ln_sq(b - 1)
                if b >= 0:
                    rms_sq(R2, b)
                nxt = b + 1 < N_BLK
                if b < 0:
                    mix_split_hi(2)
                    rms_sq(R1, 1)
                if nxt:
                    xp_out(b + 1, 0)
                    z_out(b + 1, 0)
                if b < 0:
                    mix_split_hi(3)
                if b >= 1:
                    ln_hi(b - 1, b - 1)
                if b == N_BLK - 1:
                    for i in range(BPH):
                        routing_out(0, i)
                if nxt:
                    xp_out(b + 1, 1)
                    xc_act(b + 1, 0)
                    z_out(b + 1, 1)
                    y_high(b + 1, 0)
                if b >= 0:
                    rms_hi(R2, b)
                if b < 0:
                    mix_split_hi(4)
                if nxt:
                    xp_out(b + 1, 2)
                    xc_act(b + 1, 1)
                    z_out(b + 1, 2)
                    y_high(b + 1, 1)
                    xp_out(b + 1, 3)
                    xc_act(b + 1, 2)
                    z_out(b + 1, 3)
                    y_high(b + 1, 2)
                if b < 0:
                    rms_hi(R1, 1)
                    xc_act(0, 3)
                    y_high(0, 3)
                    mix_split_hi(5)
                    mix_split_hi(6)
                else:
                    for j in range(MT):
                        relu(b, j)
                        if j == 0 and nxt:
                            xc_act(b + 1, 3)
                            y_high(b + 1, 3)
                        if b + 2 < N_BLK:
                            if j == 1:
                                rms_sq(R1, b + 2)
                            if j == 5:
                                rms_hi(R1, b + 2)
                        if b == N_BLK - 1 and j == 1:
                            routing_act(0)

            def step_silu(n, q):
                act.wait_ge(e_g, n + 1)
                nc.scalar.activation(sg[q][:], ps[:, 4], ACT.Silu).then_inc(e_sg, 1)

            def step_hi(n, q):
                act.wait_ge(e_t2, n + 1)
                nc.scalar.copy(ah[q][:], t2[q][:]).then_inc(e_ah, 1)

            def tile_act(g, between=None, i0=0):
                for q in range(BPH):
                    step_silu(BPH * g + q, q)
                    if between:
                        between(i0 + q)
                    step_hi(BPH * g + q, q)

            def sums_out(k0, done):
                act.wait_ge(e_dn, done)
                for q in range(BPH):
                    nc.scalar.copy(r_of(k0 + q)[:], ps[:, 2 * q:2 * q + 2]).then_inc(l_r, 1)

            def experts(phase_d, half):
                g0 = first_tile(phase_d, half)
                due = due_norms(phase_d, half)
                k0 = (3 if phase_d else 1) * N_BLK + half * BPH

                def between(i):
                    j, at = divmod(i - 2, 4)
                    if i == 0 and half:
                        sums_out(k0 - BPH, BPH * g0)
                    if 0 <= j < len(due) and at == 1:
                        ln_sq(due[j])
                    if i in hi_at:
                        ln_hi(hi_at[i], hi_at[i] % N_BLK)

                hi_at = {2 + 4 * j + 5: k for j, k in enumerate(due) if k < 3 * N_BLK}
                for s in range(2 * len(due) + 2):
                    tile_act(g0 + s, between, 2 * s)
                last = (TILES_1 if phase_d else TILES_L) // 2 - ROUTE_PAIRS
                with act.Fori(len(due) + 1, last) as i:
                    for s in range(2):
                        tile_act(g0 + 2 * i + s)
                def route(i):
                    if i < BPH:
                        routing_out(2 * phase_d + 1, i)
                    if i == 5:
                        routing_act(2 * phase_d + 1)
                for s in range(2 * ROUTE_PAIRS):
                    tile_act(g0 + 2 * last + s, route if half == 0 else None, 2 * s)
                if phase_d:
                    tile_act(g0 + TILES_1 - 1)
                else:
                    with act.Fori(TILES_L // 2, TILES_0 // 2) as i:
                        for s in range(2):
                            tile_act(g0 + 2 * i + s)
                if half:
                    if phase_d:
                        act.wait_ge(store, 16 * BPH)
                    sums_out(k0, BPH * (g0 + (TILES_1 if phase_d else TILES_0)))

            for half in range(N_HALF):
                experts(False, half)
            def head_q(b, h):
                act.wait_ge(q_mm, b * HEADS + h + 1)
                nc.scalar.activation(qh[h % 2][:], ps[:, q_bank(b, h)], ACT.Identity, bias=attb[:, h:h + 1]).then_inc(q_hi, 1)

            def head_exp(b, h):
                act.wait_ge(s_neg, b * HEADS + h + 1)
                for t in range(TT):
                    nc.scalar.activation(pr[h % 2][:, t], ps[:, 2 + t // 2, (t % 2) * SEQ:(t % 2 + 1) * SEQ], ACT.Exp,
                                         bias=smx[h % 2][:, t:t + 1], scale=SCALE,
                                         accum_out=ssum[h % 2][:, t:t + 1]).then_inc(s_exp, 1)

            def head_t(b, h):
                act.wait_ge(t_mm, b * HEADS + h + 1)
                nc.scalar.copy(pth[:], ps[:, 4:6].rearrange("p a (k q) -> p a k q", k=2)).then_inc(t_hi, 1)

            def head_o(b, h):
                act.wait_ge(o_mm, b * HEADS + h + 1)
                nc.scalar.activation(oh[:], ps[:, 7], ACT.Identity, bias=attb[:, HEADS + KV + h // GRP:HEADS + KV + h // GRP + 1]).then_inc(o_hi, 1)

            def kv_k(b, k):
                act.wait_ge(k_mm, b * KV + k + 1)
                nc.scalar.activation(kh[k % 2][:], ps[:, 6], ACT.Identity, bias=attb[:, HEADS + k:HEADS + k + 1]).then_inc(k_hi, 1)

            def value(b, g, h):
                act.wait_ge(v_mm, b * VP + g + 1)
                nc.scalar.copy(v_part(vh, g), ps[:, v_bank(b, g)].rearrange("p (t d) -> p t d", t=2)).then_inc(v_hi, 1)

            def att_sums(b):
                act.wait_ge(y_mm, b * HEADS + HEADS)
                for m in range(DC):
                    ins = nc.scalar.activation(ln_r[0][:, m], ps[:, m], ACT.Identity, bias=attb[:, HEADS + 2 * KV + m:HEADS + 2 * KV + m + 1])
                ins.then_inc(l_r, 1)

            def attention(b, first=False, last=False):
                mean, _, factor = att_norms(b)

                def side(h):
                    if h in mean:
                        ln_sq(mean[h])
                    if h in factor:
                        ln_hi(factor[h], att_norm_block(b, h))
                    if last and h == 4:
                        routing_act(2)

                def taken(h):
                    if last and h < BPH:
                        routing_out(2, h)

                att_schedule(b, first, last, k=kv_k, v=value, q=head_q, exp=head_exp, sums=att_sums, before=taken, t=head_t, o=head_o, end=side)

            attention(0, first=True)
            with act.Fori(1, N_BLK - 1) as b:
                attention(b)
            attention(N_BLK - 1, last=True)

            for half in range(N_HALF):
                experts(True, half)
            for k in range(4 * N_BLK - BPH, 4 * N_BLK):
                ln_sq(k)

        @block.vector
        def _(dve):
            nc.vector.memset(mean_w[:], 1.0 / D).then_inc(const_ready, 1)
            nc.vector.memset(half_c[:], -0.5).then_inc(const_ready, 1)
            nc.vector.memset(one_c[:], 1.0).then_inc(const_ready, 1)
            for e in range(NE):
                ins = nc.vector.memset(iota_f[:, e:e + 1], float(e))
            ins.then_inc(const_ready, 1)
            for i in range(2):
                nc.vector.memset(xp[i][:, :, 0:TAPS - 1], 0.0).then_inc(pad_zero, 1)

            def mix_split_lo(c):
                dve.wait_ge(mix_hi, c + 1)
                o = c * RAWW
                nc.vector.tensor_tensor(mixl[:, o:o + RAWW], ln_r[c % 2][:].rearrange("p a b -> p (a b)"),
                                        f32(mixh[:, o:o + RAWW]), ALU.subtract).then_inc(mix_lo, 1)

            def norm_floor(n, layer):
                dve.wait_ge(n_stat, n + 1)
                if layer:
                    nc.vector.tensor_scalar(n_inb[:], ps[:, STAT, 0:TT], EPS, None, ALU.add).then_inc(n_in, 1)
                else:
                    nc.vector.tensor_scalar(n_inb[:], ps[:, STAT, 0:TT], TINY, None, ALU.max).then_inc(n_in, 1)

            def stat_bc():
                return ps[:, STAT:STAT + 1].broadcast_to([P, DC, BLK])

            def rms_mul(i, b):
                dve.wait_ge(n_bc, rank[(i, b)] + 1)
                x = a_x if i == R1 else a_x1
                nc.vector.tensor_tensor(n_sqb[:], x[:], stat_bc(), ALU.mult).then_inc(n_x, 1)

            def rms_lo(i, b):
                dve.wait_ge(r_hh, r_rank[(i, b)] + 1)
                w = 0 if i == R1 else 1
                nc.vector.tensor_tensor(hl[w][:], n_sqb[:], f32(hh[w][:]), ALU.subtract).then_inc(r_hl, 1)

            def ln_center(k):
                dve.wait_ge(l_mean, k + 1)
                nc.vector.tensor_tensor(r_of(k)[:], r_of(k)[:], stat_bc(), ALU.subtract).then_inc(l_xc, 1)

            def ln_mul(k):
                dve.wait_ge(n_bc, ln_rank(k) + 1)
                nc.vector.tensor_tensor(r_of(k)[:], r_of(k)[:], stat_bc(), ALU.mult).then_inc(n_x, 1)

            def ln_lo(k, b):
                dve.wait_ge(l_xh, k + 1)
                nc.vector.tensor_tensor(xl[:, :, cols(b)], r_of(k)[:], f32(xh[:, :, cols(b)]), ALU.subtract).then_inc(l_xl, 1)

            def conv(b, ct):
                src, dst = xp[ct % 2], cacc[ct % 2]
                dve.wait_ge(xp_ev, b * CT + ct + 1)
                n = (b * CT + ct) * TAPS
                nc.vector.tensor_scalar(dst[:], src[:, :, TAPS - 1:], convw[:, ct, TAPS - 1:TAPS], convw[:, ct, TAPS:],
                                        ALU.mult, ALU.add).then_inc(conv_tap, 1)
                for k in range(1, TAPS):
                    w = TAPS - 1 - k
                    dve.wait_ge(conv_tap, n + k)
                    nc.vector.scalar_tensor_tensor(out=dst[:], in0=src[:, :, w:w + SEQ], scalar=convw[:, ct, w:w + 1],
                                                   in1=dst[:], op0=ALU.mult, op1=ALU.add).then_inc(conv_tap, 1)

            def prod(b, ct):
                dve.wait_ge(xc_silu, b * CT + ct + 1)
                if b or ct:
                    dve.wait_ge(y_lo, b * CT + ct)
                nc.vector.tensor_tensor(yt[:], sxc[:], sz[ct % 2][:], ALU.mult).then_inc(y_prod, 1)

            def relu_lo(b, j):
                dve.wait_ge(m1_hi, b * MT + j + 1)
                nc.vector.scalar_tensor_tensor(out=rl[:, j % NR], in0=ps[:, 4 + j % 3], scalar=0.0, in1=f32(rh[:, j % NR]),
                                               op0=ALU.max, op1=ALU.subtract).then_inc(m1_lo, 1)

            def advance(table, n=1000):
                for _ in range(n):
                    if next(table, None) is None:
                        return

            chain = [0]

            def bc(v):
                return v[:, :, None].broadcast_to([P, HT, NE])

            def routing_dve(u):
                def link(ins):
                    chain[0] += 1
                    ins.then_inc(g_dve, 1)

                def linked():
                    dve.wait_ge(g_dve, chain[0])

                layer, half = divmod(u, N_HALF)
                ne = E0 if layer == 0 else E1
                dve.wait_ge(g_col, u + 1)
                nc.vector.tensor_copy(lg[:, :, 0:ne], ps[:, STAT, 0:HT * ne].rearrange("p (t e) -> p t e", t=HT)).then_inc(g_lg, 1)
                if layer == 1:
                    link(nc.vector.memset(lg[:, :, ne:], -1e30))
                    link(nc.vector.memset(cw[:], 0.0))
                yield 1
                dve.wait_ge(g_lg, u + 1)
                link(nc.vector.reduce_max(lmx[:], lg[:, :, 0:ne], AX_X))
                yield 1
                linked()
                nc.vector.tensor_tensor(ex[:], lg[:], bc(lmx[:]), ALU.subtract).then_inc(g_dif, 1)
                yield 1
                if layer == 0:
                    dve.wait_ge(g_exp, 2 * (u + 1))
                    link(nc.vector.tensor_scalar(sc[:], sc[:], 1.0, None, ALU.add))
                    yield 1
                    linked()
                    link(nc.vector.reciprocal(sc[:], sc[:]))
                    yield 1
                    linked()
                else:
                    dve.wait_ge(g_exp, N_HALF + u + 1)
                    link(nc.vector.reduce_sum(den[:], ex[:, :, 0:ne], AX_X))
                    yield 1
                    linked()
                    link(nc.vector.reciprocal(den[:], den[:]))
                    yield 1
                    linked()
                    link(nc.vector.tensor_tensor(sc[:], ex[:], bc(den[:]), ALU.mult))
                    yield 1
                    linked()
                for t in range(HT):
                    ins = nc.vector.max(top[:, t], sc[:, t, 0:ne])
                    if t == HT - 1:
                        link(ins)
                    if t % 2:
                        yield 1
                linked()
                for t in range(HT):
                    ins = nc.vector.max_index(tix[:, t], top[:, t], sc[:, t, 0:ne])
                    if t == HT - 1:
                        link(ins)
                    if t % 2:
                        yield 1
                linked()
                link(nc.vector.tensor_copy(tif[:], tix[:]))
                yield 1
                linked()
                for k in range(TOP_K):
                    dst = msk if k == 0 else eqk
                    link(nc.vector.tensor_tensor(dst[:], iota_f[:, None, :].broadcast_to([P, HT, NE]),
                                                 tif[:, :, k:k + 1].broadcast_to([P, HT, NE]), ALU.is_equal))
                    yield 1
                    linked()
                    if k:
                        link(nc.vector.tensor_tensor(msk[:], msk[:], eqk[:], ALU.add))
                        yield 1
                        linked()
                if layer == 0:
                    link(nc.vector.tensor_tensor(cw[:], ex[:], msk[:], ALU.mult))
                    yield 1
                    linked()
                    link(nc.vector.reduce_sum(den[:], cw[:], AX_X))
                    yield 1
                    linked()
                    link(nc.vector.reciprocal(den[:], den[:]))
                    yield 1
                    linked()
                    link(nc.vector.tensor_tensor(cw[:], cw[:], bc(den[:]), ALU.mult))
                    yield 1
                    linked()
                    link(nc.vector.tensor_scalar(cws[:], cw[:], SMALL, None, ALU.mult))
                else:
                    link(nc.vector.tensor_tensor(cw[:, :, 0:ne], sc[:, :, 0:ne], msk[:, :, 0:ne], ALU.mult))
                    link(nc.vector.memset(cw[:, :, ne:ne + 1], 1.0))
                yield 1
                linked()
                for i, c in enumerate((cw, cws) if layer == 0 else (cw,)):
                    for part in range(3):
                        if part < 2:
                            link(nc.vector.tensor_copy(cpart[i][:, :, part], c[:]))
                            yield 1
                            linked()
                            link(nc.vector.tensor_tensor(c[:], c[:], cpart[i][:, :, part], ALU.subtract))
                            yield 1
                            linked()
                        else:
                            nc.vector.tensor_copy(cpart[i][:, :, part], c[:]).then_inc(g_part, 1)
                            yield 1

            def routing_table(u, i):
                dve.wait_ge(g_tr, tr_count(u, i) + 1)
                nc.vector.tensor_copy(cwt[i][:, u % N_HALF], ps[0:3 * NE, STAT].bitcast(BF16)).then_inc(g_cwt, 1)

            mix_split_lo(0)
            norm_floor(rank[(R1, 0)], False)
            rms_mul(R1, 0)
            mix_split_lo(1)
            dve.wait_ge(const_ready, 7)
            nc.vector.tensor_tensor(gwl[:], gwr[:], f32(gwh[:]), ALU.subtract).then_inc(gwl_ready, 1)
            rms_lo(R1, 0)
            mix_split_lo(2)
            dve.wait_ge(pad_zero, 2)
            for b in range(-1, N_BLK):
                nxt = b + 1 < N_BLK
                if b >= 1:
                    dve.wait_ge(m2_mm, b * MT)
                    dve.wait_ge(x01_done, b)
                    nc.vector.tensor_tensor(r_of(b - 1)[:], ps[:, 2:4], a_xr[:], ALU.add).then_inc(l_r, 1)
                    ln_center(b - 1)
                if b >= 0:
                    dve.wait_ge(mix_out, b + 1)
                    dve.wait_ge(axr_in, 16 * (b + 1))
                    nc.vector.tensor_tensor(a_x1[:], ps[:, 0:2], a_xr[:], ALU.add).then_inc(x1_done, 1)
                if b >= 1:
                    norm_floor(ln_rank(b - 1), True)
                if nxt:
                    conv(b + 1, 0)
                if b >= 1:
                    ln_mul(b - 1)
                if b == N_BLK - 1:
                    table = routing_dve(0)
                    advance(table, 1)
                if b >= 0:
                    norm_floor(rank[(R2, b)], False)
                if b < 0:
                    norm_floor(rank[(R1, 1)], False)
                    mix_split_lo(3)
                if nxt:
                    conv(b + 1, 1)
                if b >= 0:
                    rms_mul(R2, b)
                else:
                    rms_mul(R1, 1)
                if nxt:
                    prod(b + 1, 0)
                if b >= 1:
                    ln_lo(b - 1, b - 1)
                if b >= 0:
                    rms_lo(R2, b)
                if b < 0:
                    mix_split_lo(4)
                if nxt:
                    conv(b + 1, 2)
                    prod(b + 1, 1)
                    conv(b + 1, 3)
                    prod(b + 1, 2)
                if b < 0:
                    rms_lo(R1, 1)
                    prod(0, 3)
                    mix_split_lo(5)
                    mix_split_lo(6)
                else:
                    for j in range(MT):
                        relu_lo(b, j)
                        if j == 0 and nxt:
                            prod(b + 1, 3)
                        if b + 2 < N_BLK:
                            if j == 3:
                                norm_floor(rank[(R1, b + 2)], False)
                            if j == 5:
                                rms_mul(R1, b + 2)
                            if j == 6:
                                rms_lo(R1, b + 2)
                        if b == N_BLK - 1:
                            advance(table, 2 if j < 2 else 7)
            dve.wait_ge(m2_mm, N_BLK * MT)
            dve.wait_ge(x01_done, N_BLK)
            nc.vector.tensor_tensor(r_of(N_BLK - 1)[:], ps[:, 2:4], a_xr[:], ALU.add).then_inc(l_r, 1)
            advance(table)
            for i in range(2):
                routing_table(0, i)

            def tile_dve(g, between=None, i0=0):
                for q in range(BPH):
                    n = BPH * g + q
                    dve.wait_ge(e_u, n + 1)
                    dve.wait_ge(e_sg, n + 1)
                    nc.vector.tensor_tensor(t1[:], ps[:, 5], sg[q][:], ALU.mult).then_inc(e_t1, 1)
                    dve.wait_ge(e_t1, n + 1)
                    dve.wait_ge(e_c, n + 1)
                    nc.vector.tensor_tensor(t2[q][:], ps[:, 6], t1[:], ALU.mult).then_inc(e_t2, 1)
                    dve.wait_ge(e_ah, n + 1)
                    nc.vector.tensor_tensor(al[q][:], t2[q][:], f32(ah[q][:]), ALU.subtract).then_inc(e_al, 1)
                    if between:
                        between(i0 + q)

            def experts(phase_d, half):
                g0 = first_tile(phase_d, half)
                due = due_norms(phase_d, half)

                def between(i):
                    j, at = divmod(i - 2, 4)
                    if 0 <= j < len(due):
                        k = due[j]
                        if at == 0:
                            ln_center(k)
                        if at == 2:
                            norm_floor(ln_rank(k), True)
                        if at == 3:
                            ln_mul(k)
                    if i in lo_at:
                        ln_lo(lo_at[i], lo_at[i] % N_BLK)

                lo_at = {2 + 4 * j + 5: k for j, k in enumerate(due) if k < 3 * N_BLK}
                for s in range(2 * len(due) + 2):
                    tile_dve(g0 + s, between, 2 * s)
                last = (TILES_1 if phase_d else TILES_L) // 2 - ROUTE_PAIRS
                with dve.Fori(len(due) + 1, last) as i:
                    for s in range(2):
                        tile_dve(g0 + 2 * i + s)
                table = routing_dve(2 * phase_d + 1) if half == 0 else None
                n_tab = 1 if phase_d else 2

                def route(i):
                    if i == 2:
                        advance(table, 1)
                    if i == 3:
                        advance(table, 2)
                    if 5 <= i < 13:
                        advance(table, 4)
                    if i == 13:
                        advance(table)
                    if i >= 16 - n_tab:
                        routing_table(2 * phase_d + 1, i - (16 - n_tab))

                for s in range(2 * ROUTE_PAIRS):
                    tile_dve(g0 + 2 * last + s, route if half == 0 else None, 2 * s)
                if phase_d:
                    tile_dve(g0 + TILES_1 - 1)
                else:
                    with dve.Fori(TILES_L // 2, TILES_0 // 2) as i:
                        for s in range(2):
                            tile_dve(g0 + 2 * i + s)

            for half in range(N_HALF):
                experts(False, half)
            def head_q(b, h):
                dve.wait_ge(q_hi, b * HEADS + h + 1)
                nc.vector.scalar_tensor_tensor(out=ql[h % 2][:], in0=ps[:, q_bank(b, h)], scalar=attb[:, h:h + 1], in1=f32(qh[h % 2][:]),
                                               op0=ALU.add, op1=ALU.subtract).then_inc(q_lo, 1)

            def head_max(b, h):
                dve.wait_ge(s_mm, b * HEADS + h + 1)
                nc.vector.reduce_max(smx[h % 2][:], ps[:, 2:4].rearrange("p a (k q) -> p (a k) q", k=2), AX_X).then_inc(s_max, 1)
                dve.wait_ge(s_max, b * HEADS + h + 1)
                nc.vector.tensor_scalar(smx[h % 2][:], smx[h % 2][:], -SCALE, None, ALU.mult).then_inc(s_neg, 1)

            def head_norm(b, h):
                dve.wait_ge(s_exp, (b * HEADS + h + 1) * TT)
                nc.vector.reciprocal(ssum[h % 2][:], ssum[h % 2][:]).then_inc(s_inv, 1)
                dve.wait_ge(s_inv, b * HEADS + h + 1)
                nc.vector.tensor_tensor(pr[h % 2][:], pr[h % 2][:], ssum[h % 2][:, :, None].broadcast_to([P, TT, SEQ]), ALU.mult).then_inc(s_prob, 1)

            def head_t(b, h):
                dve.wait_ge(t_hi, b * HEADS + h + 1)
                nc.vector.tensor_tensor(ptl[:].rearrange("p a k q -> p a (k q)"), ps[:, 4:6], f32(pth[:]).rearrange("p a k q -> p a (k q)"), ALU.subtract).then_inc(t_lo, 1)

            def head_o(b, h):
                dve.wait_ge(o_hi, b * HEADS + h + 1)
                nc.vector.scalar_tensor_tensor(out=ol[:], in0=ps[:, 7], scalar=attb[:, HEADS + KV + h // GRP:HEADS + KV + h // GRP + 1], in1=f32(oh[:]),
                                               op0=ALU.add, op1=ALU.subtract).then_inc(o_lo, 1)

            def kv_k(b, k):
                dve.wait_ge(k_hi, b * KV + k + 1)
                nc.vector.scalar_tensor_tensor(out=kl[k % 2][:], in0=ps[:, 6], scalar=attb[:, HEADS + k:HEADS + k + 1], in1=f32(kh[k % 2][:]),
                                               op0=ALU.add, op1=ALU.subtract).then_inc(k_lo, 1)

            def value(b, g, h):
                dve.wait_ge(v_hi, b * VP + g + 1)
                nc.vector.tensor_tensor(v_part(vl, g), ps[:, v_bank(b, g)].rearrange("p (t d) -> p t d", t=2),
                                        f32(v_part(vh, g)), ALU.subtract).then_inc(v_lo, 1)

            def attention(b, first=False, last=False):
                mean, var, factor = att_norms(b)
                table = routing_dve(2) if last else None

                def side(h):
                    if h - 1 in factor:
                        ln_lo(factor[h - 1], att_norm_block(b, h - 1))
                    if h in mean:
                        ln_center(mean[h])
                    if h in var:
                        norm_floor(ln_rank(var[h]), True)
                    if h in factor:
                        ln_mul(factor[h])
                    if last and h == BPH:
                        advance(table, 1)
                    if last and h == 14:
                        routing_table(2, 0)

                def end(h):
                    if last and h >= 3:
                        advance(table, (2 if h == 3 else 0 if h == 4 else 4) if h < 13 else 1000)

                att_schedule(b, first, last, k=kv_k, v=value, q=head_q, mx=head_max, norm=head_norm, before=side, t=head_t, o=head_o, end=end)
            attention(0, first=True)
            with dve.Fori(1, N_BLK - 1) as b:
                attention(b)
            attention(N_BLK - 1, last=True)

            for half in range(N_HALF):
                experts(True, half)
            for k in range(4 * N_BLK - BPH, 4 * N_BLK):
                ln_center(k)
                norm_floor(ln_rank(k), True)
                ln_mul(k)

        @block.tensor
        def _(pe):
            def norm_stat(n):
                pe.wait_ge(n_sum, n + 1)
                if not isinstance(n, int) or n:
                    pe.wait_ge(n_x, n)
                for t in range(TT):
                    mm = nc.tensor.matmul(ps[:, STAT, t:t + 1], n_sumb[:, t * P:(t + 1) * P], mean_w[:, 0:1], start=True, stop=True,
                                          skip_group_check=True)
                mm.then_inc(n_stat, 1)

            def norm_bc(n):
                pe.wait_ge(n_pow, n + 1)
                for t in range(TT):
                    mm = nc.tensor.matmul(ps[:, STAT, t * P:(t + 1) * P], n_powb[:, t:t + 1].broadcast_to([P, P]), ident[:],
                                          start=True, stop=True, skip_group_check=True)
                mm.then_inc(n_bc, 1)

            def ln_mean(k):
                pe.wait_ge(l_sum, k + 1)
                pe.wait_ge(n_x, ln_rank(k))
                nc.tensor.matmul(ps[:, STAT], mean_w[:], n_sumb[:], start=True, stop=True).then_inc(l_mean, 1)

            def project(b, ct, kind):
                bank = (4 + ct % 2) if kind == 0 else 6
                n = b * CT + ct
                if kind == 0 and n >= 2:
                    pe.wait_ge(xp_ev, n - 1)
                if kind == 1 and n >= 1:
                    pe.wait_ge(z_ev, n)
                if ct == 0 and b >= 2:
                    pe.wait_ge(m1_lo, (b - 1) * MT)
                product(ps[:, bank], [(w_in_t(c, kind * CT + ct), (hh[0][:, c], hl[0][:, c])) for c in range(DC)])\
                    .then_inc(z_mm if kind else xp_mm, 1)

            def mix_product(b, ct):
                pe.wait_ge(y_lo, b * CT + ct + 1)
                if b and ct == 0:
                    pe.wait_ge(x1_done, b)
                for m in range(DC):
                    mm = product(ps[:, m], [(w_out_t(ct, m), (yh[:, ct], yl[:, ct]))], first=ct == 0, last=ct == CT - 1)
                if ct == CT - 1:
                    mm.then_inc(mix_out, 1)

            def mlp_up(b, j):
                n = b * MT + j
                if n >= 3:
                    pe.wait_ge(m1_lo, n - 2 if j >= 3 else b * MT)
                if j < 2 and b + 1 < N_BLK:
                    pe.wait_ge(xp_ev, (b + 2) * CT - 1 + j)
                if j == 2 and b + 1 < N_BLK:
                    pe.wait_ge(z_ev, (b + 2) * CT)
                product(ps[:, 4 + j % 3], [(w_m1_t(c, j), (hh[1][:, c], hl[1][:, c])) for c in range(DC)]).then_inc(m1_mm, 1)

            def mlp_down(b, j):
                pe.wait_ge(m1_lo, b * MT + j + 1)
                if b and j == 0:
                    pe.wait_ge(l_r, b)
                for m in range(DC):
                    mm = product(ps[:, 2 + m], [(w_m2_t(j, m), (rh[:, j % NR], rl[:, j % NR]))], first=j == 0, last=j == MT - 1)
                mm.then_inc(m2_mm, 1)

            def routing_logits(u, i):
                layer, half = divmod(u, N_HALF)
                ne = E0 if layer == 0 else E1
                pe.wait_ge(gwl_ready, 1)
                pe.wait_ge(l_xl, 2 * layer * N_BLK + half * BPH + i + 1)
                if i:
                    pe.wait_ge(g_lt, u * BPH + i)
                else:
                    pe.wait_ge(n_x, ROUTE_AFTER[u])
                b = half * BPH + i
                product(ps[0:ne, STAT], [((gwh[:, layer, c, 0:ne], gwl[:, layer, c, 0:ne]),
                                          (xh[:, c, b * BLK:(b + 1) * BLK], xl[:, c, b * BLK:(b + 1) * BLK])) for c in range(DC)])\
                    .then_inc(g_mm, 1)

            def routing_columns(u):
                ne = E0 if u < N_HALF else E1
                pe.wait_ge(g_lt, (u + 1) * BPH)
                for t in range(HT):
                    mm = nc.tensor.transpose(ps[:, STAT, t * ne:(t + 1) * ne], lgt[0:ne, t // TT, (t % TT) * P:(t % TT + 1) * P], ident[0:ne, 0:ne])
                mm.then_inc(g_col, 1)

            pe.wait_ge(const_ready, 7)
            norm_stat(rank[(R1, 0)])
            norm_bc(rank[(R1, 0)])
            pe.wait_ge(mix_lo, 2)
            pe.wait_ge(r_hl, 1)
            for b in range(-1, N_BLK):
                if b >= 0:
                    if b == 0:
                        pe.wait_ge(mix_lo, 3)
                    mix_product(b, 0)
                    mix_product(b, 1)
                    if b >= 1:
                        ln_mean(b - 1)
                    mix_product(b, 2)
                    mix_product(b, 3)
                    if b + 1 < N_BLK:
                        pe.wait_ge(r_hl, r_rank[(R1, b + 1)] + 1)
                nxt = b + 1 < N_BLK
                if nxt:
                    project(b + 1, 0, 0)
                if b >= 1:
                    norm_stat(ln_rank(b - 1))
                if nxt:
                    project(b + 1, 0, 1)
                if b >= 1:
                    norm_bc(ln_rank(b - 1))
                if nxt:
                    project(b + 1, 1, 0)
                if b == N_BLK - 1:
                    for i in range(BPH):
                        routing_logits(0, i)
                    routing_columns(0)
                n = rank[(R2, b)] if b >= 0 else rank[(R1, 1)]
                if b < N_BLK - 1:
                    norm_stat(n)
                if nxt:
                    project(b + 1, 1, 1)
                if b == N_BLK - 1:
                    pe.wait_ge(g_lg, 1)
                    norm_stat(n)
                norm_bc(n)
                if nxt:
                    for ct in range(2, CT):
                        project(b + 1, ct, 0)
                        project(b + 1, ct, 1)
                if b >= 0:
                    if b == 0:
                        pe.wait_ge(mix_lo, N_RAW_A)
                    pe.wait_ge(r_hl, r_rank[(R2, b)] + 1)
                    for j in range(MT + 2):
                        if j < MT:
                            mlp_up(b, j)
                        if j >= 2:
                            mlp_down(b, j - 2)
                        if b + 2 < N_BLK and j == 3:
                            norm_stat(rank[(R1, b + 2)])
                        if b + 2 < N_BLK and j == 5:
                            norm_bc(rank[(R1, b + 2)])

            def routing_transposes(u, i):
                pe.wait_ge(g_part, tr_count(u, i) + 1)
                if i:
                    pe.wait_ge(g_cwt, tr_count(u, i))
                for t in range(HT):
                    mm = nc.tensor.transpose(ps[0:3 * NE, STAT].bitcast(BF16)[:, t * P:(t + 1) * P],
                                             cpart[i][:, t].rearrange("p a e -> p (a e)"), ident_b[:])
                mm.then_inc(g_tr, 1)

            def seed(half, q):
                tok = slice((half * BPH + q) * BLK, (half * BPH + q + 1) * BLK)
                for m in range(DC):
                    nc.tensor.matmul(ps[:, 2 * q + m], ident_r[:], xh[:, m, tok], start=True, stop=False, skip_group_check=True)
                    nc.tensor.matmul(ps[:, 2 * q + m], ident_r[:], xl[:, m, tok], start=False, stop=False, skip_group_check=True)

            def down(n, s, q):
                pe.wait_ge(e_al, n + 1)
                for m in range(DC):
                    o = 2 * D + m * P
                    mm = product(ps[:, 2 * q + m], [(pair(wh[s], wl[s], o), (ah[q][:], al[q][:]))], first=False, last=True)
                mm.then_inc(e_dn, 1)

            def tile_pe(g, s, half, table, first=False, before=None, after=None, i0=0):
                pe.wait_ge(w_lo, g + 1)
                for q in range(BPH):
                    n = BPH * g + q
                    tok = slice((half * BPH + q) * BLK, (half * BPH + q + 1) * BLK)
                    if before:
                        before(i0 + q)
                    for bank, o, freed, done in ((4, 0, e_sg, e_g), (5, D, e_t1, e_u)):
                        if not isinstance(n, int) or n >= 1:
                            pe.wait_ge(freed, n)
                        product(ps[:, bank], [(pair(wh[s], wl[s], o + c * P), (xh[:, c, tok], xl[:, c, tok])) for c in range(DC)])\
                            .then_inc(done, 1)
                    if after:
                        after(i0 + q)
                    if not (first and q == 0):
                        down(n - 1, s if q else 1 - s, 1 - q)
                    if not isinstance(n, int) or n >= 1:
                        pe.wait_ge(e_t2, n)
                    if q == 0:
                        pe.wait_ge(sel_in[s], 8 * (g - s) + 16)
                    nc.tensor.matmul(ps[:, 6], selt[s][:], cwt[table][:, half, q * BLK:(q + 1) * BLK], start=True, stop=True).then_inc(e_c, 1)

            def experts(phase_d, half):
                g0 = first_tile(phase_d, half)
                due = due_norms(phase_d, half)
                k0 = (3 if phase_d else 1) * N_BLK + half * BPH

                def before(i):
                    j, at = divmod(i - 2, 4)
                    if 1 <= j <= len(due) and at == 0:
                        norm_bc(ln_rank(due[j - 1]))

                def after(i):
                    j, at = divmod(i - 2, 4)
                    if 0 <= j < len(due) and at == 0:
                        ln_mean(due[j])
                    if 0 <= j < len(due) and at == 2:
                        norm_stat(ln_rank(due[j]))
                    if i == 1:
                        pe.wait_ge(l_r, k0)
                        for q in range(BPH):
                            seed(half, q)

                pe.wait_ge(g_cwt, {(0, 0): 2, (0, 1): 4, (1, 0): 5, (1, 1): 6}[(phase_d, half)])
                for s in range(2 * len(due) + 2):
                    tile_pe(g0 + s, (g0 + s) % 2, half, 0, first=s == 0 and half == 0, before=before, after=after, i0=2 * s)
                last = (TILES_1 if phase_d else TILES_L) // 2 - ROUTE_PAIRS
                with pe.Fori(len(due) + 1, last) as i:
                    for s in range(2):
                        tile_pe(g0 + 2 * i + s, (g0 + s) % 2, half, 0)

                u = 2 * phase_d + 1
                n_tab = 1 if phase_d else 2

                def route_before(i):
                    if i < BPH:
                        routing_logits(u, i)
                    if i == BPH:
                        routing_columns(u)

                def route_after(i):
                    if i >= 16 - n_tab:
                        routing_transposes(u, i - (16 - n_tab))

                for s in range(2 * ROUTE_PAIRS):
                    tile_pe(g0 + 2 * last + s, (g0 + s) % 2, half, 0, before=route_before if half == 0 else None,
                            after=route_after if half == 0 else None, i0=2 * s)
                if phase_d:
                    tile_pe(g0 + TILES_1 - 1, (g0 + TILES_1 - 1) % 2, half, 0)
                else:
                    with pe.Fori(TILES_L // 2, TILES_0 // 2) as i:
                        for s in range(2):
                            tile_pe(g0 + 2 * i + s, s, half, 1)
                if half:
                    g = g0 + (TILES_1 if phase_d else TILES_0)
                    down(BPH * g - 1, (g - 1) % 2, 1)

            for t in range(2):
                routing_transposes(0, t)
            for half in range(N_HALF):
                experts(0, half)

            def kv_k(b, k):
                if k or not isinstance(b, int) or b:
                    pe.wait_ge(q_lo, b * HEADS + k * GRP)
                product(ps[:, 6], [(w_k_t(c, k), (xh[:, c, cols(b)], xl[:, c, cols(b)])) for c in range(DC)]).then_inc(k_mm, 1)

            def value(b, g, bank_free):
                bank_free()
                if g == 0:
                    pe.wait_ge(xb_in, b * 32 + 32)
                for t in range(2):
                    tok = slice(((g % 2) * 2 + t) * P, ((g % 2) * 2 + t + 1) * P)
                    mm = product(ps[:, v_bank(b, g), t * 2 * DH:(t + 1) * 2 * DH],
                                 [((xbh[:, c, tok], xbl[:, c, tok]), w_v_t(c, g // 2)) for c in range(DC)])
                mm.then_inc(v_mm, 1)

            def head_q(b, h, bank_free):
                bank_free()
                product(ps[:, q_bank(b, h)], [(w_q_t(c, h), (xh[:, c, cols(b)], xl[:, c, cols(b)])) for c in range(DC)]).then_inc(q_mm, 1)

            def head_s(b, h):
                pe.wait_ge(q_lo, b * HEADS + h + 1)
                if h == 0 and isinstance(b, int) and b == 0:
                    pe.wait_ge(l_r, 2 * N_BLK)
                if h or not isinstance(b, int) or b:
                    pe.wait_ge(s_exp, (b * HEADS + h) * TT)
                k = (h // GRP) % 2
                for t in range(TT):
                    sq = slice((t // 2) * SEQ, (t // 2 + 1) * SEQ)
                    mm = product(ps[:, 2 + t // 2, (t % 2) * SEQ:(t % 2 + 1) * SEQ],
                                 [((qh[h % 2][:, t * P:(t + 1) * P], ql[h % 2][:, t * P:(t + 1) * P]), (kh[k][:, sq], kl[k][:, sq]))])
                mm.then_inc(s_mm, 1)

            def head_t(b, h):
                pe.wait_ge(s_prob, b * HEADS + h + 1)
                if h or not isinstance(b, int) or b:
                    pe.wait_ge(t_lo, b * HEADS + h)
                for a in range(2):
                    for kt in range(2):
                        for qt in range(2):
                            mm = nc.tensor.transpose(ps[:, 4 + a, kt * SEQ + qt * P:kt * SEQ + (qt + 1) * P],
                                                     pr[h % 2][:, 2 * a + qt, kt * P:(kt + 1) * P], ident[:])
                mm.then_inc(t_mm, 1)

            def head_o(b, h):
                pe.wait_ge(t_lo, b * HEADS + h + 1)
                if h or not isinstance(b, int) or b:
                    pe.wait_ge(o_lo, b * HEADS + h)
                if h % (2 * GRP) == 0:
                    pe.wait_ge(v_lo, b * VP + (2 if h == 0 else VP))
                kc = slice((h // GRP) * DH, (h // GRP + 1) * DH)
                for a in range(2):
                    mm = product(ps[:, 7, a * SEQ:(a + 1) * SEQ],
                                 [((vh[:, 2 * a + kt, kc], vl[:, 2 * a + kt, kc]), (pth[:, a, kt], ptl[:, a, kt])) for kt in range(2)])
                mm.then_inc(o_mm, 1)

            def head_y(b, h):
                if h == 0:
                    pe.wait_ge(l_r, b + 2 * N_BLK)
                    for m in range(DC):
                        nc.tensor.matmul(ps[:, m], ident_r[:], xh[:, m, cols(b)], start=True, stop=False, skip_group_check=True)
                        nc.tensor.matmul(ps[:, m], ident_r[:], xl[:, m, cols(b)], start=False, stop=False, skip_group_check=True)
                pe.wait_ge(o_lo, b * HEADS + h + 1)
                for m in range(DC):
                    mm = product(ps[:, m], [(w_o_t(h, m), (oh[:], ol[:]))], first=False, last=h == HEADS - 1)
                mm.then_inc(y_mm, 1)

            def attention(b, first=False, last=False):
                mean, var, factor = att_norms(b)

                def side(h):
                    if h in mean or h in var or h in factor or (last and (h < 3 or h == 14)):
                        pe.wait_ge(o_lo, b * HEADS + h)
                    if h in mean:
                        ln_mean(mean[h])
                    if h in var:
                        norm_stat(ln_rank(var[h]))
                    if h in factor:
                        norm_bc(ln_rank(factor[h]))
                    if last and h < BPH:
                        routing_logits(2, h)
                    if last and h == BPH:
                        routing_columns(2)
                    if last and h == 14:
                        routing_transposes(2, 0)

                def sums(b, h):
                    if h in mean:
                        pe.wait_ge(l_xc, mean[h] + 1)
                    if h in var:
                        pe.wait_ge(n_in, ln_rank(var[h]) + 1)
                    if h in factor:
                        pe.wait_ge(n_x, ln_rank(factor[h]) + 1)
                    if last and h < BPH:
                        pe.wait_ge(g_lt, 2 * BPH + h + 1)
                    if last and h == BPH:
                        pe.wait_ge(g_lg, 3)
                    if last and h == 14:
                        pe.wait_ge(g_cwt, 5)
                    head_o(b, h)

                def after(done, n):
                    return lambda: pe.wait_ge(done, n)

                def query(bq, h):
                    if first and bq is b and h < 3:
                        free = lambda: None
                    elif first and bq is b and h == 3:
                        free = after(v_lo, 1)
                    elif h % GRP == 0:
                        free = after(k_lo, bq * KV + h // GRP + 1)
                    elif h % GRP == 2 and not (last and h == 14):
                        free = after(v_lo, bq * VP + {2: 2, 6: 3, 10: 4, 14: 5}[h])
                    else:
                        free = after(q_lo, bq * HEADS + h)
                    head_q(bq, h, free)

                def values(bv, g, h):
                    if h >= 0:
                        free = after(q_lo, b * HEADS + h + 4)
                    else:
                        free = after(q_lo, 3) if g else after(k_lo, 1)
                    value(bv, g, free)

                att_schedule(b, first, last, k=kv_k, v=values, q=query,
                             s=head_s, t=head_t, after=side, o=sums, y=head_y)

            pe.wait_ge(att_lo, N_RAW_C)
            pe.wait_ge(l_xl, N_BLK + 1)
            attention(0, first=True)
            with pe.Fori(1, N_BLK - 1) as b:
                attention(b)
            attention(N_BLK - 1, last=True)

            for half in range(N_HALF):
                experts(1, half)
            for k in range(4 * N_BLK - BPH, 4 * N_BLK):
                ln_mean(k)
                norm_stat(ln_rank(k))
                norm_bc(ln_rank(k))


def tr_count(u, i):
    return 2 * u + i if u < N_HALF else 2 * N_HALF + (u - N_HALF)


def att_schedule(b, first, last, k=None, v=None, q=None, s=None, mx=None, exp=None, norm=None, sums=None,
                 before=None, t=None, after=None, o=None, y=None, end=None):
    def at(h):
        return (b, h) if h < HEADS else (b + 1, h - HEADS)

    def do(step, h):
        if step and (h < HEADS or not last):
            step(*at(h))

    def y_step(h):
        if y and h:
            y(b, h - 1)
        elif y and not first:
            y(b - 1, HEADS - 1)

    def k_step(h):
        if k and (h < HEADS or not last):
            bk, hk = at(h)
            k(bk, hk // GRP)

    if first:
        for h in range(-3, 0):
            if h == -3:
                k_step(0)
            do(q, h + 3)
            if h == -1:
                do(exp, 0)
                do(norm, 0)
            if h == -1 and v:
                v(b, 0, h)
            if h >= -2:
                do(s, h + 2)
                do(mx, h + 2)
            if h == -1 and v:
                v(b, 1, h)
    for h in range(HEADS):
        if before:
            before(h)
        if t:
            t(b, h)
        if after:
            after(h)
        new_k = (h + 3) % GRP == 0
        if new_k:
            k_step(h + 3)
        else:
            do(q, h + 3)
        y_step(h)
        do(exp, h + 1)
        do(norm, h + 1)
        if sums and h == 0 and not first:
            sums(b - 1)
        if o:
            o(b, h)
        if new_k:
            do(q, h + 3)
        do(s, h + 2)
        do(mx, h + 2)
        if v and h % GRP == 2:
            if h < 8:
                v(b, 2 + h // GRP, h)
            elif not last:
                v(b + 1, h // GRP - 2, h)
        if end:
            end(h)
    if last:
        if y:
            y(b, HEADS - 1)
        if sums:
            sums(b)


def _rows(w, k):
    n = w.shape[1]
    return w.reshape(k, P, n).transpose(1, 0, 2).reshape(P, k * n)


def _tiles(gate, up, down, n_tiles):
    hidden = gate.shape[0]
    out = np.zeros((n_tiles, P, 3, D), gate.dtype)
    for w, which in ((gate, 0), (up, 1), (down, 2)):
        full = np.zeros((n_tiles * P, D), w.dtype)
        full[:hidden] = w
        full = full.reshape(n_tiles, P, D)
        if which < 2:
            full = full.reshape(n_tiles, P, DC, P).transpose(0, 3, 2, 1).reshape(n_tiles, P, D)
        out[:, :, which] = full
    return out.reshape(n_tiles, P, 3 * D)


def _selectors():
    one = 0x3F80
    s = np.zeros((TILES_0 + TILES_1, 3, NE, P), np.uint16)
    for t in range(TILES_L):
        for r in range(P):
            s[t, :, (t * P + r) // I0, r] = one
    for t in range(TILES_S):
        s[TILES_L + t, :, 2 * t:2 * t + 2, :] = one
    for t in range(TILES_1):
        for r in range(P):
            row = t * P + r
            if row < H1:
                s[TILES_0 + t, :, min(row // I1, E1), r] = one
    return s.reshape(TILES_0 + TILES_1, 3 * NE, P)


def kernel(**inputs):
    import concourse.bacc as bacc
    from concourse.bass_utils import run_bass_kernel_spmd

    a = {k: np.ascontiguousarray(v) for k, v in inputs.items()}
    x = a["L0_attn_x"].reshape(N_TOK, D)
    arrays = {
        "x_t": x.T.reshape(DC, P, N_TOK).transpose(1, 0, 2),
        "w_mix": np.concatenate([
            _rows(a["L0_attn_W_in"].T, DC), _rows(a["L0_attn_W_out"].T, CT),
            _rows(a["L0_attn_W_mlp1"].T, DC), _rows(a["L0_attn_W_mlp2"].T, MT)], axis=1),
        "conv_wb": np.concatenate([
            a["L0_attn_conv_w"].reshape(CT, P, TAPS), a["L0_attn_conv_b"].reshape(CT, P, 1)], axis=2).transpose(1, 0, 2),
    }
    gates = []
    for w in (a["L0_ffn_gate_w"], a["L1_ffn_gate_weight"]):
        g = np.zeros((NE, D), w.dtype)
        g[:w.shape[0]] = w
        gates.append(_rows(g.T, DC).reshape(P, DC, NE))
    arrays["gw0"], arrays["gw1"] = gates

    def hidden_first(w):
        return w.transpose(0, 2, 1).reshape(-1, D)

    gu, dn = a["L1_ffn_gate_up_weights"], a["L1_ffn_down_weights"]
    sgu, sdn = a["L1_ffn_shared_gate_up"], a["L1_ffn_shared_down"]
    arrays["moe_w"] = np.concatenate([
        _tiles(hidden_first(a["L0_ffn_Wg"]), hidden_first(a["L0_ffn_Wu"]), a["L0_ffn_Wd"].reshape(-1, D), TILES_L),
        _tiles(hidden_first(a["L0_ffn_cWg"]), hidden_first(a["L0_ffn_cWu"]), a["L0_ffn_cWd"].reshape(-1, D), TILES_S),
        _tiles(np.concatenate([gu[:, :I1].reshape(-1, D), sgu[:IS1]]),
               np.concatenate([gu[:, I1:].reshape(-1, D), sgu[IS1:]]),
               np.concatenate([hidden_first(dn), sdn.T]), TILES_1)])
    arrays["sel"] = _selectors()
    arrays["w_att"] = np.concatenate([
        _rows(a["L1_attn_Wq"], DC), _rows(a["L1_attn_Wk"], DC), _rows(a["L1_attn_Wv"], DC), _rows(a["L1_attn_Wo"], HEADS)], axis=1)
    arrays["att_b"] = np.concatenate([
        a["L1_attn_bq"].reshape(HEADS, P), a["L1_attn_bk"].reshape(KV, P), a["L1_attn_bv"].reshape(KV, P),
        a["L1_attn_bo"].reshape(DC, P)]).T
    arrays["ident"] = np.eye(P, dtype=np.float32)
    arrays = {k: np.ascontiguousarray(v) for k, v in arrays.items()}

    nc = bacc.Bacc("TRN2", target_bir_lowering=False, num_devices=1)
    ins = [nc.dram_tensor(f"in_{k}", v.shape, mybir.dt.from_np(v.dtype), kind="ExternalInput").ap() for k, v in arrays.items()]
    out = nc.dram_tensor("out_t", (P, DC, N_TOK), F32, kind="ExternalOutput").ap()
    by = dict(zip(arrays, ins))
    build_program(nc, by["x_t"], by["w_mix"], by["conv_wb"], by["gw0"], by["gw1"], by["moe_w"], by["sel"],
                  by["w_att"], by["att_b"], by["ident"], out)
    r = run_bass_kernel_spmd(nc, [{f"in_{k}": v for k, v in arrays.items()}], core_ids=[0])
    got = r.results[0]["out_t"]
    return np.ascontiguousarray(got.transpose(1, 0, 2).reshape(D, N_TOK).T).reshape(8, SEQ, D)
```

```python
from contextlib import ExitStack

import numpy as np

import concourse.bass as bass
from concourse import mybir

ALU = mybir.AluOpType
ACT = mybir.ActivationFunctionType
AX_X = mybir.AxisListType.X
F32 = mybir.dt.float32
F32R = mybir.dt.float32r
BF16 = mybir.dt.bfloat16
U32 = mybir.dt.uint32
U16 = mybir.dt.uint16

P = 128
D = 256
DC = D // P
N_TOK = 8 * 256
SEQ = 256
BLK = 512
N_BLK = N_TOK // BLK
BPH = 2
N_HALF = N_BLK // BPH
TT = BLK // P
D_IN = 512
CT = D_IN // P
TAPS = 4
D_MLP = 4 * D
MT = D_MLP // P
E0, I0, C0, IC0 = 32, 96, 16, 128
E1, I1, IS1 = 16, 176, 352
TILES_L = E0 * I0 // P
TILES_S = C0 * IC0 // P
H1 = E1 * I1 + IS1
TILES_1 = -(-H1 // P)
TILES_0 = TILES_L + TILES_S
NE = 32
SMALL = 0.05
HEADS, DH, KV = 16, 128, 4
GRP = HEADS // KV
VP = 4
SCALE = float(1.0 / np.sqrt(np.float32(DH)))
EPS = 1e-5
TOP_K = 4
TINY = 1e-24 / D


def build_program(nc, xT, w_mix, conv_wb, gw0, gw1, moe_w, sel, w_att, att_b, ident_d, outT):
    with ExitStack() as keep:
        stack = [keep]

        def sb(name, shape, dt=F32):
            return stack[-1].enter_context(nc.sbuf_tensor(name, shape, dt))

        def sem(name):
            return keep.enter_context(nc.semaphore(name))

        xh = sb("xh", [P, DC, N_TOK], F32R)
        xl = sb("xl", [P, DC, N_TOK], F32R)
        ident = sb("ident", [P, P])
        ident_r = sb("ident_r", [P, P], F32R)
        ident_b = sb("ident_b", [P, P], BF16)
        mean_w = sb("mean_w", [P, P])
        half_c = sb("half_c", [P, 1])
        one_c = sb("one_c", [P, 1])
        iota_f = sb("iota_f", [P, NE])
        ln_r = [sb(f"ln_r{i}", [P, DC, BLK]) for i in range(2)]
        n_sqb = sb("n_sqb", [P, DC, BLK])
        n_sumb = sb("n_sumb", [P, BLK])
        n_inb = sb("n_inb", [P, TT])
        n_powb = sb("n_powb", [P, TT])
        convw = sb("convw", [P, CT, TAPS + 1])
        attb = sb("attb", [P, HEADS + KV + KV + DC])
        gwr = sb("gwr", [P, 2, DC, NE])
        gwh = sb("gwh", [P, 2, DC, NE], F32R)
        gwl = sb("gwl", [P, 2, DC, NE], F32R)
        HT = BPH * TT
        lgt = sb("lgt", [NE, BPH, BLK])
        lg = sb("lg", [P, HT, NE])
        lmx = sb("lmx", [P, HT])
        ex = sb("ex", [P, HT, NE])
        sc = sb("sc", [P, HT, NE])
        top = sb("top", [P, HT, 8])
        tix = sb("tix", [P, HT, 8], U32)
        tif = sb("tif", [P, HT, 8])
        msk = sb("msk", [P, HT, NE])
        eqk = sb("eqk", [P, HT, NE])
        den = sb("den", [P, HT])
        cw = sb("cw", [P, HT, NE])
        cpart = [sb("cpart0", [P, HT, 3, NE], BF16)]
        cwt = [sb("cwt0", [3 * NE, N_HALF, BPH * BLK], BF16)]

        W_MIX = DC * 2 * D_IN + CT * D + DC * D_MLP + MT * D
        W_ATT = DC * HEADS * DH + 2 * DC * KV * DH + HEADS * D
        NR = 3
        WT = 3 * D
        with ExitStack() as phase:
            stack.append(phase)
            mixh = sb("mixh", [P, W_MIX], F32R)
            mixl = sb("mixl", [P, W_MIX], F32R)
            hh = [sb(f"hh{i}", [P, DC, BLK], F32R) for i in range(2)]
            hl = [sb(f"hl{i}", [P, DC, BLK], F32R) for i in range(2)]
            yh = sb("yh", [P, CT, BLK], F32R)
            stack.pop()
        atth = sb("atth", [P, W_ATT], F32R)
        attl = sb("attl", [P, W_ATT], F32R)
        with ExitStack() as tables:
            stack.append(tables)
            cws = sb("cws", [P, HT, NE])
            cpart.append(sb("cpart1", [P, HT, 3, NE], BF16))
            cwt.append(sb("cwt1", [3 * NE, N_HALF, BPH * BLK], BF16))
            with ExitStack() as phase:
                stack.append(phase)
                xp = [sb(f"xp{i}", [P, 2, SEQ + TAPS - 1]) for i in range(2)]
                cacc = [sb(f"cacc{i}", [P, 2, SEQ]) for i in range(2)]
                sxc = sb("sxc", [P, BLK])
                sz = [sb(f"sz{i}", [P, BLK]) for i in range(2)]
                yt = sb("yt", [P, BLK])
                yl = sb("yl", [P, CT, BLK], F32R)
                rh = sb("rh", [P, NR, BLK], F32R)
                rl = sb("rl", [P, NR, BLK], F32R)
                a_x = sb("a_x", [P, DC, BLK])
                a_xr = [sb(f"a_xr{i}", [P, DC, BLK]) for i in range(2)]
                a_x1 = sb("a_x1", [P, DC, BLK])
                stack.pop()
            with ExitStack() as phase:
                stack.append(phase)
                wraw = [sb(f"wraw{i}", [P, WT]) for i in range(2)]
                whl = [(sb(f"wh{i}", [P, WT], F32R), sb(f"wl{i}", [P, WT], F32R)) for i in range(2)]
                wh, wl = [h for h, _ in whl], [l for _, l in whl]
                selt = [sb(f"selt{i}", [3 * NE, P], BF16) for i in range(2)]
                sg = [sb(f"sg{i}", [P, BLK]) for i in range(2)]
                t1 = sb("t1", [P, BLK])
                t2 = [sb(f"t2_{i}", [P, BLK]) for i in range(2)]
                ah = [sb(f"ah{i}", [P, BLK], F32R) for i in range(2)]
                al = [sb(f"al{i}", [P, BLK], F32R) for i in range(2)]
                raw = sb("raw", [P, 1024])
                stack.pop()
            stack.pop()
        with ExitStack() as phase:
            stack.append(phase)
            xbh = sb("xbh", [P, DC, BLK], F32R)
            xbl = sb("xbl", [P, DC, BLK], F32R)
            qh = [sb(f"qh{i}", [P, BLK], F32R) for i in range(2)]
            ql = [sb(f"ql{i}", [P, BLK], F32R) for i in range(2)]
            kh = [sb(f"kh{i}", [P, BLK], F32R) for i in range(2)]
            kl = [sb(f"kl{i}", [P, BLK], F32R) for i in range(2)]
            vh = sb("vh", [P, TT, KV * DH], F32R)
            vl = sb("vl", [P, TT, KV * DH], F32R)
            pr = [sb(f"pr{i}", [P, TT, SEQ]) for i in range(2)]
            pth = sb("pth", [P, 2, 2, SEQ], F32R)
            ptl = sb("ptl", [P, 2, 2, SEQ], F32R)
            oh = sb("oh", [P, BLK], F32R)
            ol = sb("ol", [P, BLK], F32R)
            smx = [sb(f"smx{i}", [P, TT]) for i in range(2)]
            ssum = [sb(f"ssum{i}", [P, TT]) for i in range(2)]
            stack.pop()

        ps = keep.enter_context(nc.psum_tensor("ps", [P, 8, BLK], F32))
        STAT = 7

        def f32(ap):
            return ap.bitcast(F32)

        def cols(b):
            return bass.ds(b * BLK, BLK)

        const_in = sem("const_in")
        const_set = sem("const_set")
        const_ready = sem("const_ready")
        gwl_ready = sem("gwl_ready")
        mix_in = [sem("mix_in0"), sem("mix_in1")]
        mix_hi = sem("mix_hi")
        mix_lo = sem("mix_lo")
        mix_lo_g = sem("mix_lo_g")
        ax_in = sem("ax_in")
        axr_in = [sem("axr_in0"), sem("axr_in1")]
        n_sq = sem("n_sq")
        n_sum = sem("n_sum")
        n_stat = sem("n_stat")
        n_in = sem("n_in")
        n_pow = sem("n_pow")
        n_bc = sem("n_bc")
        n_x = sem("n_x")
        r_hh = sem("r_hh")
        r_hl = sem("r_hl")
        l_r = sem("l_r")
        l_sum = sem("l_sum")
        l_mean = sem("l_mean")
        l_xc = sem("l_xc")
        l_xh = sem("l_xh")
        l_xl = sem("l_xl")
        pad_zero = sem("pad_zero")
        xp_mm = sem("xp_mm")
        z_mm = sem("z_mm")
        xp_ev = sem("xp_ev")
        z_ev = sem("z_ev")
        conv_0 = sem("conv_0")
        conv_tap = sem("conv_tap")
        xc_silu = sem("xc_silu")
        y_prod = sem("y_prod")
        y_hi = sem("y_hi")
        y_lo = sem("y_lo")
        mix_out = sem("mix_out")
        x1_done = sem("x1_done")
        x01_done = sem("x01_done")
        m1_mm = sem("m1_mm")
        m1_hi = sem("m1_hi")
        m1_lo = sem("m1_lo")
        m2_mm = sem("m2_mm")
        g_mm = sem("g_mm")
        g_dve = sem("g_dve")
        g_lt = sem("g_lt")
        g_col = sem("g_col")
        g_lg = sem("g_lg")
        g_dif = sem("g_dif")
        g_exp = sem("g_exp")
        g_part = sem("g_part")
        g_tr = sem("g_tr")
        g_cwt = sem("g_cwt")
        w_in = [sem("w_in0"), sem("w_in1")]
        sel_in = [sem("sel_in0"), sem("sel_in1")]
        att_in = sem("att_in")
        att_hi = sem("att_hi")
        att_lo = sem("att_lo")
        w_hi = sem("w_hi")
        w_lo = sem("w_lo")
        e_g = sem("e_g")
        e_u = sem("e_u")
        e_c = sem("e_c")
        e_dn = sem("e_dn")
        e_sg = sem("e_sg")
        e_t1 = sem("e_t1")
        e_t2 = sem("e_t2")
        e_ah = sem("e_ah")
        e_al = sem("e_al")
        xb_in = sem("xb_in")
        q_mm = sem("q_mm")
        k_mm = sem("k_mm")
        v_mm = sem("v_mm")
        q_hi = sem("q_hi")
        q_lo = sem("q_lo")
        k_hi = sem("k_hi")
        k_lo = sem("k_lo")
        v_hi = sem("v_hi")
        v_lo = sem("v_lo")
        s_mm = sem("s_mm")
        s_max = sem("s_max")
        s_neg = sem("s_neg")
        s_exp = sem("s_exp")
        s_inv = sem("s_inv")
        s_prob = sem("s_prob")
        t_mm = sem("t_mm")
        t_hi = sem("t_hi")
        t_lo = sem("t_lo")
        o_mm = sem("o_mm")
        o_hi = sem("o_hi")
        o_lo = sem("o_lo")
        y_mm = sem("y_mm")
        store = sem("store")

        R1, R2, LN = "first", "second", "layer"
        LAST = N_BLK - 1
        order = [(R1, 0), (R1, 1), (R2, 0)]
        for b in range(LAST - 1):
            order += [(LN, b - 1)] * (b >= 1) + [(R1, b + 2), (R2, b + 1)]
        order += [(LN, LAST - 2), (R2, LAST)] + [(LN, k) for k in range(LAST - 1, 4 * N_BLK)]
        rank = {norm: n for n, norm in enumerate(order)}
        r_rank = {norm: n for n, norm in enumerate(x for x in order if x[0] != LN)}
        LN_OFF = rank[(LN, N_BLK)] - N_BLK

        def ln_rank(k):
            return rank[(LN, k)] if isinstance(k, int) else k + LN_OFF

        def r_of(k):
            if not isinstance(k, int):
                return ln_r[0]
            return ln_r[{2 * N_BLK - 2: 1, 2 * N_BLK - 1: 0}.get(k, 0 if 2 * N_BLK <= k < 3 * N_BLK else k % 2)]

        ROUTE_AFTER = {0: rank[(LN, LAST - 2)] + 1, 1: ln_rank(N_BLK - 1) + 1, 2: ln_rank(3 * N_BLK - 3) + 1, 3: ln_rank(3 * N_BLK - 1) + 1}

        def xp_bank(b, ct):
            return 0 if 1 <= b < LAST and ct == 3 else 4 + ct % 2

        def z_bank(b, ct):
            return 1 if 1 <= b < LAST and ct == 3 else 6

        def res(b):
            return a_x if b == LAST else a_xr[b % 2]

        def h_of(b):
            return (hh[0], hl[0]) if b == LAST else (hh[1], hl[1])

        MIX_V = 5

        def mix_split_done(eng, n):
            eng.wait_ge(mix_lo, min(n, MIX_V))
            if n > MIX_V:
                eng.wait_ge(mix_lo_g, n - MIX_V)

        def stat_bank(n):
            return 4 if isinstance(n, int) and n == len(order) - 1 else STAT

        def sum_buf(n):
            return t1 if isinstance(n, int) and n == len(order) - 1 else n_sumb

        def rms_before(n):
            return sum(x[0] != LN for x in order[:n])

        def due_norms(phase_d, half):
            k0 = (3 if phase_d else 1) * N_BLK
            return [k0, k0 + 1] if half else [k0 - 1]

        def att_norms(b):
            if isinstance(b, int) and b == 0:
                k = 2 * N_BLK - 2
                return {3: k, 8: k + 1}, {4: k, 11: k + 1}, {7: k, 12: k + 1}
            k = b + 2 * N_BLK - 1
            return {3: k}, {4: k}, {7: k}

        def att_norm_block(b, h):
            if isinstance(b, int) and b == 0:
                return N_BLK - 2 if h < 10 else N_BLK - 1
            return b - 1

        RAWW = 1024
        N_RAW_A = W_MIX // RAWW
        N_RAW_C = W_ATT // RAWW
        ROUTE_PAIRS = 4
        PAIRS_N = 2
        o_in, o_out, o_m1 = 0, DC * 2 * D_IN, DC * 2 * D_IN + CT * D
        o_m2 = o_m1 + DC * D_MLP

        def pair(hi, lo, o, n=P):
            return hi[:, o:o + n], lo[:, o:o + n]

        def w_in_t(c, ot):
            return pair(mixh, mixl, o_in + c * 2 * D_IN + ot * P)

        def w_out_t(c, m):
            return pair(mixh, mixl, o_out + c * D + m * P)

        def w_m1_t(c, j):
            return pair(mixh, mixl, o_m1 + c * D_MLP + j * P)

        def w_m2_t(c, m):
            return pair(mixh, mixl, o_m2 + c * D + m * P)

        o_q, o_k = 0, DC * HEADS * DH
        o_v = o_k + DC * KV * DH
        o_o = o_v + DC * KV * DH

        def w_q_t(c, h):
            return pair(atth, attl, o_q + c * HEADS * DH + h * DH)

        def w_k_t(c, k):
            return pair(atth, attl, o_k + c * KV * DH + k * DH)

        def w_v_t(c, g):
            return pair(atth, attl, o_v + c * KV * DH + g * 2 * DH, 2 * DH)

        def v_part(v, i):
            return v[:, (i % 2) * 2:(i % 2) * 2 + 2, (i // 2) * 2 * DH:(i // 2 + 1) * 2 * DH]

        def k_bank(b, k):
            return 6

        def q_bank(b, h):
            return {0: 4, 1: 5, 2: 7}.get(h, 6) if isinstance(b, int) and b == 0 else 6

        def v_bank(b, i):
            return 7 if isinstance(b, int) and b == 0 and i == 1 else 6

        def w_o_t(h, m):
            return pair(atth, attl, o_o + h * D + m * P)

        def product(out, terms, first=True, last=True):
            n = 0
            for (ah_, al_), (bh_, bl_) in terms:
                for a, b in ((ah_, bh_), (ah_, bl_), (al_, bh_)):
                    mm = nc.tensor.matmul(out, a, b, start=first and n == 0, stop=last and n == 3 * len(terms) - 1,
                                          skip_group_check=True)
                    n += 1
            return mm

        def first_tile(phase_d, half):
            return (N_HALF * TILES_0 + half * TILES_1) if phase_d else half * TILES_0

        block = keep.enter_context(nc.Block())

        @block.sync
        def _(sp):
            def mix_load(c):
                if c >= 2:
                    mix_split_done(sp, c - 1)
                sp.dma_start(ln_r[c % 2][:].rearrange("p a b -> p (a b)"), w_mix[:, c * RAWW:(c + 1) * RAWW]).then_inc(mix_in[c % 2], 16)

            def x_load(dst, b, done):
                sp.dma_start(dst[:], xT[:, :, b * BLK:(b + 1) * BLK]).then_inc(done, 16)

            x_load(a_x, 0, ax_in)
            mix_load(0)
            mix_load(1)
            sp.dma_start(ident[:], ident_d).then_inc(const_in, 16)
            sp.dma_start(convw[:], conv_wb).then_inc(const_in, 16)
            sp.dma_start(attb[:], att_b).then_inc(const_in, 16)
            sp.dma_start(gwr[:, 0], gw0).then_inc(const_in, 16)
            sp.dma_start(gwr[:, 1], gw1).then_inc(const_in, 16)
            mix_load(2)
            x_load(a_xr[0], 0, axr_in[0])
            x_load(a_xr[1], 1, axr_in[1])
            sp.wait_ge(n_x, rank[(R1, 0)] + 1)
            x_load(a_x, 1, ax_in)
            for c in range(3, N_RAW_A):
                mix_load(c)
            for b in range(1, N_BLK):
                if b + 1 < N_BLK:
                    sp.wait_ge(n_x, rank[(R1, b)] + 1)
                    x_load(a_x, b + 1, ax_in)
                if 2 <= b < LAST:
                    sp.wait_ge(l_r, b - 1)
                    x_load(a_xr[b % 2], b, axr_in[b % 2])

            def att_load(c):
                if not isinstance(c, int):
                    sp.wait_ge(att_lo, c)
                sp.dma_start(raw[:], w_att[:, bass.ds(c * RAWW, RAWW)]).then_inc(att_in, 16)

            def tile_loads(g, t, s, first=False):
                if not first:
                    sp.wait_ge(w_lo, g - 1)
                sp.dma_start(wraw[s][:], moe_w[t]).then_inc(w_in[s], 16)
                if not first:
                    sp.wait_ge(e_c, BPH * (g - 1))
                sp.dma_start(selt[s][:].bitcast(U16), sel[t]).then_inc(sel_in[s], 16)

            sp.wait_ge(mix_out, N_BLK)
            for half in range(N_HALF):
                for s in range(2):
                    tile_loads(half * TILES_0 + s, s, s, first=half == 0)
                if half:
                    with sp.Fori(1, TILES_0 // 2) as i:
                        for s in range(2):
                            tile_loads(half * TILES_0 + 2 * i + s, sp.snap(2 * i + s), s)
                    continue
                for s in range(2):
                    tile_loads(2 + s, 2 + s, s)
                tile_loads(2 * PAIRS_N, 2 * PAIRS_N, 0)
                sp.wait_ge(e_g, 1)
                att_load(0)
                tile_loads(2 * PAIRS_N + 1, 2 * PAIRS_N + 1, 1)
                with sp.Fori(PAIRS_N + 1, PAIRS_N + N_RAW_C) as i:
                    tile_loads(2 * i, sp.snap(2 * i), 0)
                    att_load(i - PAIRS_N)
                    tile_loads(2 * i + 1, sp.snap(2 * i + 1), 1)
                with sp.Fori(PAIRS_N + N_RAW_C, TILES_0 // 2) as i:
                    for s in range(2):
                        tile_loads(2 * i + s, sp.snap(2 * i + s), s)
            sp.wait_ge(e_dn, BPH * N_HALF * TILES_0)
            for b in range(N_BLK):
                if b:
                    sp.wait_ge(v_mm, b * VP)
                sp.wait_ge(l_xl, N_BLK + b + 1)
                sp.dma_start(f32(xbh[:]), f32(xh[:, :, b * BLK:(b + 1) * BLK])).then_inc(xb_in, 16)
                sp.dma_start(f32(xbl[:]), f32(xl[:, :, b * BLK:(b + 1) * BLK])).then_inc(xb_in, 16)
            sp.wait_ge(v_mm, N_BLK * VP)
            sp.wait_ge(s_mm, N_BLK * HEADS)
            for half in range(N_HALF):
                g0 = first_tile(True, half)
                for s in range(2):
                    tile_loads(g0 + s, TILES_0 + s, (g0 + s) % 2, first=half == 0)
                with sp.Fori(1, TILES_1 // 2) as i:
                    for s in range(2):
                        tile_loads(g0 + 2 * i + s, sp.snap(TILES_0 + 2 * i + s), (g0 + s) % 2)
                tile_loads(g0 + TILES_1 - 1, TILES_0 + TILES_1 - 1, (g0 + TILES_1 - 1) % 2)
            for b in range(N_BLK):
                sp.wait_ge(n_x, ln_rank(3 * N_BLK + b) + 1)
                sp.dma_start(outT[:, :, b * BLK:(b + 1) * BLK], r_of(3 * N_BLK + b)[:]).then_inc(store, 16)
            sp.wait_ge(store, 16 * N_BLK)

        @block.gpsimd
        def _(pool):
            def norm_sum(n):
                pool.wait_ge(n_sq, n + 1)
                nc.gpsimd.tensor_tensor(sum_buf(n)[:], n_sqb[:, 0], n_sqb[:, 1], ALU.add).then_inc(n_sum, 1)

            def norm_pow(n):
                pool.wait_ge(n_in, n + 1)
                if stat_bank(n) != STAT:
                    pool.wait_ge(n_bc, n)
                nc.gpsimd.tensor_tensor(n_powb[:], n_inb[:], half_c[:].broadcast_to([P, TT]), ALU.pow).then_inc(n_pow, 1)

            def norm(n):
                norm_sum(n)
                norm_pow(n)

            def ln_sum(k):
                pool.wait_ge(l_r, k + 1)
                if sum_buf(ln_rank(k)) is n_sumb:
                    pool.wait_ge(n_stat, ln_rank(k))
                nc.gpsimd.tensor_tensor(sum_buf(ln_rank(k))[:], r_of(k)[:, 0], r_of(k)[:, 1], ALU.add).then_inc(l_sum, 1)

            def ln(k):
                ln_sum(k)
                norm(ln_rank(k))

            def y_low(b, ct):
                pool.wait_ge(y_hi, b * CT + ct + 1)
                if b >= 1:
                    pool.wait_ge(mix_out, b)
                nc.gpsimd.tensor_tensor(yl[:, ct], yt[:], f32(yh[:, ct]), ALU.subtract).then_inc(y_lo, 1)

            def mix_split_lo(c):
                pool.wait_ge(mix_hi, c + 1)
                o = c * RAWW
                nc.gpsimd.tensor_tensor(mixl[:, o:o + RAWW], ln_r[c % 2][:].rearrange("p a b -> p (a b)"),
                                        f32(mixh[:, o:o + RAWW]), ALU.subtract).then_inc(mix_lo_g, 1)

            def ln_lo(k):
                pool.wait_ge(l_xh, k + 1)
                nc.gpsimd.tensor_tensor(xl[:, :, k * BLK:(k + 1) * BLK], r_of(k)[:], f32(xh[:, :, k * BLK:(k + 1) * BLK]),
                                        ALU.subtract).then_inc(l_xl, 1)

            norm_sum(rank[(R1, 0)])
            pool.wait_ge(const_set, 4)
            norm_pow(rank[(R1, 0)])
            norm(rank[(R1, 1)])
            for ct in range(CT):
                y_low(0, ct)
            def x_sum(b):
                pool.wait_ge(x1_done, b + 1)
                nc.gpsimd.tensor_tensor(res(b)[:], res(b)[:], a_x1[:], ALU.add).then_inc(x01_done, 1)

            for b in range(LAST):
                norm(rank[(R2, b)])
                if b >= 1:
                    ln_sum(b - 1)
                if b == 0:
                    mix_split_lo(5)
                elif b == LAST - 1:
                    norm_sum(ln_rank(b - 1))
                y_low(b + 1, 0)
                if b == 0:
                    mix_split_lo(6)
                x_sum(b)
                y_low(b + 1, 1)
                if b < LAST - 1:
                    y_low(b + 1, 2)
                    if b >= 1:
                        norm(ln_rank(b - 1))
                    norm(rank[(R1, b + 2)])
                    y_low(b + 1, 3)
                    if b >= 1:
                        ln_lo(b - 1)
                else:
                    y_low(b + 1, 2)
                    norm_pow(ln_rank(b - 1))
                    y_low(b + 1, 3)
            norm(rank[(R2, LAST)])
            x_sum(LAST)
            ln(LAST - 1)

            def pool_round(out, x):
                return nc.gpsimd.tensor_tensor(out, x, one_c[:].broadcast_to(list(x.shape)), ALU.mult)

            def tile_split(g, s, first=False):
                pool.wait_ge(w_in[s], 8 * (g - s) + 16)
                if not first:
                    pool.wait_ge(e_dn, BPH * (g - 1))
                pool_round(wh[s][:], wraw[s][:]).then_inc(w_hi, 1)
                pool.wait_ge(w_hi, g + 1)
                nc.gpsimd.tensor_tensor(wl[s][:], wraw[s][:], f32(wh[s][:]), ALU.subtract).then_inc(w_lo, 1)

            def att_split(c):
                pool.wait_ge(att_in, 16 * c + 16)
                at = bass.ds(c * RAWW, RAWW)
                pool_round(atth[:, at], raw[:]).then_inc(att_hi, 1)
                pool.wait_ge(att_hi, c + 1)
                nc.gpsimd.tensor_tensor(attl[:, at], raw[:], f32(atth[:, at]), ALU.subtract).then_inc(att_lo, 1)

            def first_pairs(phase_d, half):
                g0 = first_tile(phase_d, half)
                tile_split(g0, g0 % 2, first=g0 == 0)
                if phase_d and not half:
                    pool.wait_ge(y_mm, N_BLK * HEADS)
                tile_split(g0 + 1, (g0 + 1) % 2, first=g0 == 0)
                for i, k in enumerate(due_norms(phase_d, half)):
                    g = g0 + 2 * (i + 1)
                    ln_sum(k)
                    tile_split(g, g % 2)
                    norm_sum(ln_rank(k))
                    tile_split(g + 1, (g + 1) % 2)
                    norm_pow(ln_rank(k))

            for half in range(N_HALF):
                first_pairs(False, half)

                def pairs(first, end, chunks=False):
                    with pool.Fori(first, end) as i:
                        for s in range(2):
                            tile_split(half * TILES_0 + 2 * i + s, s)
                        if chunks:
                            att_split(i - PAIRS_N)
                if half == 0:
                    pairs(PAIRS_N, PAIRS_N + N_RAW_C, chunks=True)
                    pairs(PAIRS_N + N_RAW_C, TILES_0 // 2)
                else:
                    pairs(3, TILES_0 // 2)
            ln(2 * N_BLK - 2)
            with pool.Fori(0, N_BLK) as b:
                ln(2 * N_BLK - 1 + b)
            for half in range(N_HALF):
                g0 = first_tile(True, half)
                first_pairs(True, half)
                with pool.Fori(2 + half, TILES_1 // 2) as i:
                    for s in range(2):
                        tile_split(g0 + 2 * i + s, (g0 + s) % 2)
                tile_split(g0 + TILES_1 - 1, (g0 + TILES_1 - 1) % 2)
            last_two = range(4 * N_BLK - BPH, 4 * N_BLK)
            for k in last_two:
                ln_sum(k)
            for k in last_two:
                norm_sum(ln_rank(k))
            for k in last_two:
                norm_pow(ln_rank(k))

        @block.scalar
        def _(act):
            def mix_split_hi(c):
                act.wait_ge(mix_in[c % 2], 16 * (c // 2 + 1))
                nc.scalar.copy(mixh[:, c * RAWW:(c + 1) * RAWW], ln_r[c % 2][:].rearrange("p a b -> p (a b)")).then_inc(mix_hi, 1)

            def norm_sq(n, x):
                if not isinstance(n, int) or n:
                    act.wait_ge(n_sum, n)
                if isinstance(n, int) and 0 < n <= rank[(LN, LAST)] and order[n - 1][0] != LN:
                    act.wait_ge(r_hl, rms_before(n))
                nc.scalar.activation(n_sqb[:], x[:], ACT.Square).then_inc(n_sq, 1)

            def rms_hi(i, b):
                act.wait_ge(n_x, rank[(i, b)] + 1)
                if i == R1 and b >= 1:
                    act.wait_ge(z_mm, b * CT)
                if i == R2 and b == LAST:
                    act.wait_ge(z_mm, N_BLK * CT)
                elif i == R2 and b >= 1:
                    act.wait_ge(m1_mm, b * MT)
                nc.scalar.copy((hh[0] if i == R1 else h_of(b)[0])[:], n_sqb[:]).then_inc(r_hh, 1)

            def rms_sq(i, b):
                if i == R1:
                    act.wait_ge(ax_in, 16 * (b + 1))
                else:
                    act.wait_ge(x1_done, b + 1)
                norm_sq(rank[(i, b)], a_x if i == R1 else a_x1)

            def ln_sq(k):
                act.wait_ge(l_xc, k + 1)
                norm_sq(ln_rank(k), r_of(k))

            def ln_hi(k, b):
                act.wait_ge(n_x, ln_rank(k) + 1)
                nc.scalar.copy(xh[:, :, cols(b)], r_of(k)[:]).then_inc(l_xh, 1)

            def xp_out(b, ct):
                act.wait_ge(xp_mm, b * CT + ct + 1)
                bank = ps[:, xp_bank(b, ct)].rearrange("p (a t) -> p a t", a=2)
                nc.scalar.copy(xp[ct % 2][:, :, TAPS - 1:], bank).then_inc(xp_ev, 1)
                if b * CT + ct >= 2:
                    act.wait_ge(xc_silu, b * CT + ct - 1)
                nc.scalar.activation(cacc[ct % 2][:], bank, ACT.Identity, bias=convw[:, ct, TAPS:], scale=convw[:, ct, TAPS - 1:TAPS]).then_inc(conv_0, 1)

            def z_out(b, ct):
                act.wait_ge(z_mm, b * CT + ct + 1)
                nc.scalar.activation(sz[ct % 2][:], ps[:, z_bank(b, ct)], ACT.Silu).then_inc(z_ev, 1)

            def xc_act(b, ct):
                act.wait_ge(conv_tap, (b * CT + ct + 1) * (TAPS - 1))
                nc.scalar.activation(sxc[:], cacc[ct % 2][:].rearrange("p a t -> p (a t)"), ACT.Silu).then_inc(xc_silu, 1)

            def y_high(b, ct):
                act.wait_ge(y_prod, b * CT + ct + 1)
                if b >= 1:
                    act.wait_ge(mix_out, b)
                nc.scalar.copy(yh[:, ct], yt[:]).then_inc(y_hi, 1)

            def relu(b, j):
                act.wait_ge(m1_mm, b * MT + j + 1)
                if b or j >= NR:
                    act.wait_ge(m2_mm, b * MT + j - NR + 1)
                nc.scalar.activation(rh[:, j % NR], ps[:, 4 + j % 3], ACT.Relu).then_inc(m1_hi, 1)

            def routing_out(u, i):
                ne = E0 if u < N_HALF else E1
                act.wait_ge(g_mm, u * BPH + i + 1)
                nc.scalar.copy(lgt[0:ne, i], ps[0:ne, STAT]).then_inc(g_lt, 1)

            def routing_act(u):
                act.wait_ge(g_dif, u + 1)
                nc.scalar.activation(ex[:], ex[:], ACT.Exp).then_inc(g_exp, 1)
                if u < N_HALF:
                    nc.scalar.activation(sc[:], lg[:], ACT.Exp, scale=-1.0).then_inc(g_exp, 1)

            rms_sq(R1, 0)
            mix_split_hi(0)
            mix_split_hi(1)
            act.wait_ge(const_in, 5 * 16)
            nc.scalar.copy(gwh[:], gwr[:]).then_inc(const_ready, 1)
            nc.scalar.copy(ident_r[:], ident[:]).then_inc(const_ready, 1)
            nc.scalar.copy(ident_b[:], ident[:]).then_inc(const_ready, 1)
            rms_hi(R1, 0)
            for b in range(-1, LAST):
                if b >= 0:
                    rms_sq(R2, b)
                else:
                    mix_split_hi(2)
                    rms_sq(R1, 1)
                xp_out(b + 1, 0)
                z_out(b + 1, 0)
                if b == 0:
                    mix_split_hi(5)
                xp_out(b + 1, 1)
                if b >= 0:
                    rms_hi(R2, b)
                    if b == 0:
                        mix_split_hi(6)
                    z_out(b + 1, 1)
                    xc_act(b + 1, 0)
                else:
                    xc_act(b + 1, 0)
                    z_out(b + 1, 1)
                xp_out(b + 1, 2)
                if b == LAST - 1:
                    ln_sq(b - 1)
                y_high(b + 1, 0)
                xc_act(b + 1, 1)
                z_out(b + 1, 2)
                y_high(b + 1, 1)
                if b in (-1, LAST - 1):
                    xp_out(b + 1, 3)
                    xc_act(b + 1, 2)
                    z_out(b + 1, 3)
                    y_high(b + 1, 2)
                if b < 0:
                    rms_hi(R1, 1)
                    xc_act(0, 3)
                    y_high(0, 3)
                    mix_split_hi(3)
                    mix_split_hi(4)
                elif b < LAST - 1:
                    for j in range(MT):
                        relu(b, j)
                        if j == 0:
                            xc_act(b + 1, 2)
                        if j == 1:
                            y_high(b + 1, 2)
                            if b >= 1:
                                ln_sq(b - 1)
                        if j == 2:
                            xp_out(b + 1, 3)
                            z_out(b + 1, 3)
                        if j == 4:
                            xc_act(b + 1, 3)
                            rms_sq(R1, b + 2)
                        if j == 5 and b >= 1:
                            ln_hi(b - 1, b - 1)
                        if j == 6:
                            y_high(b + 1, 3)
                        if j == 7:
                            rms_hi(R1, b + 2)
                else:
                    for j in range(MT):
                        relu(b, j)
                        if j == 0:
                            xc_act(b + 1, 3)
                            y_high(b + 1, 3)
                        if j == 2:
                            ln_hi(LAST - 2, LAST - 2)
                        if j in (2, 3):
                            routing_out(0, j - 2)
                        if j == 4:
                            rms_sq(R2, LAST)
                        if j == 6:
                            routing_act(0)
                        if j == 7:
                            rms_hi(R2, LAST)
            for j in range(MT):
                relu(LAST, j)
                if j == 2:
                    ln_sq(LAST - 1)
                if j == 6:
                    ln_hi(LAST - 1, LAST - 1)

            def step_silu(n, q):
                act.wait_ge(e_g, n + 1)
                nc.scalar.activation(sg[q][:], ps[:, 4], ACT.Silu).then_inc(e_sg, 1)

            def step_hi(n, q):
                act.wait_ge(e_t2, n + 1)
                nc.scalar.copy(ah[q][:], t2[q][:]).then_inc(e_ah, 1)

            def tile_act(g, between=None, i0=0):
                for q in range(BPH):
                    step_silu(BPH * g + q, q)
                    if between:
                        between(i0 + q)
                    step_hi(BPH * g + q, q)

            def sums_out(k0, done):
                for q in range(BPH):
                    act.wait_ge(e_dn, done - BPH + 1 + q)
                    nc.scalar.copy(r_of(k0 + q)[:], ps[:, 2 * q:2 * q + 2]).then_inc(l_r, 1)

            def experts(phase_d, half):
                g0 = first_tile(phase_d, half)
                due = due_norms(phase_d, half)
                k0 = (3 if phase_d else 1) * N_BLK + half * BPH

                def between(i):
                    j, at = divmod(i - 2, 4)
                    if i == 0 and half:
                        sums_out(k0 - BPH, BPH * g0)
                    if 0 <= j < len(due) and at == 1:
                        ln_sq(due[j])
                    if i in hi_at:
                        ln_hi(hi_at[i], hi_at[i] % N_BLK)

                hi_at = {2 + 4 * j + 5: k for j, k in enumerate(due) if k < 3 * N_BLK}
                for s in range(2 * len(due) + 2):
                    tile_act(g0 + s, between, 2 * s)
                last = (TILES_1 if phase_d else TILES_L) // 2 - ROUTE_PAIRS
                with act.Fori(len(due) + 1, last) as i:
                    for s in range(2):
                        tile_act(g0 + 2 * i + s)
                def route(i):
                    if i < BPH:
                        routing_out(2 * phase_d + 1, i)
                    if i == 5:
                        routing_act(2 * phase_d + 1)
                for s in range(2 * ROUTE_PAIRS):
                    tile_act(g0 + 2 * last + s, route if half == 0 else None, 2 * s)
                if phase_d:
                    tile_act(g0 + TILES_1 - 1)
                else:
                    with act.Fori(TILES_L // 2, TILES_0 // 2) as i:
                        for s in range(2):
                            tile_act(g0 + 2 * i + s)
                if half:
                    if phase_d:
                        act.wait_ge(store, 16 * BPH)
                    sums_out(k0, BPH * (g0 + (TILES_1 if phase_d else TILES_0)))

            for half in range(N_HALF):
                experts(False, half)
            def head_q(b, h):
                act.wait_ge(q_mm, b * HEADS + h + 1)
                nc.scalar.activation(qh[h % 2][:], ps[:, q_bank(b, h)], ACT.Identity, bias=attb[:, h:h + 1]).then_inc(q_hi, 1)

            def head_exp(b, h):
                act.wait_ge(s_neg, b * HEADS + h + 1)
                for t in range(TT):
                    nc.scalar.activation(pr[h % 2][:, t], ps[:, 2 + t // 2, (t % 2) * SEQ:(t % 2 + 1) * SEQ], ACT.Exp,
                                         bias=smx[h % 2][:, t:t + 1], scale=SCALE,
                                         accum_out=ssum[h % 2][:, t:t + 1]).then_inc(s_exp, 1)

            def head_t(b, h):
                for a in range(2):
                    act.wait_ge(t_mm, (b * HEADS + h) * 2 + a + 1)
                    nc.scalar.copy(pth[:, a], ps[:, 4 + a].rearrange("p (k q) -> p k q", k=2)).then_inc(t_hi, 1)

            def head_o(b, h):
                act.wait_ge(o_mm, b * HEADS + h + 1)
                nc.scalar.activation(oh[:], ps[:, 7], ACT.Identity, bias=attb[:, HEADS + KV + h // GRP:HEADS + KV + h // GRP + 1]).then_inc(o_hi, 1)

            def kv_k(b, k):
                act.wait_ge(k_mm, b * KV + k + 1)
                nc.scalar.activation(kh[k % 2][:], ps[:, 6], ACT.Identity, bias=attb[:, HEADS + k:HEADS + k + 1]).then_inc(k_hi, 1)

            def value(b, g, h):
                act.wait_ge(v_mm, b * VP + g + 1)
                nc.scalar.copy(v_part(vh, g), ps[:, v_bank(b, g)].rearrange("p (t d) -> p t d", t=2)).then_inc(v_hi, 1)

            def att_sums(b):
                act.wait_ge(y_mm, b * HEADS + HEADS)
                for m in range(DC):
                    ins = nc.scalar.activation(ln_r[0][:, m], ps[:, m], ACT.Identity, bias=attb[:, HEADS + 2 * KV + m:HEADS + 2 * KV + m + 1])
                ins.then_inc(l_r, 1)

            def attention(b, first=False, last=False):
                mean, _, factor = att_norms(b)

                def side(h):
                    if h in mean:
                        ln_sq(mean[h])
                    if h in factor:
                        ln_hi(factor[h], att_norm_block(b, h))
                    if last and h == 4:
                        routing_act(2)

                def taken(h):
                    if last and h < BPH:
                        routing_out(2, h)

                att_schedule(b, first, last, k=kv_k, v=value, q=head_q, exp=head_exp, sums=att_sums, before=taken, t=head_t, o=head_o, end=side)

            attention(0, first=True)
            with act.Fori(1, N_BLK - 1) as b:
                attention(b)
            attention(N_BLK - 1, last=True)

            for half in range(N_HALF):
                experts(True, half)
            for k in range(4 * N_BLK - BPH, 4 * N_BLK):
                ln_sq(k)

        @block.vector
        def _(dve):
            nc.vector.memset(mean_w[:], 1.0 / D).then_inc(const_set, 1)
            nc.vector.memset(half_c[:], -0.5).then_inc(const_set, 1)
            nc.vector.memset(one_c[:], 1.0).then_inc(const_set, 1)
            for e in range(NE):
                ins = nc.vector.memset(iota_f[:, e:e + 1], float(e))
            ins.then_inc(const_set, 1)
            for i in range(2):
                nc.vector.memset(xp[i][:, :, 0:TAPS - 1], 0.0).then_inc(pad_zero, 1)

            def mix_split_lo(c):
                dve.wait_ge(mix_hi, c + 1)
                o = c * RAWW
                nc.vector.tensor_tensor(mixl[:, o:o + RAWW], ln_r[c % 2][:].rearrange("p a b -> p (a b)"),
                                        f32(mixh[:, o:o + RAWW]), ALU.subtract).then_inc(mix_lo, 1)

            def norm_floor(n, layer):
                dve.wait_ge(n_stat, n + 1)
                if layer:
                    if stat_bank(n) != STAT:
                        dve.wait_ge(n_pow, n)
                    nc.vector.tensor_scalar(n_inb[:], ps[:, stat_bank(n), 0:TT], EPS, None, ALU.add).then_inc(n_in, 1)
                else:
                    nc.vector.tensor_scalar(n_inb[:], ps[:, STAT, 0:TT], TINY, None, ALU.max).then_inc(n_in, 1)

            def stat_bc(n):
                return ps[:, stat_bank(n):stat_bank(n) + 1].broadcast_to([P, DC, BLK])

            def rms_mul(i, b):
                dve.wait_ge(n_bc, rank[(i, b)] + 1)
                x = a_x if i == R1 else a_x1
                nc.vector.tensor_tensor(n_sqb[:], x[:], stat_bc(rank[(i, b)]), ALU.mult).then_inc(n_x, 1)

            def rms_lo(i, b):
                dve.wait_ge(r_hh, r_rank[(i, b)] + 1)
                high, low = (hh[0], hl[0]) if i == R1 else h_of(b)
                nc.vector.tensor_tensor(low[:], n_sqb[:], f32(high[:]), ALU.subtract).then_inc(r_hl, 1)

            def ln_center(k):
                dve.wait_ge(l_mean, k + 1)
                nc.vector.tensor_tensor(r_of(k)[:], r_of(k)[:], stat_bc(ln_rank(k)), ALU.subtract).then_inc(l_xc, 1)

            def ln_mul(k):
                dve.wait_ge(n_bc, ln_rank(k) + 1)
                nc.vector.tensor_tensor(r_of(k)[:], r_of(k)[:], stat_bc(ln_rank(k)), ALU.mult).then_inc(n_x, 1)

            def ln_lo(k, b):
                dve.wait_ge(l_xh, k + 1)
                nc.vector.tensor_tensor(xl[:, :, cols(b)], r_of(k)[:], f32(xh[:, :, cols(b)]), ALU.subtract).then_inc(l_xl, 1)

            def conv(b, ct):
                src, dst = xp[ct % 2], cacc[ct % 2]
                dve.wait_ge(conv_0, b * CT + ct + 1)
                n = (b * CT + ct) * (TAPS - 1)
                for k in range(TAPS - 1):
                    w = TAPS - 2 - k
                    if k:
                        dve.wait_ge(conv_tap, n + k)
                    nc.vector.scalar_tensor_tensor(out=dst[:], in0=src[:, :, w:w + SEQ], scalar=convw[:, ct, w:w + 1],
                                                   in1=dst[:], op0=ALU.mult, op1=ALU.add).then_inc(conv_tap, 1)

            def prod(b, ct):
                dve.wait_ge(xc_silu, b * CT + ct + 1)
                if b or ct:
                    dve.wait_ge(y_lo, b * CT + ct)
                nc.vector.tensor_tensor(yt[:], sxc[:], sz[ct % 2][:], ALU.mult).then_inc(y_prod, 1)

            def relu_lo(b, j):
                dve.wait_ge(m1_hi, b * MT + j + 1)
                nc.vector.scalar_tensor_tensor(out=rl[:, j % NR], in0=ps[:, 4 + j % 3], scalar=0.0, in1=f32(rh[:, j % NR]),
                                               op0=ALU.max, op1=ALU.subtract).then_inc(m1_lo, 1)

            def advance(table, n=1000):
                for _ in range(n):
                    if next(table, None) is None:
                        return

            chain = [0]

            def bc(v):
                return v[:, :, None].broadcast_to([P, HT, NE])

            def routing_dve(u):
                def link(ins):
                    chain[0] += 1
                    ins.then_inc(g_dve, 1)

                def linked():
                    dve.wait_ge(g_dve, chain[0])

                layer, half = divmod(u, N_HALF)
                ne = E0 if layer == 0 else E1
                dve.wait_ge(g_col, u + 1)
                nc.vector.tensor_copy(lg[:, :, 0:ne], ps[:, STAT, 0:HT * ne].rearrange("p (t e) -> p t e", t=HT)).then_inc(g_lg, 1)
                if layer == 1:
                    link(nc.vector.memset(lg[:, :, ne:], -1e30))
                    link(nc.vector.memset(cw[:], 0.0))
                yield 1
                dve.wait_ge(g_lg, u + 1)
                link(nc.vector.reduce_max(lmx[:], lg[:, :, 0:ne], AX_X))
                yield 1
                linked()
                nc.vector.tensor_tensor(ex[:], lg[:], bc(lmx[:]), ALU.subtract).then_inc(g_dif, 1)
                yield 1
                if layer == 0:
                    dve.wait_ge(g_exp, 2 * (u + 1))
                    link(nc.vector.tensor_scalar(sc[:], sc[:], 1.0, None, ALU.add))
                    yield 1
                    linked()
                    link(nc.vector.reciprocal(sc[:], sc[:]))
                    yield 1
                    linked()
                else:
                    dve.wait_ge(g_exp, N_HALF + u + 1)
                    link(nc.vector.reduce_sum(den[:], ex[:, :, 0:ne], AX_X))
                    yield 1
                    linked()
                    link(nc.vector.reciprocal(den[:], den[:]))
                    yield 1
                    linked()
                    link(nc.vector.tensor_tensor(sc[:], ex[:], bc(den[:]), ALU.mult))
                    yield 1
                    linked()
                for t in range(HT):
                    ins = nc.vector.max(top[:, t], sc[:, t, 0:ne])
                    if t == HT - 1:
                        link(ins)
                    if t % 2:
                        yield 1
                linked()
                for t in range(HT):
                    ins = nc.vector.max_index(tix[:, t], top[:, t], sc[:, t, 0:ne])
                    if t == HT - 1:
                        link(ins)
                    if t % 2:
                        yield 1
                linked()
                link(nc.vector.tensor_copy(tif[:], tix[:]))
                yield 1
                linked()
                for k in range(TOP_K):
                    dst = msk if k == 0 else eqk
                    link(nc.vector.tensor_tensor(dst[:], iota_f[:, None, :].broadcast_to([P, HT, NE]),
                                                 tif[:, :, k:k + 1].broadcast_to([P, HT, NE]), ALU.is_equal))
                    yield 1
                    linked()
                    if k:
                        link(nc.vector.tensor_tensor(msk[:], msk[:], eqk[:], ALU.add))
                        yield 1
                        linked()
                if layer == 0:
                    link(nc.vector.tensor_tensor(cw[:], ex[:], msk[:], ALU.mult))
                    yield 1
                    linked()
                    link(nc.vector.reduce_sum(den[:], cw[:], AX_X))
                    yield 1
                    linked()
                    link(nc.vector.reciprocal(den[:], den[:]))
                    yield 1
                    linked()
                    link(nc.vector.tensor_tensor(cw[:], cw[:], bc(den[:]), ALU.mult))
                    yield 1
                    linked()
                    link(nc.vector.tensor_scalar(cws[:], cw[:], SMALL, None, ALU.mult))
                else:
                    link(nc.vector.tensor_tensor(cw[:, :, 0:ne], sc[:, :, 0:ne], msk[:, :, 0:ne], ALU.mult))
                    link(nc.vector.memset(cw[:, :, ne:ne + 1], 1.0))
                yield 1
                linked()
                for i, c in enumerate((cw, cws) if layer == 0 else (cw,)):
                    for part in range(3):
                        if part < 2:
                            link(nc.vector.tensor_copy(cpart[i][:, :, part], c[:]))
                            yield 1
                            linked()
                            link(nc.vector.tensor_tensor(c[:], c[:], cpart[i][:, :, part], ALU.subtract))
                            yield 1
                            linked()
                        else:
                            nc.vector.tensor_copy(cpart[i][:, :, part], c[:]).then_inc(g_part, 1)
                            yield 1

            def routing_table(u, i):
                dve.wait_ge(g_tr, tr_count(u, i) + 1)
                nc.vector.tensor_copy(cwt[i][:, u % N_HALF], ps[0:3 * NE, STAT].bitcast(BF16)).then_inc(g_cwt, 1)

            mix_split_lo(0)
            mix_split_lo(1)
            norm_floor(rank[(R1, 0)], False)
            rms_mul(R1, 0)
            rms_lo(R1, 0)
            mix_split_lo(2)
            dve.wait_ge(const_ready, 3)
            nc.vector.tensor_tensor(gwl[:], gwr[:], f32(gwh[:]), ALU.subtract).then_inc(gwl_ready, 1)
            dve.wait_ge(pad_zero, 2)
            def mlp_sum(b):
                dve.wait_ge(m2_mm, (b + 1) * MT)
                dve.wait_ge(x01_done, b + 1)
                nc.vector.tensor_tensor(r_of(b)[:], ps[:, 2:4], res(b)[:], ALU.add).then_inc(l_r, 1)

            def mixer_sum(b):
                dve.wait_ge(mix_out, b + 1)
                if b:
                    dve.wait_ge(x01_done, b)
                if b < LAST:
                    dve.wait_ge(axr_in[b % 2], 16 * (b // 2 + 1))
                nc.vector.tensor_tensor(a_x1[:], ps[:, 0:2], res(b)[:], ALU.add).then_inc(x1_done, 1)

            for b in range(-1, LAST):
                n = (R2, b) if b >= 0 else (R1, 1)
                if b >= 0:
                    mixer_sum(b)
                if b >= 1:
                    mlp_sum(b - 1)
                if b >= 0:
                    norm_floor(rank[n], False)
                    conv(b + 1, 0)
                    rms_mul(*n)
                    rms_lo(*n)
                    if b == LAST - 1:
                        ln_center(b - 1)
                    conv(b + 1, 1)
                    prod(b + 1, 0)
                else:
                    conv(b + 1, 0)
                    norm_floor(rank[n], False)
                    conv(b + 1, 1)
                    prod(b + 1, 0)
                conv(b + 1, 2)
                prod(b + 1, 1)
                if b < 0:
                    rms_mul(R1, 1)
                if b in (-1, LAST - 1):
                    conv(b + 1, 3)
                    prod(b + 1, 2)
                if b == LAST - 1:
                    norm_floor(ln_rank(b - 1), True)
                if b < 0:
                    rms_lo(R1, 1)
                    prod(0, 3)
                    mix_split_lo(3)
                    mix_split_lo(4)
                elif b < LAST - 1:
                    for j in range(MT):
                        relu_lo(b, j)
                        if j == 0 and b >= 1:
                            ln_center(b - 1)
                        if j == 1:
                            prod(b + 1, 2)
                        if j == 3:
                            if b >= 1:
                                norm_floor(ln_rank(b - 1), True)
                            conv(b + 1, 3)
                        if j == 4 and b >= 1:
                            ln_mul(b - 1)
                        if j == 5:
                            norm_floor(rank[(R1, b + 2)], False)
                        if j == 6:
                            prod(b + 1, 3)
                            rms_mul(R1, b + 2)
                        if j == 7:
                            rms_lo(R1, b + 2)
                else:
                    table = routing_dve(0)
                    for j in range(MT):
                        relu_lo(b, j)
                        if j == 0:
                            prod(b + 1, 3)
                        if j == 1:
                            ln_mul(LAST - 2)
                        if j == 2:
                            ln_lo(LAST - 2, LAST - 2)
                        if j == 3:
                            mixer_sum(LAST)
                        if j == 4:
                            advance(table, 1)
                        if j == 5:
                            norm_floor(rank[(R2, LAST)], False)
                            advance(table, 2)
                        if j == 6:
                            rms_mul(R2, LAST)
                        if j == 7:
                            rms_lo(R2, LAST)
            mlp_sum(LAST - 1)
            for j in range(MT):
                relu_lo(LAST, j)
                if j == 1:
                    ln_center(LAST - 1)
                if j == 3:
                    norm_floor(ln_rank(LAST - 1), True)
                if j == 5:
                    ln_mul(LAST - 1)
                if j == 6:
                    ln_lo(LAST - 1, LAST - 1)
                advance(table, 5 if j < 5 else 3)
            mlp_sum(LAST)
            advance(table)
            for i in range(2):
                routing_table(0, i)

            def tile_dve(g, between=None, i0=0):
                for q in range(BPH):
                    n = BPH * g + q
                    dve.wait_ge(e_u, n + 1)
                    dve.wait_ge(e_sg, n + 1)
                    nc.vector.tensor_tensor(t1[:], ps[:, 5], sg[q][:], ALU.mult).then_inc(e_t1, 1)
                    dve.wait_ge(e_t1, n + 1)
                    dve.wait_ge(e_c, n + 1)
                    nc.vector.tensor_tensor(t2[q][:], ps[:, 6], t1[:], ALU.mult).then_inc(e_t2, 1)
                    dve.wait_ge(e_ah, n + 1)
                    nc.vector.tensor_tensor(al[q][:], t2[q][:], f32(ah[q][:]), ALU.subtract).then_inc(e_al, 1)
                    if between:
                        between(i0 + q)

            def experts(phase_d, half):
                g0 = first_tile(phase_d, half)
                due = due_norms(phase_d, half)

                def between(i):
                    j, at = divmod(i - 2, 4)
                    if 0 <= j < len(due):
                        k = due[j]
                        if at == 0:
                            ln_center(k)
                        if at == 2:
                            norm_floor(ln_rank(k), True)
                        if at == 3:
                            ln_mul(k)
                    if i in lo_at:
                        ln_lo(lo_at[i], lo_at[i] % N_BLK)

                lo_at = {2 + 4 * j + 5: k for j, k in enumerate(due) if k < 3 * N_BLK}
                for s in range(2 * len(due) + 2):
                    tile_dve(g0 + s, between, 2 * s)
                last = (TILES_1 if phase_d else TILES_L) // 2 - ROUTE_PAIRS
                with dve.Fori(len(due) + 1, last) as i:
                    for s in range(2):
                        tile_dve(g0 + 2 * i + s)
                table = routing_dve(2 * phase_d + 1) if half == 0 else None
                n_tab = 1 if phase_d else 2

                def route(i):
                    if i == 2:
                        advance(table, 1)
                    if i == 3:
                        advance(table, 2)
                    if 5 <= i < 13:
                        advance(table, 4)
                    if i == 13:
                        advance(table)
                    if i >= 16 - n_tab:
                        routing_table(2 * phase_d + 1, i - (16 - n_tab))

                for s in range(2 * ROUTE_PAIRS):
                    tile_dve(g0 + 2 * last + s, route if half == 0 else None, 2 * s)
                if phase_d:
                    tile_dve(g0 + TILES_1 - 1)
                else:
                    with dve.Fori(TILES_L // 2, TILES_0 // 2) as i:
                        for s in range(2):
                            tile_dve(g0 + 2 * i + s)

            for half in range(N_HALF):
                experts(False, half)
            def head_q(b, h):
                dve.wait_ge(q_hi, b * HEADS + h + 1)
                nc.vector.scalar_tensor_tensor(out=ql[h % 2][:], in0=ps[:, q_bank(b, h)], scalar=attb[:, h:h + 1], in1=f32(qh[h % 2][:]),
                                               op0=ALU.add, op1=ALU.subtract).then_inc(q_lo, 1)

            def head_max(b, h):
                dve.wait_ge(s_mm, b * HEADS + h + 1)
                nc.vector.reduce_max(smx[h % 2][:], ps[:, 2:4].rearrange("p a (k q) -> p (a k) q", k=2), AX_X).then_inc(s_max, 1)
                dve.wait_ge(s_max, b * HEADS + h + 1)
                nc.vector.tensor_scalar(smx[h % 2][:], smx[h % 2][:], -SCALE, None, ALU.mult).then_inc(s_neg, 1)

            def head_norm(b, h):
                dve.wait_ge(s_exp, (b * HEADS + h + 1) * TT)
                nc.vector.reciprocal(ssum[h % 2][:], ssum[h % 2][:]).then_inc(s_inv, 1)
                dve.wait_ge(s_inv, b * HEADS + h + 1)
                nc.vector.tensor_tensor(pr[h % 2][:], pr[h % 2][:], ssum[h % 2][:, :, None].broadcast_to([P, TT, SEQ]), ALU.mult).then_inc(s_prob, 1)

            def head_t(b, h):
                for a in range(2):
                    dve.wait_ge(t_hi, (b * HEADS + h) * 2 + a + 1)
                    nc.vector.tensor_tensor(ptl[:, a].rearrange("p k q -> p (k q)"), ps[:, 4 + a], f32(pth[:, a]).rearrange("p k q -> p (k q)"),
                                            ALU.subtract).then_inc(t_lo, 1)

            def head_o(b, h):
                dve.wait_ge(o_hi, b * HEADS + h + 1)
                nc.vector.scalar_tensor_tensor(out=ol[:], in0=ps[:, 7], scalar=attb[:, HEADS + KV + h // GRP:HEADS + KV + h // GRP + 1], in1=f32(oh[:]),
                                               op0=ALU.add, op1=ALU.subtract).then_inc(o_lo, 1)

            def kv_k(b, k):
                dve.wait_ge(k_hi, b * KV + k + 1)
                nc.vector.scalar_tensor_tensor(out=kl[k % 2][:], in0=ps[:, 6], scalar=attb[:, HEADS + k:HEADS + k + 1], in1=f32(kh[k % 2][:]),
                                               op0=ALU.add, op1=ALU.subtract).then_inc(k_lo, 1)

            def value(b, g, h):
                dve.wait_ge(v_hi, b * VP + g + 1)
                nc.vector.tensor_tensor(v_part(vl, g), ps[:, v_bank(b, g)].rearrange("p (t d) -> p t d", t=2),
                                        f32(v_part(vh, g)), ALU.subtract).then_inc(v_lo, 1)

            def attention(b, first=False, last=False):
                mean, var, factor = att_norms(b)
                table = routing_dve(2) if last else None

                def side(h):
                    if h - 1 in factor:
                        ln_lo(factor[h - 1], att_norm_block(b, h - 1))
                    if h in mean:
                        ln_center(mean[h])
                    if h in var:
                        norm_floor(ln_rank(var[h]), True)
                    if h in factor:
                        ln_mul(factor[h])
                    if last and h == BPH:
                        advance(table, 1)
                    if last and h == 14:
                        routing_table(2, 0)

                def end(h):
                    if last and h >= 3:
                        advance(table, (2 if h == 3 else 0 if h == 4 else 4) if h < 13 else 1000)

                att_schedule(b, first, last, k=kv_k, v=value, q=head_q, mx=head_max, norm=head_norm, before=side, t=head_t, o=head_o, end=end)
            attention(0, first=True)
            with dve.Fori(1, N_BLK - 1) as b:
                attention(b)
            attention(N_BLK - 1, last=True)

            for half in range(N_HALF):
                experts(True, half)
            for step in (ln_center, lambda k: norm_floor(ln_rank(k), True), ln_mul):
                for k in range(4 * N_BLK - BPH, 4 * N_BLK):
                    step(k)

        @block.tensor
        def _(pe):
            def norm_stat(n):
                pe.wait_ge(n_sum, n + 1)
                if stat_bank(n) == STAT and (not isinstance(n, int) or n):
                    pe.wait_ge(n_x, n)
                for t in range(TT):
                    mm = nc.tensor.matmul(ps[:, stat_bank(n), t:t + 1], sum_buf(n)[:, t * P:(t + 1) * P], mean_w[:, 0:1], start=True, stop=True,
                                          skip_group_check=True)
                mm.then_inc(n_stat, 1)

            def norm_bc(n):
                pe.wait_ge(n_pow, n + 1)
                for t in range(TT):
                    mm = nc.tensor.transpose(ps[:, stat_bank(n), t * P:(t + 1) * P], n_powb[:, t:t + 1].broadcast_to([P, P]), ident[:])
                mm.then_inc(n_bc, 1)

            def ln_mean(k):
                n = ln_rank(k)
                pe.wait_ge(l_sum, k + 1)
                if stat_bank(n) == STAT:
                    pe.wait_ge(n_x, n)
                else:
                    pe.wait_ge(e_sg, BPH * N_HALF * (TILES_0 + TILES_1))
                nc.tensor.matmul(ps[:, stat_bank(n)], mean_w[:], sum_buf(n)[:], start=True, stop=True).then_inc(l_mean, 1)

            def project(b, ct, kind):
                bank = z_bank(b, ct) if kind else xp_bank(b, ct)
                n = b * CT + ct
                beside = 1 <= b < LAST
                if beside and ct == 3:
                    pe.wait_ge(x1_done, b)
                elif kind == 0 and n >= 2:
                    pe.wait_ge(conv_0, n - 1)
                elif kind == 1 and n >= 1:
                    pe.wait_ge(z_ev, n)
                if ct == 0 and b >= 2:
                    pe.wait_ge(m1_lo, (b - 1) * MT)
                product(ps[:, bank], [(w_in_t(c, kind * CT + ct), (hh[0][:, c], hl[0][:, c])) for c in range(DC)])\
                    .then_inc(z_mm if kind else xp_mm, 1)

            def mix_product(b, ct):
                pe.wait_ge(y_lo, b * CT + ct + 1)
                if b and ct == 0:
                    pe.wait_ge(x1_done, b)
                    if b < LAST:
                        pe.wait_ge(conv_0, (b + 1) * CT)
                        pe.wait_ge(z_ev, (b + 1) * CT)
                for m in range(DC):
                    mm = product(ps[:, m], [(w_out_t(ct, m), (yh[:, ct], yl[:, ct]))], first=ct == 0, last=ct == CT - 1)
                if ct == CT - 1:
                    mm.then_inc(mix_out, 1)

            def mlp_up(b, j):
                n = b * MT + j
                if n >= 3:
                    pe.wait_ge(m1_lo, n - 2 if j >= 3 else b * MT)
                so_far = (b + 1) * CT + (3 if b + 1 < LAST else CT)
                if j < 2 and b + 1 < N_BLK:
                    pe.wait_ge(conv_0, so_far)
                if j == 2 and b + 1 < N_BLK:
                    pe.wait_ge(z_ev, so_far)
                product(ps[:, 4 + j % 3], [(w_m1_t(c, j), (h_of(b)[0][:, c], h_of(b)[1][:, c])) for c in range(DC)]).then_inc(m1_mm, 1)

            def mlp_down(b, j):
                pe.wait_ge(m1_lo, b * MT + j + 1)
                if b == 0 and j == 0:
                    mix_split_done(pe, N_RAW_A)
                if b and j == 0:
                    pe.wait_ge(l_r, b)
                for m in range(DC):
                    mm = product(ps[:, 2 + m], [(w_m2_t(j, m), (rh[:, j % NR], rl[:, j % NR]))], first=j == 0, last=j == MT - 1)
                mm.then_inc(m2_mm, 1)

            def routing_logits(u, i):
                layer, half = divmod(u, N_HALF)
                ne = E0 if layer == 0 else E1
                pe.wait_ge(gwl_ready, 1)
                pe.wait_ge(l_xl, 2 * layer * N_BLK + half * BPH + i + 1)
                if i:
                    pe.wait_ge(g_lt, u * BPH + i)
                else:
                    pe.wait_ge(n_x, ROUTE_AFTER[u])
                b = half * BPH + i
                product(ps[0:ne, STAT], [((gwh[:, layer, c, 0:ne], gwl[:, layer, c, 0:ne]),
                                          (xh[:, c, b * BLK:(b + 1) * BLK], xl[:, c, b * BLK:(b + 1) * BLK])) for c in range(DC)])\
                    .then_inc(g_mm, 1)

            def routing_columns(u):
                ne = E0 if u < N_HALF else E1
                pe.wait_ge(g_lt, (u + 1) * BPH)
                for t in range(HT):
                    mm = nc.tensor.transpose(ps[:, STAT, t * ne:(t + 1) * ne], lgt[0:ne, t // TT, (t % TT) * P:(t % TT + 1) * P], ident[0:ne, 0:ne])
                mm.then_inc(g_col, 1)

            pe.wait_ge(const_set, 4)
            norm_stat(rank[(R1, 0)])
            pe.wait_ge(const_ready, 3)
            norm_bc(rank[(R1, 0)])
            mix_split_done(pe, 2)
            pe.wait_ge(r_hl, 1)
            for b in range(-1, LAST):
                if b == 0:
                    mix_split_done(pe, 3)
                    for ct in range(CT):
                        mix_product(0, ct)
                if b >= 0:
                    pe.wait_ge(r_hl, r_rank[(R1, b + 1)] + 1)
                n = rank[(R2, b)] if b >= 0 else rank[(R1, 1)]
                project(b + 1, 0, 0)
                project(b + 1, 0, 1)
                norm_stat(n)
                project(b + 1, 1, 0)
                project(b + 1, 1, 1)
                norm_bc(n)
                if b == LAST - 1:
                    ln_mean(b - 1)
                project(b + 1, 2, 0)
                project(b + 1, 2, 1)
                if b in (-1, LAST - 1):
                    project(b + 1, 3, 0)
                    project(b + 1, 3, 1)
                if b == LAST - 1:
                    norm_stat(ln_rank(b - 1))
                if b >= 0:
                    if b == 0:
                        mix_split_done(pe, MIX_V)
                    pe.wait_ge(r_hl, r_rank[(R2, b)] + 1)
                    for j in range(MT + 2):
                        if j == MT and b < LAST - 1:
                            for ct in range(CT):
                                mix_product(b + 1, ct)
                        if j < MT:
                            mlp_up(b, j)
                        if j >= 2:
                            mlp_down(b, j - 2)
                        if b + 2 < N_BLK:
                            if j == 1:
                                for kind in range(2):
                                    project(b + 1, 3, kind)
                            if j == 5:
                                norm_stat(rank[(R1, b + 2)])
                            if j == 7:
                                norm_bc(rank[(R1, b + 2)])
                            if b >= 1:
                                if j == 0:
                                    ln_mean(b - 1)
                                if j == 3:
                                    norm_stat(ln_rank(b - 1))
                                if j == 4:
                                    norm_bc(ln_rank(b - 1))
                        else:
                            if j == 1:
                                norm_bc(ln_rank(LAST - 2))
                            if j in (2, 3):
                                routing_logits(0, j - 2)
                            if j == 4:
                                routing_columns(0)
                            if j in (2, 3):
                                for ct in range(2):
                                    mix_product(LAST, 2 * (j - 2) + ct)
                            if j == 5:
                                pe.wait_ge(g_lg, 1)
                                norm_stat(rank[(R2, LAST)])
                            if j == 7:
                                norm_bc(rank[(R2, LAST)])
            pe.wait_ge(r_hl, r_rank[(R2, LAST)] + 1)
            for j in range(MT + 2):
                if j < MT:
                    mlp_up(LAST, j)
                if j >= 2:
                    mlp_down(LAST, j - 2)
                if j == 1:
                    ln_mean(LAST - 1)
                if j == 3:
                    norm_stat(ln_rank(LAST - 1))
                if j == 5:
                    norm_bc(ln_rank(LAST - 1))

            def routing_transposes(u, i):
                pe.wait_ge(g_part, tr_count(u, i) + 1)
                if i:
                    pe.wait_ge(g_cwt, tr_count(u, i))
                for t in range(HT):
                    mm = nc.tensor.transpose(ps[0:3 * NE, STAT].bitcast(BF16)[:, t * P:(t + 1) * P],
                                             cpart[i][:, t].rearrange("p a e -> p (a e)"), ident_b[:])
                mm.then_inc(g_tr, 1)

            def seed(half, q):
                tok = slice((half * BPH + q) * BLK, (half * BPH + q + 1) * BLK)
                for m in range(DC):
                    nc.tensor.matmul(ps[:, 2 * q + m], ident_r[:], xh[:, m, tok], start=True, stop=False, skip_group_check=True)
                    nc.tensor.matmul(ps[:, 2 * q + m], ident_r[:], xl[:, m, tok], start=False, stop=False, skip_group_check=True)

            def down(n, s, q):
                pe.wait_ge(e_al, n + 1)
                for m in range(DC):
                    o = 2 * D + m * P
                    mm = product(ps[:, 2 * q + m], [(pair(wh[s], wl[s], o), (ah[q][:], al[q][:]))], first=False, last=True)
                mm.then_inc(e_dn, 1)

            def tile_pe(g, s, half, table, first=False, before=None, after=None, i0=0):
                pe.wait_ge(w_lo, g + 1)
                for q in range(BPH):
                    n = BPH * g + q
                    tok = slice((half * BPH + q) * BLK, (half * BPH + q + 1) * BLK)
                    if before:
                        before(i0 + q)
                    for bank, o, freed, done in ((4, 0, e_sg, e_g), (5, D, e_t1, e_u)):
                        if not isinstance(n, int) or n >= 1:
                            pe.wait_ge(freed, n)
                        product(ps[:, bank], [(pair(wh[s], wl[s], o + c * P), (xh[:, c, tok], xl[:, c, tok])) for c in range(DC)])\
                            .then_inc(done, 1)
                    if after:
                        after(i0 + q)
                    if not (first and q == 0):
                        down(n - 1, s if q else 1 - s, 1 - q)
                    if not isinstance(n, int) or n >= 1:
                        pe.wait_ge(e_t2, n)
                    if q == 0:
                        pe.wait_ge(sel_in[s], 8 * (g - s) + 16)
                    nc.tensor.matmul(ps[:, 6], selt[s][:], cwt[table][:, half, q * BLK:(q + 1) * BLK], start=True, stop=True).then_inc(e_c, 1)

            def experts(phase_d, half):
                g0 = first_tile(phase_d, half)
                due = due_norms(phase_d, half)
                k0 = (3 if phase_d else 1) * N_BLK + half * BPH

                def before(i):
                    j, at = divmod(i - 2, 4)
                    if 1 <= j <= len(due) and at == 0:
                        norm_bc(ln_rank(due[j - 1]))

                def after(i):
                    j, at = divmod(i - 2, 4)
                    if 0 <= j < len(due) and at == 0:
                        ln_mean(due[j])
                    if 0 <= j < len(due) and at == 2:
                        norm_stat(ln_rank(due[j]))
                    if i == 1:
                        pe.wait_ge(l_r, k0)
                        for q in range(BPH):
                            seed(half, q)

                pe.wait_ge(g_cwt, {(0, 0): 2, (0, 1): 4, (1, 0): 5, (1, 1): 6}[(phase_d, half)])
                for s in range(2 * len(due) + 2):
                    tile_pe(g0 + s, (g0 + s) % 2, half, 0, first=s == 0 and half == 0, before=before, after=after, i0=2 * s)
                last = (TILES_1 if phase_d else TILES_L) // 2 - ROUTE_PAIRS
                with pe.Fori(len(due) + 1, last) as i:
                    for s in range(2):
                        tile_pe(g0 + 2 * i + s, (g0 + s) % 2, half, 0)

                u = 2 * phase_d + 1
                n_tab = 1 if phase_d else 2

                def route_before(i):
                    if i < BPH:
                        routing_logits(u, i)
                    if i == BPH:
                        routing_columns(u)

                def route_after(i):
                    if i >= 16 - n_tab:
                        routing_transposes(u, i - (16 - n_tab))

                for s in range(2 * ROUTE_PAIRS):
                    tile_pe(g0 + 2 * last + s, (g0 + s) % 2, half, 0, before=route_before if half == 0 else None,
                            after=route_after if half == 0 else None, i0=2 * s)
                if phase_d:
                    tile_pe(g0 + TILES_1 - 1, (g0 + TILES_1 - 1) % 2, half, 0)
                else:
                    with pe.Fori(TILES_L // 2, TILES_0 // 2) as i:
                        for s in range(2):
                            tile_pe(g0 + 2 * i + s, s, half, 1)
                if half:
                    g = g0 + (TILES_1 if phase_d else TILES_0)
                    down(BPH * g - 1, (g - 1) % 2, 1)

            for t in range(2):
                routing_transposes(0, t)
            for half in range(N_HALF):
                experts(0, half)

            def kv_k(b, k):
                if k or not isinstance(b, int) or b:
                    pe.wait_ge(q_lo, b * HEADS + k * GRP)
                product(ps[:, 6], [(w_k_t(c, k), (xh[:, c, cols(b)], xl[:, c, cols(b)])) for c in range(DC)]).then_inc(k_mm, 1)

            def value(b, g, bank_free):
                bank_free()
                if g == 0:
                    pe.wait_ge(xb_in, b * 32 + 32)
                for t in range(2):
                    tok = slice(((g % 2) * 2 + t) * P, ((g % 2) * 2 + t + 1) * P)
                    mm = product(ps[:, v_bank(b, g), t * 2 * DH:(t + 1) * 2 * DH],
                                 [((xbh[:, c, tok], xbl[:, c, tok]), w_v_t(c, g // 2)) for c in range(DC)])
                mm.then_inc(v_mm, 1)

            def head_q(b, h, bank_free):
                bank_free()
                product(ps[:, q_bank(b, h)], [(w_q_t(c, h), (xh[:, c, cols(b)], xl[:, c, cols(b)])) for c in range(DC)]).then_inc(q_mm, 1)

            def head_s(b, h):
                pe.wait_ge(q_lo, b * HEADS + h + 1)
                if h == 0 and isinstance(b, int) and b == 0:
                    pe.wait_ge(l_r, 2 * N_BLK)
                if h or not isinstance(b, int) or b:
                    pe.wait_ge(s_exp, (b * HEADS + h) * TT)
                k = (h // GRP) % 2
                for t in range(TT):
                    sq = slice((t // 2) * SEQ, (t // 2 + 1) * SEQ)
                    mm = product(ps[:, 2 + t // 2, (t % 2) * SEQ:(t % 2 + 1) * SEQ],
                                 [((qh[h % 2][:, t * P:(t + 1) * P], ql[h % 2][:, t * P:(t + 1) * P]), (kh[k][:, sq], kl[k][:, sq]))])
                mm.then_inc(s_mm, 1)

            def head_t(b, h):
                pe.wait_ge(s_prob, b * HEADS + h + 1)
                if h or not isinstance(b, int) or b:
                    pe.wait_ge(t_lo, (b * HEADS + h) * 2)
                for a in range(2):
                    for kt in range(2):
                        for qt in range(2):
                            mm = nc.tensor.transpose(ps[:, 4 + a, kt * SEQ + qt * P:kt * SEQ + (qt + 1) * P],
                                                     pr[h % 2][:, 2 * a + qt, kt * P:(kt + 1) * P], ident[:])
                    mm.then_inc(t_mm, 1)

            def head_o(b, h):
                if h or not isinstance(b, int) or b:
                    pe.wait_ge(o_lo, b * HEADS + h)
                if h % (2 * GRP) == 0:
                    pe.wait_ge(v_lo, b * VP + (2 if h == 0 else VP))
                kc = slice((h // GRP) * DH, (h // GRP + 1) * DH)
                for a in range(2):
                    pe.wait_ge(t_lo, (b * HEADS + h) * 2 + a + 1)
                    mm = product(ps[:, 7, a * SEQ:(a + 1) * SEQ],
                                 [((vh[:, 2 * a + kt, kc], vl[:, 2 * a + kt, kc]), (pth[:, a, kt], ptl[:, a, kt])) for kt in range(2)])
                mm.then_inc(o_mm, 1)

            def head_y(b, h):
                if h == 0:
                    pe.wait_ge(l_r, b + 2 * N_BLK)
                    for m in range(DC):
                        nc.tensor.matmul(ps[:, m], ident_r[:], xh[:, m, cols(b)], start=True, stop=False, skip_group_check=True)
                        nc.tensor.matmul(ps[:, m], ident_r[:], xl[:, m, cols(b)], start=False, stop=False, skip_group_check=True)
                pe.wait_ge(o_lo, b * HEADS + h + 1)
                for m in range(DC):
                    mm = product(ps[:, m], [(w_o_t(h, m), (oh[:], ol[:]))], first=False, last=h == HEADS - 1)
                mm.then_inc(y_mm, 1)

            def attention(b, first=False, last=False):
                mean, var, factor = att_norms(b)

                def side(h):
                    if h in mean or h in var or h in factor or (last and (h < 3 or h == 14)):
                        pe.wait_ge(o_lo, b * HEADS + h)
                    if h in mean:
                        ln_mean(mean[h])
                    if h in var:
                        norm_stat(ln_rank(var[h]))
                    if h in factor:
                        norm_bc(ln_rank(factor[h]))
                    if last and h < BPH:
                        routing_logits(2, h)
                    if last and h == BPH:
                        routing_columns(2)
                    if last and h == 14:
                        routing_transposes(2, 0)

                def sums(b, h):
                    if h in mean:
                        pe.wait_ge(l_xc, mean[h] + 1)
                    if h in var:
                        pe.wait_ge(n_in, ln_rank(var[h]) + 1)
                    if h in factor:
                        pe.wait_ge(n_x, ln_rank(factor[h]) + 1)
                    if last and h < BPH:
                        pe.wait_ge(g_lt, 2 * BPH + h + 1)
                    if last and h == BPH:
                        pe.wait_ge(g_lg, 3)
                    if last and h == 14:
                        pe.wait_ge(g_cwt, 5)
                    head_o(b, h)

                def after(done, n):
                    return lambda: pe.wait_ge(done, n)

                def query(bq, h):
                    if first and bq is b and h < 3:
                        free = lambda: None
                    elif first and bq is b and h == 3:
                        free = after(v_lo, 1)
                    elif h % GRP == 0:
                        free = after(k_lo, bq * KV + h // GRP + 1)
                    elif h % GRP == 2 and not (last and h == 14):
                        free = after(v_lo, bq * VP + {2: 2, 6: 3, 10: 4, 14: 5}[h])
                    else:
                        free = after(q_lo, bq * HEADS + h)
                    head_q(bq, h, free)

                def values(bv, g, h):
                    if h >= 0:
                        free = after(q_lo, b * HEADS + h + 4)
                    else:
                        free = after(q_lo, 3) if g else after(k_lo, 1)
                    value(bv, g, free)

                att_schedule(b, first, last, k=kv_k, v=values, q=query,
                             s=head_s, t=head_t, after=side, o=sums, y=head_y)

            pe.wait_ge(att_lo, N_RAW_C)
            pe.wait_ge(l_xl, N_BLK + 1)
            attention(0, first=True)
            with pe.Fori(1, N_BLK - 1) as b:
                attention(b)
            attention(N_BLK - 1, last=True)

            for half in range(N_HALF):
                experts(1, half)
            for step in (ln_mean, lambda k: norm_stat(ln_rank(k)), lambda k: norm_bc(ln_rank(k))):
                for k in range(4 * N_BLK - BPH, 4 * N_BLK):
                    step(k)


def tr_count(u, i):
    return 2 * u + i if u < N_HALF else 2 * N_HALF + (u - N_HALF)


def att_schedule(b, first, last, k=None, v=None, q=None, s=None, mx=None, exp=None, norm=None, sums=None,
                 before=None, t=None, after=None, o=None, y=None, end=None):
    def at(h):
        return (b, h) if h < HEADS else (b + 1, h - HEADS)

    def do(step, h):
        if step and (h < HEADS or not last):
            step(*at(h))

    def y_step(h):
        if y and h:
            y(b, h - 1)
        elif y and not first:
            y(b - 1, HEADS - 1)

    def k_step(h):
        if k and (h < HEADS or not last):
            bk, hk = at(h)
            k(bk, hk // GRP)

    if first:
        for h in range(-3, 0):
            if h == -3:
                k_step(0)
            do(q, h + 3)
            if h == -1:
                do(exp, 0)
                do(norm, 0)
            if h == -1 and v:
                v(b, 0, h)
            if h >= -2:
                do(s, h + 2)
                do(mx, h + 2)
            if h == -1 and v:
                v(b, 1, h)
    for h in range(HEADS):
        if before:
            before(h)
        if t:
            t(b, h)
        if after:
            after(h)
        new_k = (h + 3) % GRP == 0
        if new_k:
            k_step(h + 3)
        else:
            do(q, h + 3)
        y_step(h)
        do(exp, h + 1)
        do(norm, h + 1)
        if sums and h == 0 and not first:
            sums(b - 1)
        if o:
            o(b, h)
        if new_k:
            do(q, h + 3)
        if v and h % GRP == 2:
            if h < 8:
                v(b, 2 + h // GRP, h)
            elif not last:
                v(b + 1, h // GRP - 2, h)
        do(s, h + 2)
        do(mx, h + 2)
        if end:
            end(h)
    if last:
        if y:
            y(b, HEADS - 1)
        if sums:
            sums(b)


def _rows(w, k):
    n = w.shape[1]
    return w.reshape(k, P, n).transpose(1, 0, 2).reshape(P, k * n)


def _tiles(gate, up, down, n_tiles):
    hidden = gate.shape[0]
    out = np.zeros((n_tiles, P, 3, D), gate.dtype)
    for w, which in ((gate, 0), (up, 1), (down, 2)):
        full = np.zeros((n_tiles * P, D), w.dtype)
        full[:hidden] = w
        full = full.reshape(n_tiles, P, D)
        if which < 2:
            full = full.reshape(n_tiles, P, DC, P).transpose(0, 3, 2, 1).reshape(n_tiles, P, D)
        out[:, :, which] = full
    return out.reshape(n_tiles, P, 3 * D)


def _selectors():
    one = 0x3F80
    s = np.zeros((TILES_0 + TILES_1, 3, NE, P), np.uint16)
    for t in range(TILES_L):
        for r in range(P):
            s[t, :, (t * P + r) // I0, r] = one
    for t in range(TILES_S):
        s[TILES_L + t, :, 2 * t:2 * t + 2, :] = one
    for t in range(TILES_1):
        for r in range(P):
            row = t * P + r
            if row < H1:
                s[TILES_0 + t, :, min(row // I1, E1), r] = one
    return s.reshape(TILES_0 + TILES_1, 3 * NE, P)


def kernel(**inputs):
    import concourse.bacc as bacc
    from concourse.bass_utils import run_bass_kernel_spmd

    a = {k: np.ascontiguousarray(v) for k, v in inputs.items()}
    x = a["L0_attn_x"].reshape(N_TOK, D)
    arrays = {
        "x_t": x.T.reshape(DC, P, N_TOK).transpose(1, 0, 2),
        "w_mix": np.concatenate([
            _rows(a["L0_attn_W_in"].T, DC), _rows(a["L0_attn_W_out"].T, CT),
            _rows(a["L0_attn_W_mlp1"].T, DC), _rows(a["L0_attn_W_mlp2"].T, MT)], axis=1),
        "conv_wb": np.concatenate([
            a["L0_attn_conv_w"].reshape(CT, P, TAPS), a["L0_attn_conv_b"].reshape(CT, P, 1)], axis=2).transpose(1, 0, 2),
    }
    gates = []
    for w in (a["L0_ffn_gate_w"], a["L1_ffn_gate_weight"]):
        g = np.zeros((NE, D), w.dtype)
        g[:w.shape[0]] = w
        gates.append(_rows(g.T, DC).reshape(P, DC, NE))
    arrays["gw0"], arrays["gw1"] = gates

    def hidden_first(w):
        return w.transpose(0, 2, 1).reshape(-1, D)

    gu, dn = a["L1_ffn_gate_up_weights"], a["L1_ffn_down_weights"]
    sgu, sdn = a["L1_ffn_shared_gate_up"], a["L1_ffn_shared_down"]
    arrays["moe_w"] = np.concatenate([
        _tiles(hidden_first(a["L0_ffn_Wg"]), hidden_first(a["L0_ffn_Wu"]), a["L0_ffn_Wd"].reshape(-1, D), TILES_L),
        _tiles(hidden_first(a["L0_ffn_cWg"]), hidden_first(a["L0_ffn_cWu"]), a["L0_ffn_cWd"].reshape(-1, D), TILES_S),
        _tiles(np.concatenate([gu[:, :I1].reshape(-1, D), sgu[:IS1]]),
               np.concatenate([gu[:, I1:].reshape(-1, D), sgu[IS1:]]),
               np.concatenate([hidden_first(dn), sdn.T]), TILES_1)])
    arrays["sel"] = _selectors()
    arrays["w_att"] = np.concatenate([
        _rows(a["L1_attn_Wq"], DC), _rows(a["L1_attn_Wk"], DC), _rows(a["L1_attn_Wv"], DC), _rows(a["L1_attn_Wo"], HEADS)], axis=1)
    arrays["att_b"] = np.concatenate([
        a["L1_attn_bq"].reshape(HEADS, P), a["L1_attn_bk"].reshape(KV, P), a["L1_attn_bv"].reshape(KV, P),
        a["L1_attn_bo"].reshape(DC, P)]).T
    arrays["ident"] = np.eye(P, dtype=np.float32)
    arrays = {k: np.ascontiguousarray(v) for k, v in arrays.items()}

    nc = bacc.Bacc("TRN2", target_bir_lowering=False, num_devices=1)
    ins = [nc.dram_tensor(f"in_{k}", v.shape, mybir.dt.from_np(v.dtype), kind="ExternalInput").ap() for k, v in arrays.items()]
    out = nc.dram_tensor("out_t", (P, DC, N_TOK), F32, kind="ExternalOutput").ap()
    by = dict(zip(arrays, ins))
    build_program(nc, by["x_t"], by["w_mix"], by["conv_wb"], by["gw0"], by["gw1"], by["moe_w"], by["sel"],
                  by["w_att"], by["att_b"], by["ident"], out)
    r = run_bass_kernel_spmd(nc, [{f"in_{k}": v for k, v in arrays.items()}], core_ids=[0])
    got = r.results[0]["out_t"]
    return np.ascontiguousarray(got.transpose(1, 0, 2).reshape(D, N_TOK).T).reshape(8, SEQ, D)
```
